# Optimizing a Trainium2 kernel written in Bass

```python
import numpy as np
import jax
import jax.numpy as jnp

def _softmax(x, axis=-1):
    return jax.nn.softmax(x, axis=axis)

def _gelu(x):
    return jax.nn.gelu(x, approximate=True)

def _silu(x):
    return jax.nn.silu(x)

def _sigmoid(x):
    return jax.nn.sigmoid(x)

def _layernorm(x, axis=-1, eps=1e-05):
    m = jnp.mean(x, axis=axis, keepdims=True)
    v = jnp.var(x, axis=axis, keepdims=True)
    return (x - m) / jnp.sqrt(v + eps)

def _scatter_add(tgt, idx, src, axis=0):
    return tgt.at[idx].add(src)

def _segment_sum(src, seg, n):
    return jax.ops.segment_sum(src, seg, n)
kernel_name = 'mk_perceiver_d2_seqx_r4_5e82a1'

def setup_inputs(seed: int=0):
    np.random.seed(seed)
    _w = jnp.asarray

    def _rec_inputs():
        import jax
        import jax.numpy as jnp
        _rk = jax.random.key(seed)
        x = -0.000125 + 0.9999 * jax.random.normal(jax.random.fold_in(_rk, 1), (32, 32, 256), jnp.float32)
        _lenS = 32 - jax.random.randint(jax.random.fold_in(_rk, 7), (32,), 0, max(1, 32 // 4) + 1, jnp.int32)
        _lenS2 = 257 - jax.random.randint(jax.random.fold_in(_rk, 8), (32,), 0, max(1, 257 // 4) + 1, jnp.int32)
        _ctx_1024P = jax.random.normal(jax.random.fold_in(_rk, 11), (32, 16, 256), jnp.float32)
        _ctx_1024c = jax.random.dirichlet(jax.random.fold_in(_rk, 511), 0.3 * jnp.ones((16,), jnp.float32), (32, 257))
        _ctx_1024t = jnp.einsum('bsk,bkd->bsd', _ctx_1024c, _ctx_1024P)
        _ctx_1024t = _ctx_1024t * jax.lax.rsqrt(jnp.mean(jnp.square(_ctx_1024t)) + 1e-12) * 0.953939
        ctx_1024 = -1.52775e-05 + 0.999936 * (_ctx_1024t + 0.3 * jax.random.normal(jax.random.fold_in(_rk, 611), (32, 257, 256), jnp.float32))
        return (x, ctx_1024)
    x, ctx_1024 = _rec_inputs()

    def _L0_xattn_setup():
        import jax, jax.numpy as jnp
        import numpy as np
        B, LP, LQ, H = (16, 512, 512, 256)
        key = jax.random.key(seed)
        k1, k2, k3 = jax.random.split(key, 3)
        proj_p = jax.random.normal(k1, (B, LP, H), dtype=jnp.float32)
        proj_q = jax.random.normal(k2, (B, LQ, H), dtype=jnp.float32)
        W = jax.random.normal(k3, (H, H), dtype=jnp.float32) * (1.0 / np.sqrt(H))
        b = jnp.zeros((H,), dtype=jnp.float32)
        return {'proj_p': proj_p, 'proj_q': proj_q, 'W': W, 'b': b}
    _L0_xattn_all = _L0_xattn_setup()
    _L0_xattn_in = {k: v for k, v in _L0_xattn_all.items() if k in ('W', 'b')}
    del _L0_xattn_all

    def _L0_attn_setup():
        import jax, jax.numpy as jnp
        import numpy as np
        import math
        N_HEAD = 16

        def sparsemax_lastdim(z):
            z_sorted = jnp.flip(jnp.sort(z, axis=-1), axis=-1)
            cs = jnp.cumsum(z_sorted, axis=-1)
            d = z.shape[-1]
            rho = jnp.arange(1, d + 1, dtype=z.dtype)
            support = 1.0 + rho * z_sorted > cs
            k = jnp.maximum(jnp.sum(support, axis=-1, keepdims=True), 1)
            cs_k = jnp.take_along_axis(cs, k - 1, axis=-1)
            tau = (cs_k - 1.0) / k.astype(z.dtype)
            return jnp.maximum(z - tau, 0.0)
        key = jax.random.key(seed)
        k1, k2, k3, k4, k5 = jax.random.split(key, 5)
        B, T, C = (2, 512, 256)
        x = jax.random.normal(k1, (B, T, C), dtype=jnp.float32)
        w_attn = jax.random.normal(k2, (C, 3 * C), dtype=jnp.float32) * (1.0 / math.sqrt(C))
        b_attn = jax.random.normal(k3, (3 * C,), dtype=jnp.float32) * 0.02
        w_proj = jax.random.normal(k4, (C, C), dtype=jnp.float32) * (1.0 / math.sqrt(C))
        b_proj = jax.random.normal(k5, (C,), dtype=jnp.float32) * 0.02
        return {'x': x, 'w_attn': w_attn, 'b_attn': b_attn, 'w_proj': w_proj, 'b_proj': b_proj}
    _L0_attn_all = _L0_attn_setup()
    _L0_attn_in = {k: v for k, v in _L0_attn_all.items() if k in ('w_attn', 'b_attn', 'w_proj', 'b_proj')}
    del _L0_attn_all

    def _L0_ffn_setup():
        import jax, jax.numpy as jnp
        import numpy as np
        E = 16
        F_C = 2.0
        D = 256
        I = 4 * D
        IS = 2 * D
        B, S = (4, 256)
        key = jax.random.key(seed)
        ks = jax.random.split(key, 8)
        w = 0.02
        return {'hidden_states': jax.random.normal(ks[0], (B, S, D), dtype=jnp.float32), 'gate_w': jax.random.normal(ks[1], (E, D), dtype=jnp.float32) * w, 'Wg': jax.random.normal(ks[2], (E, I, D), dtype=jnp.float32) * w, 'Wu': jax.random.normal(ks[3], (E, I, D), dtype=jnp.float32) * w, 'Wd': jax.random.normal(ks[4], (E, D, I), dtype=jnp.float32) * w, 'Sg': jax.random.normal(ks[5], (IS, D), dtype=jnp.float32) * w, 'Su': jax.random.normal(ks[6], (IS, D), dtype=jnp.float32) * w, 'Sd': jax.random.normal(ks[7], (D, IS), dtype=jnp.float32) * w}
    _L0_ffn_all = _L0_ffn_setup()
    _L0_ffn_in = {k: v for k, v in _L0_ffn_all.items() if k in ('gate_w', 'Wg', 'Wu', 'Wd', 'Sg', 'Su', 'Sd')}
    del _L0_ffn_all

    def _L1_xattn_setup():
        import jax, jax.numpy as jnp
        import numpy as np
        DIM = 256
        NUM_HEADS = 8
        HEAD_DIM = 64
        INNER = NUM_HEADS * HEAD_DIM
        key = jax.random.key(seed)
        ks = jax.random.split(key, 7)
        B, N, M = (8, 128, 1024)
        x = jax.random.normal(ks[0], (B, N, DIM), dtype=jnp.float32)
        context = jax.random.normal(ks[1], (B, M, DIM), dtype=jnp.float32)
        s_in = 1.0 / np.sqrt(DIM)
        s_inner = 1.0 / np.sqrt(INNER)
        Wq = jax.random.normal(ks[2], (DIM, INNER), dtype=jnp.float32) * s_in
        Wk = jax.random.normal(ks[3], (DIM, INNER), dtype=jnp.float32) * s_in
        Wv = jax.random.normal(ks[4], (DIM, INNER), dtype=jnp.float32) * s_in
        Wo = jax.random.normal(ks[5], (INNER, DIM), dtype=jnp.float32) * s_inner
        bo = jax.random.normal(ks[6], (DIM,), dtype=jnp.float32) * 0.01
        return {'x': x, 'context': context, 'Wq': Wq, 'Wk': Wk, 'Wv': Wv, 'Wo': Wo, 'bo': bo}
    _L1_xattn_all = _L1_xattn_setup()
    _L1_xattn_in = {k: v for k, v in _L1_xattn_all.items() if k in ('Wq', 'Wk', 'Wv', 'Wo', 'bo')}
    del _L1_xattn_all

    def _L1_attn_setup():
        import jax, jax.numpy as jnp
        import numpy as np
        THETA = 10000.0
        NUM_HEADS = 16

        def _rope_tables(seq_len, d_k, dtype):
            exponent = jnp.arange(d_k // 2, dtype=jnp.float32) * (2.0 / d_k)
            inv_freq = THETA ** (-exponent)
            pos = jnp.arange(seq_len, dtype=jnp.float32)
            angles = pos[:, None] * inv_freq[None, :]
            return (jnp.cos(angles).astype(dtype), jnp.sin(angles).astype(dtype))

        def _apply_rope(x, cos, sin):
            x1 = x[..., 0::2]
            x2 = x[..., 1::2]
            r1 = x1 * cos - x2 * sin
            r2 = x1 * sin + x2 * cos
            return jnp.stack([r1, r2], axis=-1).reshape(x.shape)
        key = jax.random.key(seed)
        ks = jax.random.split(key, 5)
        B, N, D = (2, 1024, 256)
        std = (2.0 / (D + D)) ** 0.5
        return {'x': jax.random.normal(ks[0], (B, N, D), dtype=jnp.float32), 'Wq': jax.random.normal(ks[1], (D, D), dtype=jnp.float32) * std, 'Wk': jax.random.normal(ks[2], (D, D), dtype=jnp.float32) * std, 'Wv': jax.random.normal(ks[3], (D, D), dtype=jnp.float32) * std, 'Wo': jax.random.normal(ks[4], (D, D), dtype=jnp.float32) * std}
    _L1_attn_all = _L1_attn_setup()
    _L1_attn_in = {k: v for k, v in _L1_attn_all.items() if k in ('Wq', 'Wk', 'Wv', 'Wo')}
    del _L1_attn_all

    def _L1_ffn_setup():
        import jax, jax.numpy as jnp
        import numpy as np
        key = jax.random.key(seed)
        ks = jax.random.split(key, 6)
        B, L, D, E = (4, 512, 256, 4)
        H = 4 * D
        x = jax.random.normal(ks[0], (B, L, D), dtype=jnp.float32)
        rW1 = jax.random.normal(ks[1], (D, 2 * D), dtype=jnp.float32) * (2.0 / D) ** 0.5
        rb1 = jnp.zeros((2 * D,), dtype=jnp.float32)
        rW2 = jax.random.normal(ks[2], (2 * D, E), dtype=jnp.float32) * (2.0 / (2 * D)) ** 0.5
        rb2 = jnp.zeros((E,), dtype=jnp.float32)
        We1 = jax.random.normal(ks[3], (E, D, H), dtype=jnp.float32) * (2.0 / D) ** 0.5
        be1 = jnp.zeros((E, H), dtype=jnp.float32)
        We2 = jax.random.normal(ks[4], (E, H, D), dtype=jnp.float32) * (2.0 / H) ** 0.5
        be2 = jnp.zeros((E, D), dtype=jnp.float32)
        return {'x': x, 'rW1': rW1, 'rb1': rb1, 'rW2': rW2, 'rb2': rb2, 'We1': We1, 'be1': be1, 'We2': We2, 'be2': be2}
    _L1_ffn_all = _L1_ffn_setup()
    _L1_ffn_in = {k: v for k, v in _L1_ffn_all.items() if k in ('rW1', 'rb1', 'rW2', 'rb2', 'We1', 'be1', 'We2', 'be2')}
    del _L1_ffn_all
    return {'x': x, 'ctx_1024': ctx_1024, 'L0_xattn_W': _L0_xattn_in['W'], 'L0_xattn_b': _L0_xattn_in['b'], 'L0_attn_w_attn': _L0_attn_in['w_attn'], 'L0_attn_b_attn': _L0_attn_in['b_attn'], 'L0_attn_w_proj': _L0_attn_in['w_proj'], 'L0_attn_b_proj': _L0_attn_in['b_proj'], 'L0_ffn_gate_w': _L0_ffn_in['gate_w'], 'L0_ffn_Wg': _L0_ffn_in['Wg'], 'L0_ffn_Wu': _L0_ffn_in['Wu'], 'L0_ffn_Wd': _L0_ffn_in['Wd'], 'L0_ffn_Sg': _L0_ffn_in['Sg'], 'L0_ffn_Su': _L0_ffn_in['Su'], 'L0_ffn_Sd': _L0_ffn_in['Sd'], 'L1_xattn_Wq': _L1_xattn_in['Wq'], 'L1_xattn_Wk': _L1_xattn_in['Wk'], 'L1_xattn_Wv': _L1_xattn_in['Wv'], 'L1_xattn_Wo': _L1_xattn_in['Wo'], 'L1_xattn_bo': _L1_xattn_in['bo'], 'L1_attn_Wq': _L1_attn_in['Wq'], 'L1_attn_Wk': _L1_attn_in['Wk'], 'L1_attn_Wv': _L1_attn_in['Wv'], 'L1_attn_Wo': _L1_attn_in['Wo'], 'L1_ffn_rW1': _L1_ffn_in['rW1'], 'L1_ffn_rb1': _L1_ffn_in['rb1'], 'L1_ffn_rW2': _L1_ffn_in['rW2'], 'L1_ffn_rb2': _L1_ffn_in['rb2'], 'L1_ffn_We1': _L1_ffn_in['We1'], 'L1_ffn_be1': _L1_ffn_in['be1'], 'L1_ffn_We2': _L1_ffn_in['We2'], 'L1_ffn_be2': _L1_ffn_in['be2']}

def reference(x, ctx_1024, L0_xattn_W, L0_xattn_b, L0_attn_w_attn, L0_attn_b_attn, L0_attn_w_proj, L0_attn_b_proj, L0_ffn_gate_w, L0_ffn_Wg, L0_ffn_Wu, L0_ffn_Wd, L0_ffn_Sg, L0_ffn_Su, L0_ffn_Sd, L1_xattn_Wq, L1_xattn_Wk, L1_xattn_Wv, L1_xattn_Wo, L1_xattn_bo, L1_attn_Wq, L1_attn_Wk, L1_attn_Wv, L1_attn_Wo, L1_ffn_rW1, L1_ffn_rb1, L1_ffn_rW2, L1_ffn_rb2, L1_ffn_We1, L1_ffn_be1, L1_ffn_We2, L1_ffn_be2):
    import jax
    import jax.numpy as jnp

    def _L0_xattn_ref(proj_p, proj_q, W, b):
        import jax, jax.numpy as jnp
        import numpy as np
        B, LP, LQ, H = (16, 512, 512, 256)
        trans_q = jnp.einsum('bqh,oh->bqo', proj_q, W) + b
        att_weights = jnp.einsum('bph,bqh->bpq', proj_p, trans_q)
        att_norm = jax.nn.softmax(att_weights, axis=-1)
        att_vec = jnp.einsum('bpq,bqh->bph', att_norm, proj_q)
        out = jax.nn.relu(jnp.einsum('bph,oh->bpo', att_vec, W) + b)
        return out

    def _L0_attn_ref(x, w_attn, b_attn, w_proj, b_proj):
        import jax, jax.numpy as jnp
        import numpy as np
        import math
        N_HEAD = 16

        def sparsemax_lastdim(z):
            z_sorted = jnp.flip(jnp.sort(z, axis=-1), axis=-1)
            cs = jnp.cumsum(z_sorted, axis=-1)
            d = z.shape[-1]
            rho = jnp.arange(1, d + 1, dtype=z.dtype)
            support = 1.0 + rho * z_sorted > cs
            k = jnp.maximum(jnp.sum(support, axis=-1, keepdims=True), 1)
            cs_k = jnp.take_along_axis(cs, k - 1, axis=-1)
            tau = (cs_k - 1.0) / k.astype(z.dtype)
            return jnp.maximum(z - tau, 0.0)
        B, T, C = x.shape
        H = N_HEAD
        hd = C // H
        qkv = x @ w_attn + b_attn
        q, k, v = jnp.split(qkv, 3, axis=-1)
        q = q.reshape(B, T, H, hd).transpose(0, 2, 1, 3)
        k = k.reshape(B, T, H, hd).transpose(0, 2, 1, 3)
        v = v.reshape(B, T, H, hd).transpose(0, 2, 1, 3)
        att = jnp.einsum('bhqd,bhkd->bhqk', q, k) * (1.0 / math.sqrt(hd))
        causal = jnp.tril(jnp.ones((T, T), dtype=bool))
        att = jnp.where(causal[None, None], att, -jnp.inf)
        att = sparsemax_lastdim(att)
        y = jnp.einsum('bhqk,bhkd->bhqd', att, v)
        y = y.transpose(0, 2, 1, 3).reshape(B, T, C)
        return y @ w_proj + b_proj

    def _L0_ffn_ref(hidden_states, gate_w, Wg, Wu, Wd, Sg, Su, Sd):
        import jax, jax.numpy as jnp
        import numpy as np
        E = 16
        F_C = 2.0
        D = 256
        I = 4 * D
        IS = 2 * D
        B, S = (4, 256)
        b, s, d = hidden_states.shape
        T = b * s
        C = int(T * F_C / E)
        flat_x = hidden_states.reshape(T, d)
        logits = flat_x @ gate_w.T
        scores = jax.nn.softmax(logits, axis=-1).T
        topk_weight, topk_idx = jax.lax.top_k(scores, C)
        xg = flat_x[topk_idx]
        g = jnp.einsum('ecd,eid->eci', xg, Wg)
        u = jnp.einsum('ecd,eid->eci', xg, Wu)
        h = jax.nn.gelu(g, approximate=False) * u
        eo = jnp.einsum('eci,edi->ecd', h, Wd)
        eo = eo * topk_weight[..., None]
        flat_out = jnp.zeros_like(flat_x).at[topk_idx.reshape(-1)].add(eo.reshape(-1, d))
        out = flat_out.reshape(b, s, d)
        sg = hidden_states @ Sg.T
        su = hidden_states @ Su.T
        shared = jax.nn.gelu(sg, approximate=False) * su @ Sd.T
        return out + shared

    def _L1_xattn_ref(x, context, Wq, Wk, Wv, Wo, bo):
        import jax, jax.numpy as jnp
        import numpy as np
        DIM = 256
        NUM_HEADS = 8
        HEAD_DIM = 64
        INNER = NUM_HEADS * HEAD_DIM
        B, N, _ = x.shape
        M = context.shape[1]
        scale = HEAD_DIM ** (-0.5)
        q = (x @ Wq).reshape(B, N, NUM_HEADS, HEAD_DIM).transpose(0, 2, 1, 3)
        k = (context @ Wk).reshape(B, M, NUM_HEADS, HEAD_DIM).transpose(0, 2, 1, 3)
        v = (context @ Wv).reshape(B, M, NUM_HEADS, HEAD_DIM).transpose(0, 2, 1, 3)
        attn = jax.nn.softmax(jnp.einsum('bhnd,bhmd->bhnm', q, k) * scale, axis=-1)
        out = jnp.einsum('bhnm,bhmd->bhnd', attn, v)
        out = out.transpose(0, 2, 1, 3).reshape(B, N, INNER)
        return out @ Wo + bo

    def _L1_attn_ref(x, Wq, Wk, Wv, Wo):
        import jax, jax.numpy as jnp
        import numpy as np
        THETA = 10000.0
        NUM_HEADS = 16

        def _rope_tables(seq_len, d_k, dtype):
            exponent = jnp.arange(d_k // 2, dtype=jnp.float32) * (2.0 / d_k)
            inv_freq = THETA ** (-exponent)
            pos = jnp.arange(seq_len, dtype=jnp.float32)
            angles = pos[:, None] * inv_freq[None, :]
            return (jnp.cos(angles).astype(dtype), jnp.sin(angles).astype(dtype))

        def _apply_rope(x, cos, sin):
            x1 = x[..., 0::2]
            x2 = x[..., 1::2]
            r1 = x1 * cos - x2 * sin
            r2 = x1 * sin + x2 * cos
            return jnp.stack([r1, r2], axis=-1).reshape(x.shape)
        B, N, D = x.shape
        H = NUM_HEADS
        d_k = D // H

        def proj(W):
            y = jnp.einsum('oi,bni->bno', W, x)
            return y.reshape(B, N, H, d_k).transpose(0, 2, 1, 3)
        Q, K, V = (proj(Wq), proj(Wk), proj(Wv))
        cos, sin = _rope_tables(N, d_k, x.dtype)
        Q = _apply_rope(Q, cos, sin)
        K = _apply_rope(K, cos, sin)
        scores = jnp.einsum('bhnd,bhmd->bhnm', Q, K) / jnp.sqrt(jnp.asarray(d_k, x.dtype))
        causal = jnp.tril(jnp.ones((N, N), dtype=bool))
        scores = jnp.where(causal, scores, -jnp.inf)
        attn = jax.nn.softmax(scores, axis=-1)
        out = jnp.einsum('bhnm,bhmd->bhnd', attn, V)
        out = out.transpose(0, 2, 1, 3).reshape(B, N, D)
        return jnp.einsum('oi,bni->bno', Wo, out)

    def _L1_ffn_ref(x, rW1, rb1, rW2, rb2, We1, be1, We2, be2):
        import jax, jax.numpy as jnp
        import numpy as np
        E = We1.shape[0]
        top_k = min(2, E)
        rh = jax.nn.gelu(x @ rW1 + rb1, approximate=False)
        router_logits = rh @ rW2 + rb2
        router_probs = jax.nn.softmax(router_logits, axis=-1)
        expert_weights, expert_indices = jax.lax.top_k(router_probs, top_k)
        one_hot = jax.nn.one_hot(expert_indices, E, dtype=x.dtype)
        token_mask = one_hot.sum(axis=2)
        combine_w = (one_hot * expert_weights[..., None]).sum(axis=2)
        out = jnp.zeros_like(x)
        for e in range(E):
            xi = x * token_mask[..., e:e + 1]
            h = jax.nn.gelu(xi @ We1[e] + be1[e], approximate=False)
            yo = h @ We2[e] + be2[e]
            out = out + yo * combine_w[..., e:e + 1]
        return out
    x = x + _L0_xattn_ref(_layernorm(x, axis=-1), ctx_1024, L0_xattn_W, L0_xattn_b)
    x = x + _L0_attn_ref(_layernorm(x, axis=-1), L0_attn_w_attn, L0_attn_b_attn, L0_attn_w_proj, L0_attn_b_proj)
    x = x + _L0_ffn_ref(_layernorm(x, axis=-1), L0_ffn_gate_w, L0_ffn_Wg, L0_ffn_Wu, L0_ffn_Wd, L0_ffn_Sg, L0_ffn_Su, L0_ffn_Sd)
    x = x + _L1_xattn_ref(_layernorm(x, axis=-1), ctx_1024, L1_xattn_Wq, L1_xattn_Wk, L1_xattn_Wv, L1_xattn_Wo, L1_xattn_bo)
    x = x + _L1_attn_ref(_layernorm(x, axis=-1), L1_attn_Wq, L1_attn_Wk, L1_attn_Wv, L1_attn_Wo)
    x = x + _L1_ffn_ref(_layernorm(x, axis=-1), L1_ffn_rW1, L1_ffn_rb1, L1_ffn_rW2, L1_ffn_rb2, L1_ffn_We1, L1_ffn_be1, L1_ffn_We2, L1_ffn_be2)
    return x

_drawn_inputs = setup_inputs


def setup_inputs(seed=0):
    import zlib

    import numpy as np

    out = dict(_drawn_inputs(seed))
    spreads = {'L0_xattn_b': (0.0, 0.1),
     'L1_ffn_rb1': (0.0, 1.841),
     'L1_ffn_rb2': (0.0, 1.625),
     'L1_ffn_be1': (0.0, 2.0),
     'L1_ffn_be2': (0.0, 2.0)}
    factors = {'L0_ffn_gate_w': 6.758,
     'L0_ffn_Wg': 8.0,
     'L0_ffn_Wu': 5.038,
     'L0_ffn_Wd': 8.0,
     'L1_xattn_bo': 101.67,
     'L0_ffn_Sg': 8.0,
     'L0_ffn_Su': 8.0,
     'L0_ffn_Sd': 8.0,
     'L1_xattn_Wq': 5.129,
     'L1_xattn_Wk': 5.089,
     'L1_attn_Wq': 3.95,
     'L1_attn_Wk': 3.906}
    for name, (base, spread) in spreads.items():
        noise = np.random.default_rng([zlib.crc32(name.encode()), seed]).standard_normal(out[name].shape)
        drawn = base * np.exp(spread * noise) if base else spread * noise
        out[name] = jnp.asarray(drawn.astype(out[name].dtype))
    for name, factor in factors.items():
        out[name] = (out[name] * factor).astype(out[name].dtype)
    return out
```

```python
from contextlib import ExitStack

import concourse.bass as bass
import numpy as np
from concourse import mybir

F32 = mybir.dt.float32
F32R = mybir.dt.float32r
U32 = mybir.dt.uint32
ALU = mybir.AluOpType
ACT = mybir.ActivationFunctionType
AX_X = mybir.AxisListType.X

B, L, D = 32, 32, 256
NK = 257
P = 128
T = B * L
G = T // P
BG = P // L
DT = D // P
H, HD = 16, 16
HPT = P // HD
QH = P // L
NQ = H // QH
E0, I0, C0 = 16, 1024, 128
IS = 512
XH, XD = 8, 64
XI = XH * XD
E1, I1 = 4, 1024
RH = 512
HALF = T // 2
NEG = -1.0e30
EPS = 1e-5

C_ID, C_CAUSAL, C_HEAD, C_BATCH, C_INV, C_COS, C_SIN, C_TRI, C_END = np.cumsum(
    [0, P, L, HPT, BG, L, L, L, E1 * E1]).tolist()
K_B, K_BQ, K_BK, K_RB1, K_BE1, K_END = np.cumsum([0, DT, DT, DT, RH // P, E1 * I1 // P]).tolist()
R_B, R_BV, R_BP, R_BO, R_RB2, R_BE2, R_END = np.cumsum([0, D, D, D, D, E1, E1 * D]).tolist()


def sort_steps(n):
    p = 1
    while p < n:
        k = p
        while k >= 1:
            yield p, k
            k //= 2
        p *= 2


def build(nc, a, out, stop=None):
    with ExitStack() as ctx:
        def sb(name, shape, dt=F32):
            return ctx.enter_context(nc.sbuf_tensor(name, shape, dt))

        def sem(name):
            return ctx.enter_context(nc.semaphore(name))

        bank = [ctx.enter_context(nc.psum_tensor(f"bank{i}", [P, 512], F32)) for i in range(8)]

        x = sb("x", [P, G, D])
        z = sb("z", [P, G, D])
        zT = sb("zT", [P, DT, T])
        const = sb("const", [P, C_END])
        bcol = sb("bcol", [P, K_END])
        brow = sb("brow", [1, R_END])
        ones = sb("ones", [1, P])
        w_even = sb("w_even", [P, 3072 + E0 * DT])
        w_odd = sb("w_odd", [P, 4096 + 64])
        stats = sb("stats", [P, G, 6])
        mv = sb("mv", [P, G, 2])
        veps = sb("veps", [P, G])
        std = sb("std", [P, G])
        rstd = sb("rstd", [P, G])
        small = sb("small", [P, 1024])
        arena_at = nc.sbuf_base
        arena = sb("arena", [P, 35904])
        z_dram = nc.dram_tensor("z_rows", [T, D], F32)
        acc_dram = nc.dram_tensor("acc_rows", [T, D], F32)

        def shaped(v, dims):
            if len(dims) == 1:
                return v
            names = "abcdef"[:len(dims)]
            return v.rearrange(f"p ({' '.join(names)}) -> p {' '.join(names)}",
                               **{c: d for c, d in zip(names[1:], dims[1:])})

        def area(off, *dims):
            return shaped(arena[:, off:off + int(np.prod(dims))], dims)

        def rounded(name, off, *dims):
            n = int(np.prod(dims))
            t = nc.alloc_sbuf_tensor_at(name, [P, n], F32R, offset=arena_at + 4 * off)
            return shaped(t[:, :], dims)

        def split(name, off, *dims):
            return rounded(name + "_hi", off, *dims), rounded(name + "_lo", off + int(np.prod(dims)), *dims)

        def matmul3(pe, o, lhsT, rhs, at_l, at_r, start, stop):
            for n, (i, j) in enumerate(((0, 0), (0, 1), (1, 0))):
                r = pe.matmul(o, lhsT[i][at_l], rhs[j][at_r], start=(start and n == 0), stop=(stop and n == 2))
            return r

        ident = const[:, C_ID:C_ID + P]

        ln_var, ln_std, ln_z = sem("ln_var"), sem("ln_std"), sem("ln_z")
        ln_turned, ln_zT_act, ln_zT_dve = sem("ln_turned"), sem("ln_zT_act"), sem("ln_zT_dve")
        dve_chain, act_chain = sem("dve_chain"), sem("act_chain")
        loaded_x, loaded_c = sem("loaded_x"), sem("loaded_c")
        w_loaded = [sem(f"w_loaded{s}") for s in range(6)]
        x_done = sem("x_done")
        stored = sem("stored")
        tick = sb("tick", [P, 1])
        chain = {"dve": 0, "act": 0}

        def link(eng, ins):
            name, s = ("dve", dve_chain) if eng is nc.vector else ("act", act_chain)
            chain[name] += 1
            ins.then_inc(s, 1)
            eng.wait_ge(s, chain[name])

        def dve_layernorm(k):
            dve = nc.vector
            if k == 0:
                dve.wait_ge(loaded_x, 16)
            for g in range(G):
                i = dve.bn_stats(stats[:, g, :], x[:, g, :])
            link(dve, i)
            for g in range(G):
                i = dve.bn_aggr(mv[:, g, :], stats[:, g, :])
            link(dve, i)
            dve.tensor_scalar(veps[:, :], mv[:, :, 1], EPS, None, ALU.add).then_inc(ln_var, 1)
            dve.wait_ge(ln_std, k + 1)
            link(dve, dve.reciprocal(rstd[:, :], std[:, :]))
            for g in range(G):
                dve.tensor_scalar(z[:, g, :], x[:, g, :], mv[:, g, 0:1], rstd[:, g:g + 1],
                                  ALU.subtract, ALU.mult).then_inc(ln_z, 1)
            for j in (1, 3):
                dve.wait_ge(ln_turned, 4 * k + j + 1)
                dve.tensor_copy(zT[:, :, 256 * j:256 * j + 256],
                                bank[j][:, :].rearrange("p (k t) -> p k t", k=DT)).then_inc(ln_zT_dve, 1)

        def dve_end_stage(dve):
            dve.memset(tick[:, :], 0.0).then_inc(x_done, 1)

        def act_layernorm(k):
            act = nc.scalar
            act.wait_ge(ln_var, k + 1)
            act.activation(std[:, :], veps[:, :], ACT.Sqrt).then_inc(ln_std, 1)
            for j in (0, 2):
                act.wait_ge(ln_turned, 4 * k + j + 1)
                act.activation(zT[:, :, 256 * j:256 * j + 256],
                               bank[j][:, :].rearrange("p (k t) -> p k t", k=DT),
                               ACT.Copy).then_inc(ln_zT_act, 1)

        def pe_layernorm(k):
            pe = nc.tensor
            if k == 0:
                pe.wait_ge(loaded_c, 48)
            else:
                pe.wait_ge(x_done, k)
            for j in range(4):
                pe.wait_ge(ln_z, G * k + 2 * j + 2)
                for g in (2 * j, 2 * j + 1):
                    for dt in range(DT):
                        c = dt * 256 + (g % 2) * P
                        i = pe.transpose(bank[j][:, c:c + P], z[:, g, dt * P:dt * P + P], ident)
                i.then_inc(ln_turned, 1)
            pe.wait_ge(ln_zT_act, 2 * k + 2)
            pe.wait_ge(ln_zT_dve, 2 * k + 2)

        def staggered(n, *steps):
            for t in range(n + len(steps) - 1):
                for lag, step in reversed(list(enumerate(steps))):
                    if step is not None and 0 <= t - lag < n:
                        step(t - lag)

        ctxT_v = a["ctxT"]
        ctx_v = a["ctx"]
        last_v = a["ctx_last"]
        ringT = [area(2056 * s, DT, BG, NK) for s in range(2)]
        ringN = [area(4112 + 2048 * s, BG, 2, D) for s in range(2)]
        ringL = [area(8208 + 1024 * s, 1024) for s in range(2)]
        RING_END = 10256
        keys_loaded = {k: [sem(f"{n}_keys_loaded{s}") for s in range(2)] for k, n in ((0, "a"), (3, "d"))}
        rows_loaded = {k: [sem(f"{n}_rows_loaded{s}") for s in range(2)] for k, n in ((0, "a"), (3, "d"))}
        wa_o = w_even[:, 0:DT * D].rearrange("p (k n) -> p k n", k=DT)
        wa_T = w_even[:, DT * D:2 * DT * D].rearrange("p (k n) -> p k n", k=DT)
        zwT = area(RING_END, DT, T)
        a_p = [area(RING_END + 2048 + 272 * s, NK) for s in range(2)]
        a_pT = [area(RING_END + 2592 + 384 * s, 384) for s in range(2)]
        a_att = [area(RING_END + 3360 + 256 * s, D) for s in range(2)]
        a_attT = [area(RING_END + 3872 + 256 * s, D) for s in range(2)]
        zb = small[:, 0:G]
        a_max, a_top, a_nb = small[:, 8:16], small[:, 16:24], small[:, 24:32]
        a_sum, a_inv = small[:, 32:40], small[:, 40:48]
        a_edge = [small[:, 48 + 4 * s:52 + 4 * s] for s in range(2)]
        a_zw, a_zw_out, a_zb, a_zb_out = sem("a_zw"), sem("a_zw_out"), sem("a_zb"), sem("a_zb_out")
        a_s, a_nbias, a_exp, a_edged, a_turn, a_turned = (
            sem("a_s"), sem("a_nbias"), sem("a_exp"), sem("a_edged"), sem("a_turn"), sem("a_turned"))
        a_av, a_norm, a_attturn, a_attturned, a_y, a_x = (
            sem("a_av"), sem("a_norm"), sem("a_attturn"), sem("a_attturned"), sem("a_y"), sem("a_x"))

        def sp_context(sp, k, keys_used, rows_used, per_group):
            for g in range(G):
                s = g % 2
                if g >= 2:
                    sp.wait_ge(keys_used, per_group[0] * (g - 1))
                sp.dma_start(ringT[s], ctxT_v[g].rearrange("p (k b n) -> p k b n", k=DT, b=BG)).then_inc(keys_loaded[k][s], 16)
                if g >= 2:
                    sp.wait_ge(rows_used, per_group[1] * (g - 1))
                sp.dma_start(ringN[s], ctx_v[g].rearrange("p (b k d) -> p b k d", b=BG, k=2)).then_inc(rows_loaded[k][s], 16)
                if k == 0:
                    dst, src = ringL[s][0:BG, 0:D], last_v[g * BG:g * BG + BG, :]
                else:
                    dst, src = ringL[s][0:1, :].rearrange("o (b d) -> o b d", b=BG), last_v[None, g * BG:g * BG + BG, :]
                sp.dma_start(dst, src).then_inc(rows_loaded[k][s], 16)

        def sp_stage_a(sp):
            sp_context(sp, 0, a_s, a_av, (1, 1))

        def pe_stage_a(pe):
            pe.wait_ge(w_loaded[0], 16)
            for m in range(DT):
                for n in range(2):
                    for k in range(DT):
                        i = pe.matmul(bank[4 + 2 * m + n][:, :], wa_o[:, k, m * P:m * P + P],
                                      zT[:, k, n * 512:n * 512 + 512], start=(k == 0), stop=(k == DT - 1))
                    i.then_inc(a_zw, 1)
            for g in range(G):
                for k in range(DT):
                    i = pe.matmul(bank[0][:, g:g + 1], zT[:, k, g * P:g * P + P],
                                  bcol[:, K_B + k:K_B + k + 1], start=(k == 0), stop=(k == DT - 1))
            i.then_inc(a_zb, 1)
            pe.wait_ge(a_zw_out, 4)
            pe.wait_ge(a_zb_out, 1)

            def scores(g):
                pe.wait_ge(keys_loaded[0][g % 2], 16 * (g // 2 + 1))
                if g >= 2:
                    pe.wait_ge(a_exp, g - 1)
                for b in range(BG):
                    c = g * P + b * L
                    for k in range(DT):
                        i = pe.matmul(bank[g % 2][b * L:b * L + L, 0:NK], zwT[:, k, c:c + L],
                                      ringT[g % 2][:, k, b, :], start=(k == 0), stop=(k == DT - 1))
                i.then_inc(a_s, 1)

            def turn_p(g):
                pe.wait_ge(a_edged, g + 1)
                if g >= 2:
                    pe.wait_ge(a_turned, g - 1)
                bk, p = bank[2 + g % 2], a_p[g % 2]
                pe.transpose(bk[:, 0:P], p[:, 0:P], ident)
                pe.transpose(bk[:, P:2 * P], p[:, P:2 * P], ident)
                pe.transpose(bk[0:BG, 2 * P:3 * P], a_edge[g % 2], ident).then_inc(a_turn, 1)

            def values(g):
                pe.wait_ge(a_turned, g + 1)
                pe.wait_ge(rows_loaded[0][g % 2], 32 * (g // 2 + 1))
                if g >= 2:
                    pe.wait_ge(a_norm, g - 1)
                o, pT = bank[4 + g % 2], a_pT[g % 2]
                for b in range(BG):
                    for k in range(2):
                        pe.matmul(o[b * L:b * L + L, 0:D], pT[:, k * P + b * L:k * P + b * L + L],
                                  ringN[g % 2][:, b, k, :], start=(k == 0), stop=False, skip_group_check=True)
                pe.matmul(o[:, 0:D], pT[0:BG, 2 * P:3 * P], ringL[g % 2][0:BG, 0:D],
                          start=False, stop=True, skip_group_check=True).then_inc(a_av, 1)

            def turn_att(g):
                pe.wait_ge(a_norm, g + 1)
                if g >= 1:
                    pe.wait_ge(a_attturned, g)
                pe.transpose(bank[6][:, 0:P], a_att[g % 2][:, 0:P], ident)
                pe.transpose(bank[6][:, P:2 * P], a_att[g % 2][:, P:2 * P], ident).then_inc(a_attturn, 1)

            def project(g):
                pe.wait_ge(a_attturned, g + 1)
                if g >= 1:
                    pe.wait_ge(a_x, g)
                for k in range(DT):
                    pe.matmul(bank[7][:, 0:D], a_attT[g % 2][:, k * P:k * P + P], wa_T[:, k, :],
                              start=(k == 0), stop=False)
                pe.matmul(bank[7][:, 0:D], ones[0:1, :], brow[0:1, R_B:R_B + D],
                          start=False, stop=True).then_inc(a_y, 1)

            staggered(G, scores, turn_p, values, turn_att, project)

        def act_stage_a(act):
            for j in range(4):
                act.wait_ge(a_zw, j + 1)
                m, n = j // 2, j % 2
                act.activation(zwT[:, m, n * 512:n * 512 + 512], bank[4 + j][:, :], ACT.Copy).then_inc(a_zw_out, 1)

            def exps(g):
                act.wait_ge(a_nbias, g + 1)
                if g >= 2:
                    act.wait_ge(a_turn, g - 1)
                act.activation(a_p[g % 2], bank[g % 2][:, 0:NK], ACT.Exp, bias=a_nb[:, g:g + 1],
                               accum_out=a_sum[:, g:g + 1]).then_inc(a_exp, 1)

            def turned_p(g):
                act.wait_ge(a_turn, g + 1)
                if g >= 2:
                    act.wait_ge(a_av, g - 1)
                act.activation(a_pT[g % 2][:, 0:2 * P], bank[2 + g % 2][:, 0:2 * P], ACT.Copy)
                act.activation(a_pT[g % 2][0:BG, 2 * P:3 * P], bank[2 + g % 2][0:BG, 2 * P:3 * P],
                               ACT.Copy).then_inc(a_turned, 1)

            def turned_att(g):
                act.wait_ge(a_attturn, g + 1)
                if g >= 2:
                    act.wait_ge(a_y, g - 1)
                act.activation(a_attT[g % 2], bank[6][:, 0:D], ACT.Copy).then_inc(a_attturned, 1)

            staggered(G, exps, turned_p, None, turned_att)

        def dve_stage_a(dve):
            dve.wait_ge(a_zb, 1)
            dve.tensor_copy(zb, bank[0][:, 0:G]).then_inc(a_zb_out, 1)
            dve.wait_ge(a_zb_out, 1)

            def maxima(g):
                dve.wait_ge(a_s, g + 1)
                c = slice(g, g + 1)
                link(dve, dve.tensor_reduce(a_max[:, c], bank[g % 2][:, 0:NK], AX_X, ALU.max))
                link(dve, dve.tensor_tensor(a_top[:, c], a_max[:, c], zb[:, c], ALU.add))
                dve.tensor_tensor(a_nb[:, c], zb[:, c], a_top[:, c], ALU.subtract).then_inc(a_nbias, 1)

            def edges(g):
                dve.wait_ge(a_exp, g + 1)
                dve.reciprocal(a_inv[:, g:g + 1], a_sum[:, g:g + 1])
                dve.tensor_scalar(a_edge[g % 2], const[:, C_BATCH:C_BATCH + BG], a_p[g % 2][:, NK - 1:NK], None,
                                  ALU.mult).then_inc(a_edged, 1)

            def normalize(g):
                dve.wait_ge(a_av, g + 1)
                dve.wait_ge(a_edged, g + 1)
                if g >= 2:
                    dve.wait_ge(a_attturn, g - 1)
                dve.tensor_scalar(a_att[g % 2], bank[4 + g % 2][:, 0:D], a_inv[:, g:g + 1], None,
                                  ALU.mult).then_inc(a_norm, 1)

            def residual(g):
                dve.wait_ge(a_y, g + 1)
                dve.scalar_tensor_tensor(out=x[:, g, :], in0=bank[7][:, 0:D], scalar=0.0, in1=x[:, g, :],
                                         op0=ALU.max, op1=ALU.add).then_inc(a_x, 1)

            def maxima_edges(g):
                maxima(g)
                edges(g)

            staggered(G, maxima_edges, None, normalize, None, residual)
            dve.wait_ge(a_x, G)

        Kx = area(0, DT, B, HPT, L)
        Vx = area(16384, B, NQ, QH, HD)
        S = area(24576, G, H * L)
        qT = area(28672, DT, T)
        kT = area(30720, DT, T)
        pT = [area(32768 + 512 * s, NQ, P) for s in range(2)]
        vrow = area(33792, G, D)
        yT = area(28672, DT, T)
        sort_a, sort_b = area(0, G * H * L), area(4096, G * H * L)
        notfirst = area(8192, G * H * L)
        sums = area(12288, G * H * L)
        rot = area(0, DT, T)

        SELF_SEMS = ("q", "qk_act", "qk_dve", "v", "v_out", "zeroed", "vx", "kx_act", "kx_dve", "roped",
                     "s", "s_out", "probs", "turn", "turned", "av", "y", "proj", "added", "sorted", "carried")
        self_sems = {k: {s: sem(f"{n}_{s}") for s in SELF_SEMS} for k, n in ((1, "b"), (4, "e"))}

        def pe_self(pe, k, w):
            q = self_sems[k]
            pe.wait_ge(w_loaded[k], 16)
            c = 0
            for n in range(2):
                for j in range(2):
                    for m in range(DT):
                        if c >= 4:
                            pe.wait_ge(q["qk_act"], c // 4 * 2)
                            pe.wait_ge(q["qk_dve"], c // 4 * 2)
                        for kk in range(DT):
                            i = pe.matmul(bank[c % 4][:, :], w(j)[:, kk, m * P:m * P + P],
                                          zT[:, kk, n * 512:n * 512 + 512], start=(kk == 0), stop=(kk == DT - 1))
                        i.then_inc(q["q"], 1)
                        c += 1
            for g in range(G):
                if g >= 4:
                    pe.wait_ge(q["v_out"], g - 3)
                o = bank[4 + g % 4][:, 0:D]
                for kk in range(DT):
                    i = pe.matmul(o, zT[:, kk, g * P:g * P + P], w(2)[:, kk, :], start=(kk == 0),
                                  stop=(kk == DT - 1 and k == 4))
                if k == 1:
                    i = pe.matmul(o, ones[0:1, :], brow[0:1, R_BV:R_BV + D], start=False, stop=True)
                i.then_inc(q["v"], 1)
            pe.wait_ge(q["qk_act"], 4)
            pe.wait_ge(q["qk_dve"], 4)
            for g in range(G):
                half = g // 4
                pe.wait_ge(q["kx_act"], HPT * (half + 1))
                pe.wait_ge(q["kx_dve"], HPT * (half + 1))
                if g >= 2:
                    pe.wait_ge(q["s_out"], g - 1)
                for b in range(BG):
                    c = g * P + b * L
                    for kk in range(DT):
                        i = pe.matmul(bank[g % 2][b * L:b * L + L, kk * 256:kk * 256 + 256], qT[:, kk, c:c + L],
                                      Kx[:, kk, g * BG + b, :, :].rearrange("p h j -> p (h j)"), start=True, stop=True)
                i.then_inc(q["s"], 1)
            pe.wait_ge(q["s_out"], G)

            def turn(g):
                pe.wait_ge(q["probs"], g + 1)
                if g >= 2:
                    pe.wait_ge(q["turned"], g - 1)
                for m in range(NQ):
                    i = pe.transpose(bank[2 + g % 2][:, m * P:m * P + P], S[:, g, m * P:m * P + P], ident)
                i.then_inc(q["turn"], 1)

            def values(g):
                pe.wait_ge(q["turned"], g + 1)
                if g == 0:
                    pe.wait_ge(q["vx"], 1)
                if g >= 2:
                    pe.wait_ge(q["y"], g - 1)
                for b in range(BG):
                    for m in range(NQ):
                        r, kk = (m % 2) * 64, m // 2
                        c = kk * P + b * L
                        i = pe.matmul(bank[4 + g % 2][r:r + 64, c:c + L],
                                      Vx[:, g * BG + b, m, :, :].rearrange("p h d -> p (h d)"),
                                      pT[g % 2][:, m, b * L:b * L + L], start=True, stop=True)
                i.then_inc(q["av"], 1)

            def project(g):
                pe.wait_ge(q["y"], g + 1)
                if g >= 2:
                    pe.wait_ge(q["added"], g - 1)
                o = bank[6 + g % 2][:, 0:D]
                for kk in range(DT):
                    i = pe.matmul(o, yT[:, kk, g * P:g * P + P], w(3)[:, kk, :], start=(kk == 0),
                                  stop=(kk == DT - 1 and k == 4))
                if k == 1:
                    i = pe.matmul(o, ones[0:1, :], brow[0:1, R_BP:R_BP + D], start=False, stop=True)
                i.then_inc(q["proj"], 1)

            staggered(G, turn, values, project)

        def act_self(act, k):
            q = self_sems[k]
            for n in range(2):
                for m in range(DT):
                    act.wait_ge(q["q"], 4 * n + 3 + m)
                    dst = kT[:, m, n * 512:n * 512 + 512]
                    if k == 1:
                        i = act.activation(dst, bank[2 + m][:, :], ACT.Identity, bias=bcol[:, K_BK + m:K_BK + m + 1])
                    else:
                        i = act.activation(dst, bank[2 + m][:, :], ACT.Copy)
                    i.then_inc(q["qk_act"], 1)
            for g in range(G):
                act.wait_ge(q["v"], g + 1)
                act.activation(vrow[:, g, :], bank[4 + g % 4][:, 0:D], ACT.Copy).then_inc(q["v_out"], 1)
            if k == 1:
                act.wait_ge(q["qk_act"], 4)
            else:
                act.wait_ge(q["roped"], 2)
            for n in range(2):
                for h in range(HPT):
                    act.activation(Kx[:, 0, n * 16:n * 16 + 16, h, :],
                                   kT[:, 0, n * 512:n * 512 + 512].rearrange("p (b j) -> p b j", j=L),
                                   ACT.Copy, scale=const[:, C_HEAD + h:C_HEAD + h + 1]).then_inc(q["kx_act"], 1)
            if k == 1:
                src, dst, carried = None, sort_a, 0
                for s, (p_, k_) in enumerate(sort_steps(L)):
                    if k_ < p_:
                        act.wait_ge(q["sorted"], 2 * s)
                        if carried:
                            act.wait_ge(q["carried"], carried)
                        c = 2 * p_ // k_
                        u = [t.rearrange("p (r c i) -> p r c i", c=c, i=k_)[:, :, 0:c:c - 1, :] for t in (src, dst)]
                        act.activation(u[1], u[0], ACT.Copy).then_inc(q["carried"], 1)
                        carried += 1
                    src, dst = dst, (sort_b if dst is sort_a else sort_a)
                for g in range(G):
                    act.wait_ge(q["sorted"], 2 * 15 + 1 + g)
                    act.activation(S[:, g, :], S[:, g, :], ACT.Relu).then_inc(q["probs"], 1)
            else:
                for g in range(G):
                    act.wait_ge(q["sorted"], g + 1)
                    act.activation(S[:, g, :], S[:, g, :], ACT.Exp, scale=0.25).then_inc(q["carried"], 1)

            def turned(g):
                act.wait_ge(q["turn"], g + 1)
                if g >= 2:
                    act.wait_ge(q["av"], g - 1)
                act.activation(pT[g % 2].rearrange("p m t -> p (m t)"), bank[2 + g % 2][:, :],
                               ACT.Copy).then_inc(q["turned"], 1)

            staggered(G, turned)

        def pool_self(pool, k):
            q = self_sems[k]
            pool.wait_ge(x_done, k)
            pool.memset(arena[:, 16384:24576], 0.0).then_inc(q["zeroed"], 1)
            pool.wait_ge(q["zeroed"], 1)
            pool.wait_ge(q["v_out"], G)
            vx = Vx.rearrange("p (g b) m h d -> p g b m h d", b=BG)
            vr = vrow.rearrange("p g (m h d) -> p g m h d", m=NQ, h=QH)
            for b in range(BG):
                for h in range(QH):
                    i = pool.tensor_copy(vx[h * L:h * L + L, :, b, :, h, :], vr[b * L:b * L + L, :, :, h, :])
            i.then_inc(q["vx"], 1)

        def dve_self(dve, k):
            q = self_sems[k]
            for n in range(2):
                for m in range(DT):
                    dve.wait_ge(q["q"], 4 * n + 1 + m)
                    dst = qT[:, m, n * 512:n * 512 + 512]
                    if k == 1:
                        i = dve.tensor_scalar(dst, bank[m][:, :], bcol[:, K_BQ + m:K_BQ + m + 1], HD ** -0.5,
                                              ALU.add, ALU.mult)
                    else:
                        i = dve.tensor_copy(dst, bank[m][:, :])
                    i.then_inc(q["qk_dve"], 1)
            dve.wait_ge(q["qk_act"], 4)
            if k == 4:
                dve.wait_ge(q["qk_dve"], 4)
                swap = [i ^ 1 for i in range(32)]
                cos, sin = (const[:, None, c:c + L].broadcast_to([P, DT * B, L]) for c in (C_COS, C_SIN))
                rows = [t.rearrange("p k (b j) -> p (k b) j", j=L) for t in (rot, qT, kT)]
                for t in (1, 2):
                    link(dve, dve.stream_shuffle(rot.rearrange("p k t -> p (k t)"),
                                                 (qT, kT)[t - 1].rearrange("p k t -> p (k t)"), swap))
                    link(dve, dve.tensor_tensor(rows[0], rows[0], sin, ALU.mult))
                    link(dve, dve.tensor_tensor(rows[t], rows[t], cos, ALU.mult))
                    dve.tensor_tensor(rows[t], rows[t], rows[0], ALU.add).then_inc(q["roped"], 1)
                    dve.wait_ge(q["roped"], t)
            for n in range(2):
                for h in range(HPT):
                    dve.tensor_scalar(Kx[:, 1, n * 16:n * 16 + 16, h, :],
                                      kT[:, 1, n * 512:n * 512 + 512].rearrange("p (b j) -> p b j", j=L),
                                      const[:, C_HEAD + h:C_HEAD + h + 1], None, ALU.mult).then_inc(q["kx_dve"], 1)
            causal = const[:, None, C_CAUSAL:C_CAUSAL + L].broadcast_to([P, H, L])
            for g in range(G):
                dve.wait_ge(q["s"], g + 1)
                dve.tensor_tensor(S[:, g, :].rearrange("p (h j) -> p h j", j=L),
                                  bank[g % 2][:, :].rearrange("p (h j) -> p h j", j=L), causal,
                                  ALU.add).then_inc(q["s_out"], 1)
            dve.wait_ge(q["s_out"], G)
            flat = S.rearrange("p g n -> p (g n)")
            rows = flat.rearrange("p (r j) -> p r j", j=L)
            stat = small[:, 0:G * H]
            stat_b = stat[:, :, None].broadcast_to([P, G * H, L])
            if k == 1:
                dve.wait_ge(q["s"], G)
                link(dve, dve.memset(notfirst, 1.0))
                link(dve, dve.memset(notfirst.rearrange("p (r j) -> p r j", j=L)[:, :, 0:1], 0.0))
                src, dst = flat, sort_a
                carried = 0
                for s, (p_, k_) in enumerate(sort_steps(L)):
                    if s:
                        dve.wait_ge(q["sorted"], 2 * s)
                        dve.wait_ge(q["carried"], carried) if carried else None
                    if k_ == p_:
                        u, v = (t.rearrange("p (r c i) -> p r c i", c=2, i=k_) for t in (src, dst))
                        lo, hi, olo, ohi = u[:, :, 0, :], u[:, :, 1, :], v[:, :, 0, :], v[:, :, 1, :]
                    else:
                        u, v = (t.rearrange("p (r n) -> p r n", n=2 * p_)[:, :, k_:2 * p_ - k_]
                                .rearrange("p r (m c i) -> p r m c i", c=2, i=k_) for t in (src, dst))
                        lo, hi, olo, ohi = u[:, :, :, 0, :], u[:, :, :, 1, :], v[:, :, :, 0, :], v[:, :, :, 1, :]
                        carried += 1
                    dve.tensor_tensor(olo, lo, hi, ALU.max).then_inc(q["sorted"], 1)
                    dve.tensor_tensor(ohi, lo, hi, ALU.min).then_inc(q["sorted"], 1)
                    src, dst = dst, (sort_b if dst is sort_a else sort_a)
                dve.wait_ge(q["sorted"], 30)
                dve.wait_ge(q["carried"], carried)
                link(dve, dve.tensor_tensor_scan(sums, notfirst, src, 0.0, ALU.mult, ALU.add))
                inv = const[:, None, C_INV:C_INV + L].broadcast_to([P, G * H, L])
                sums_r = sums.rearrange("p (r j) -> p r j", j=L)
                link(dve, dve.scalar_tensor_tensor(out=sums_r, in0=sums_r, scalar=-1.0, in1=inv,
                                                   op0=ALU.add, op1=ALU.mult))
                link(dve, dve.tensor_reduce(stat, sums_r, AX_X, ALU.max))
                for g in range(G):
                    r = slice(g * H, g * H + H)
                    dve.tensor_tensor(rows[:, r, :], rows[:, r, :], stat_b[:, r, :],
                                      ALU.subtract).then_inc(q["sorted"], 1)
            else:
                for g in range(G):
                    r = slice(g * H, g * H + H)
                    link(dve, dve.tensor_reduce(stat[:, r], rows[:, r, :], AX_X, ALU.max))
                    dve.tensor_tensor(rows[:, r, :], rows[:, r, :], stat_b[:, r, :],
                                      ALU.subtract).then_inc(q["sorted"], 1)
                for g in range(G):
                    r = slice(g * H, g * H + H)
                    dve.wait_ge(q["carried"], g + 1)
                    link(dve, dve.tensor_reduce(stat[:, r], rows[:, r, :], AX_X, ALU.add))
                    link(dve, dve.reciprocal(stat[:, r], stat[:, r]))
                    dve.tensor_tensor(rows[:, r, :], rows[:, r, :], stat_b[:, r, :],
                                      ALU.mult).then_inc(q["probs"], 1)

            def out_T(g):
                dve.wait_ge(q["av"], g + 1)
                dve.tensor_copy(yT[:, :, g * P:g * P + P],
                                bank[4 + g % 2][:, 0:D].rearrange("p (k t) -> p k t", k=DT)).then_inc(q["y"], 1)

            def residual(g):
                dve.wait_ge(q["proj"], g + 1)
                dve.tensor_tensor(x[:, g, :], bank[6 + g % 2][:, 0:D], x[:, g, :], ALU.add).then_inc(q["added"], 1)

            staggered(G, None, out_T, residual)
            dve.wait_ge(q["added"], G)

        def w_b(j):
            return w_odd[:, j * DT * D:(j + 1) * DT * D].rearrange("p (k n) -> p k n", k=DT)

        def w_e(j):
            return w_even[:, j * DT * D:(j + 1) * DT * D].rearrange("p (k n) -> p k n", k=DT)

        we = [[area(6144 * s, DT, I0), area(6144 * s + 2048, DT, I0), area(6144 * s + 4096, I0 // P, D)]
              for s in range(3)]
        c_gate = w_even[:, 3072:3072 + DT * E0].rearrange("p (k n) -> p k n", k=DT)
        c_sg, c_su = (w_even[:, j * 1024:(j + 1) * 1024].rearrange("p (k n) -> p k n", k=DT) for j in range(2))
        c_sd = w_even[:, 2048:3072].rearrange("p (k n) -> p k n", k=IS // P)
        c_sT = area(18432, IS // P, T)
        c_tmp = [area(22528 + 512 * s, 512) for s in range(2)]
        c_sc = area(23552, T // 2)[0:32 + E0, :]
        c_val = area(24064, C0)[0:32 + E0, :]
        c_idx = area(24192, C0)[0:32 + E0, :].bitcast(U32)
        c_idxf = area(24320, C0)[0:32 + E0, :]
        c_val2, c_idx2 = area(24448, C0)[0:E0, :], area(24576, C0)[0:E0, :]
        c_first = area(24704, C0)[0:E0, :]
        c_p = area(24832, G, E0)
        c_valT = area(24960, E0)
        c_idxT = area(24976, E0).bitcast(U32)
        c_xg = area(24992, E0, D)
        c_xgT = [area(29088 + 256 * s, DT, C0) for s in range(2)]
        c_hg = area(29600, 2, 512)
        c_h = area(30624, 2, 512)
        c_hT = [area(31648 + 1024 * s, I0 // P, C0) for s in range(2)]
        c_eo = [area(33696 + 256 * s, D) for s in range(2)]
        c_m, c_r = small[:, 0:G], small[:, 8:16]
        we_loaded = [sem(f"we_loaded{s}") for s in range(3)]
        z_stored, acc_stored, acc_back = sem("z_stored"), sem("acc_stored"), sem("acc_back")
        c_logit, c_sub, c_exp, c_prob, c_scT, c_sc_out = (
            sem("c_logit"), sem("c_sub"), sem("c_exp"), sem("c_prob"), sem("c_scT"), sem("c_sc_out"))
        c_sgu, c_sgel, c_sh, c_sy, c_sx = sem("c_sgu"), sem("c_sgel"), sem("c_sh"), sem("c_sy"), sem("c_sx")
        c_top, c_topT, c_pick = sem("c_top"), sem("c_topT"), sem("c_pick")
        c_got = [sem(f"c_got{s}") for s in range(E0 // 4)]
        c_xt, c_xt_out, c_gu, c_gel, c_hm = sem("c_xt"), sem("c_xt_out"), sem("c_gu"), sem("c_gel"), sem("c_hm")
        c_ht, c_hT_act, c_hT_dve, c_down, c_eo_out, c_added = (
            sem("c_ht"), sem("c_hT_act"), sem("c_hT_dve"), sem("c_down"), sem("c_eo_out"), sem("c_added"))

        N_TOP = 3 * (C0 // 8) + 2

        def sp_stage_c(sp):
            sp.wait_ge(ln_z, 3 * G)
            sp.dma_start(z_dram.rearrange("(g p) d -> p g d", p=P), z[:, :, :]).then_inc(z_stored, 16)
            for e in range(E0):
                s = e % 3
                if e == 0:
                    sp.wait_ge(x_done, 2)
                if e == 3:
                    sp.wait_ge(c_sx, G)
                    sp.dma_start(acc_dram.rearrange("(g p) d -> p g d", p=P), x[:, :, :]).then_inc(acc_stored, 16)
                if e >= 3:
                    sp.wait_ge(c_down, e - 2)
                for j, name in enumerate(("we_g", "we_u", "we_d")):
                    sp.dma_start(we[s][j].rearrange("p k n -> p (k n)"), a[name][e]).then_inc(we_loaded[s], 16)
            sp.wait_ge(c_added, 16 * E0)
            sp.dma_start(x[:, :, :], acc_dram.rearrange("(g p) d -> p g d", p=P)).then_inc(acc_back, 16)

        def pe_stage_c(pe):
            pe.wait_ge(w_loaded[2], 16)
            for g in range(G):
                for k in range(DT):
                    i = pe.matmul(bank[4][:, g * E0:g * E0 + E0], zT[:, k, g * P:g * P + P], c_gate[:, k, :],
                                  start=(k == 0), stop=(k == DT - 1))
            i.then_inc(c_logit, 1)

            def shared(c):
                m, n = c // 2, c % 2
                if c >= 2:
                    pe.wait_ge(c_sh, c - 1)
                for w, o in ((c_sg, bank[c % 2]), (c_su, bank[2 + c % 2])):
                    for k in range(DT):
                        i = pe.matmul(o[:, :], w[:, k, m * P:m * P + P], zT[:, k, n * 512:n * 512 + 512],
                                      start=(k == 0), stop=(k == DT - 1))
                i.then_inc(c_sgu, 1)

            for c in range(8):
                shared(c)
                if c == 1:
                    pe.wait_ge(c_prob, 1)
                    for g in range(G):
                        i = pe.transpose(bank[5 + g // 4][0:E0, (g % 4) * P:(g % 4) * P + P], c_p[:, g, :], ident)
                    i.then_inc(c_scT, 1)
            pe.wait_ge(c_sh, 8)
            for g in range(G):
                if g == 4:
                    pe.wait_ge(c_top, N_TOP)
                    pe.transpose(bank[4][:, 128:128 + E0], c_val[0:E0, :], ident[0:E0, 0:E0])
                    pe.transpose(bank[4][:, 144:144 + E0], c_idxf[0:E0, :], ident[0:E0, 0:E0]).then_inc(c_topT, 1)
                if g >= 2:
                    pe.wait_ge(c_sx, g - 1)
                for m in range(IS // P):
                    i = pe.matmul(bank[6 + g % 2][:, 0:D], c_sT[:, m, g * P:g * P + P], c_sd[:, m, :],
                                  start=(m == 0), stop=(m == IS // P - 1))
                i.then_inc(c_sy, 1)

            def turn_x(e):
                pe.wait_ge(c_got[e // 4], 4 * 16)
                if e >= 1:
                    pe.wait_ge(c_xt_out, e)
                for k in range(DT):
                    i = pe.transpose(bank[0][:, k * P:k * P + P], c_xg[:, e, k * P:k * P + P], ident)
                i.then_inc(c_xt, 1)

            def gate_up(e, c):
                if c == 0:
                    pe.wait_ge(c_xt_out, e + 1)
                    pe.wait_ge(we_loaded[e % 3], 48 * (e // 3 + 1))
                if e >= 1:
                    pe.wait_ge(c_hm, 2 * e - 1 + c)
                elif c == 0:
                    pe.wait_ge(c_pick, 2)
                for j in range(2):
                    for k in range(DT):
                        i = pe.matmul(bank[1 + 2 * j + c][:, :], c_xgT[e % 2][:, k, :],
                                      we[e % 3][j][:, k, c * 512:c * 512 + 512], start=(k == 0), stop=(k == DT - 1))
                i.then_inc(c_gu, 1)

            def turn_h(e, c):
                pe.wait_ge(c_hm, 2 * e + c + 1)
                if e >= 1:
                    pe.wait_ge((c_hT_act, c_hT_dve)[c], e)
                if e == 0:
                    pe.wait_ge(c_sx, G)
                for m in range(4):
                    i = pe.transpose(bank[5 + c][:, m * P:m * P + P], c_h[:, c, m * P:m * P + P], ident)
                i.then_inc(c_ht, 1)

            def down(e):
                pe.wait_ge(c_hT_act, e + 1)
                pe.wait_ge(c_hT_dve, e + 1)
                if e >= 1:
                    pe.wait_ge(c_eo_out, e)
                for m in range(I0 // P):
                    i = pe.matmul(bank[7][:, 0:D], c_hT[e % 2][:, m, :], we[e % 3][2][:, m, :],
                                  start=(m == 0), stop=(m == I0 // P - 1))
                i.then_inc(c_down, 1)

            turn_x(0)
            for e in range(E0 + 1):
                if e < E0:
                    gate_up(e, 0)
                if e >= 1:
                    turn_h(e - 1, 1)
                if e < E0:
                    gate_up(e, 1)
                if e + 1 < E0:
                    turn_x(e + 1)
                if e >= 1:
                    down(e - 1)
                if e < E0:
                    turn_h(e, 0)

        def act_stage_c(act):
            act.wait_ge(c_sub, 1)
            act.activation(c_p, c_p, ACT.Exp).then_inc(c_exp, 1)
            for c in range(8):
                act.wait_ge(c_sgu, c + 1)
                if c >= 2:
                    act.wait_ge(c_sh, c - 1)
                act.activation(c_tmp[c % 2], bank[c % 2][:, :], ACT.Gelu).then_inc(c_sgel, 1)

            def x_out(e):
                act.wait_ge(c_xt, e + 1)
                if e >= 2:
                    act.wait_ge(c_gu, 2 * (e - 1))
                act.activation(c_xgT[e % 2].rearrange("p k t -> p (k t)"), bank[0][:, 0:D], ACT.Copy).then_inc(c_xt_out, 1)

            x_out(0)
            for e in range(E0):
                for c in range(2):
                    act.wait_ge(c_gu, 2 * e + c + 1)
                    act.activation(c_hg[:, c, :], bank[1 + c][:, :], ACT.Gelu).then_inc(c_gel, 1)
                if e + 1 < E0:
                    x_out(e + 1)
                act.wait_ge(c_ht, 2 * e + 1)
                if e >= 2:
                    act.wait_ge(c_down, e - 1)
                act.activation(c_hT[e % 2][:, 0:4, :].rearrange("p m t -> p (m t)"), bank[5][:, :],
                               ACT.Copy).then_inc(c_hT_act, 1)

        def dve_stage_c(dve):
            def picks():
                dve.wait_ge(c_topT, 1)
                dve.tensor_copy(c_idxT, bank[4][:, 144:144 + E0]).then_inc(c_pick, 1)
                dve.tensor_copy(c_valT, bank[4][:, 128:128 + E0]).then_inc(c_pick, 1)

            link(dve, dve.memset(c_sc[0:32, :], 0.0))
            dve.wait_ge(c_logit, 1)
            logits = bank[4][:, 0:P].rearrange("p (g e) -> p g e", g=G)
            m_b, r_b = (t[:, :, None].broadcast_to([P, G, E0]) for t in (c_m, c_r))
            link(dve, dve.tensor_reduce(c_m, logits, AX_X, ALU.max))
            dve.tensor_tensor(c_p, logits, m_b, ALU.subtract).then_inc(c_sub, 1)
            dve.wait_ge(c_exp, 1)
            link(dve, dve.tensor_reduce(c_r, c_p, AX_X, ALU.add))
            link(dve, dve.reciprocal(c_r, c_r))
            dve.tensor_tensor(c_p, c_p, r_b, ALU.mult).then_inc(c_prob, 1)

            def shared(c):
                dve.wait_ge(c_sgel, c + 1)
                m, n = c // 2, c % 2
                dve.tensor_tensor(c_sT[:, m, n * 512:n * 512 + 512], bank[2 + c % 2][:, :], c_tmp[c % 2],
                                  ALU.mult).then_inc(c_sh, 1)

            shared(0)
            shared(1)
            dve.wait_ge(c_scT, 1)
            for j in range(2):
                dve.tensor_copy(c_sc[32 * j:32 * j + E0, :], bank[5 + j][0:E0, :]).then_inc(c_sc_out, 1)
            dve.wait_ge(c_sc_out, 2)
            for r in range(C0 // 8):
                v, ix = c_val[:, 8 * r:8 * r + 8], c_idx[:, 8 * r:8 * r + 8]
                dve.max(v, c_sc).then_inc(c_top, 1)
                dve.wait_ge(c_top, 3 * r + 1)
                dve.max_index(ix, v, c_sc).then_inc(c_top, 1)
                dve.wait_ge(c_top, 3 * r + 2)
                dve.match_replace(c_sc, v, c_sc, -1.0).then_inc(c_top, 1)
                if r % 2 == 1 and 2 + r // 2 < 8:
                    shared(2 + r // 2)
                dve.wait_ge(c_top, 3 * r + 3)
            up = slice(C0 - 1, None, -1)
            dve.tensor_copy(c_val2, c_val[32:32 + E0, up])
            link(dve, dve.tensor_copy(c_idxf, c_idx))
            dve.tensor_scalar(c_idx2, c_idxf[32:32 + E0, up], float(T // 2), None, ALU.add)
            link(dve, dve.tensor_tensor(c_first, c_val[0:E0, :], c_val2, ALU.is_ge))
            link(dve, dve.tensor_tensor(c_idxf[0:E0, :], c_idxf[0:E0, :], c_idx2, ALU.subtract))
            link(dve, dve.tensor_tensor(c_idxf[0:E0, :], c_idxf[0:E0, :], c_first, ALU.mult))
            dve.tensor_tensor(c_idxf[0:E0, :], c_idxf[0:E0, :], c_idx2, ALU.add).then_inc(c_top, 1)
            dve.tensor_tensor(c_val[0:E0, :], c_val[0:E0, :], c_val2, ALU.max).then_inc(c_top, 1)
            for g in range(G):
                if g == 5:
                    picks()
                dve.wait_ge(c_sy, g + 1)
                dve.tensor_tensor(x[:, g, :], bank[6 + g % 2][:, 0:D], x[:, g, :], ALU.add).then_inc(c_sx, 1)
            dve.wait_ge(c_pick, 2)

            def hidden(e, c):
                dve.wait_ge(c_gel, 2 * e + c + 1)
                if e >= 1:
                    dve.wait_ge(c_ht, 2 * e - 1 + c)
                dve.tensor_tensor(c_h[:, c, :], bank[3 + c][:, :], c_hg[:, c, :], ALU.mult).then_inc(c_hm, 1)

            def h_out(e):
                dve.wait_ge(c_ht, 2 * e + 2)
                if e >= 2:
                    dve.wait_ge(c_down, e - 1)
                dve.tensor_copy(c_hT[e % 2][:, 4:8, :].rearrange("p m t -> p (m t)"), bank[6][:, :]).then_inc(c_hT_dve, 1)

            def weigh(e):
                dve.wait_ge(c_down, e + 1)
                if e >= 2:
                    dve.wait_ge(c_added, 16 * (e - 1))
                dve.tensor_scalar(c_eo[e % 2], bank[7][:, 0:D], c_valT[:, e:e + 1], None, ALU.mult).then_inc(c_eo_out, 1)

            for e in range(E0 + 1):
                if e < E0:
                    hidden(e, 0)
                if e >= 1:
                    h_out(e - 1)
                if e < E0:
                    hidden(e, 1)
                if e >= 1:
                    weigh(e - 1)
            dve.wait_ge(acc_back, 16)

        def pool_stage_c(pool):
            def gather(e):
                pool.indirect_dma_start(c_xg[:, e, :], None, z_dram[:, :], bass.IndirectOffsetOnAxis(
                    ap=c_idxT[:, e:e + 1], axis=0)).then_inc(c_got[e // 4], 16)

            pool.wait_ge(c_pick, 1)
            pool.wait_ge(z_stored, 16)
            for e in range(E0):
                gather(e)
            pool.wait_ge(acc_stored, 16)
            for e in range(E0):
                pool.wait_ge(c_eo_out, e + 1)
                if e >= 1:
                    pool.wait_ge(c_added, 16 * e)
                pool.indirect_dma_start(acc_dram[:, :], bass.IndirectOffsetOnAxis(ap=c_idxT[:, e:e + 1], axis=0),
                                        c_eo[e % 2], None, compute_op=ALU.add).then_inc(c_added, 16)

        w_d = [w_odd[:, j * 1024:(j + 1) * 1024].rearrange("p (k n) -> p k n", k=k)
               for j, k in enumerate((DT, XI // P, DT, XI // P))]
        d_q = area(26640, XI // P, T)
        d_qk = area(10256, DT, B // 2, XH * L)
        d_aT = area(18448, DT, B // 2, XH * L)
        d_oT = area(30736, XI // P, T)
        d_p = [[area(34832 + 260 * (2 * s + j), NK) for j in range(2)] for s in range(2)]
        zf = z[:, :, :].rearrange("p g d -> p (g d)")
        d_pT = [zf[:, 512 * s:512 * s + 512].rearrange("p (k r) -> p k r", k=2) for s in range(2)]
        d_last = [zf[0:1, 1024 + 256 * s:1280 + 256 * s] for s in range(2)]
        d_mx, d_nb, d_sum, d_inv = (small[:, 64 * j:64 * j + 64] for j in range(4))
        (d_qd, d_q_out, d_qkd, d_qk_act, d_qk_dve, d_s, d_nbias, d_exp, d_norm, d_turn, d_turned, d_av, d_a_out,
         d_o, d_o_out, d_y, d_x) = (sem("d_" + n) for n in (
             "q", "q_out", "qk", "qk_act", "qk_dve", "s", "nbias", "exp", "norm", "turn", "turned", "av", "a_out",
             "o", "o_out", "y", "x"))

        def sp_stage_d(sp):
            sp.wait_ge(x_done, 3)
            sp_context(sp, 3, d_s, d_av, (2 * BG, BG))

        def pe_stage_d(pe):
            pe.wait_ge(w_loaded[3], 16)
            for c in range(8):
                m, n = c % 4, c // 4
                if c >= 4:
                    pe.wait_ge(d_q_out, c - 3)
                for k in range(DT):
                    i = pe.matmul(bank[4 + c % 4][:, :], w_d[0][:, k, m * P:m * P + P],
                                  zT[:, k, n * 512:n * 512 + 512], start=(k == 0), stop=(k == DT - 1))
                i.then_inc(d_qd, 1)
            pe.wait_ge(d_q_out, 8)
            for half in range(2):
                b0 = half * (B // 2)
                for c in range(16):
                    h, dt = c // 2, c % 2
                    r = (h % 2) * 64
                    if c >= 4:
                        pe.wait_ge((d_qk_act, d_qk_dve)[c % 2], 8 * half + (c - 4) // 2 + 1)
                    elif half:
                        pe.wait_ge(d_x, 4)
                    pe.matmul(bank[c % 4][:, :], w_d[1][r:r + 64, h // 2, dt * P:dt * P + P],
                              d_q[r:r + 64, h // 2, half * 512:half * 512 + 512], start=True, stop=True).then_inc(d_qkd, 1)
                pe.wait_ge(d_qk_act, 8 * (half + 1))
                pe.wait_ge(d_qk_dve, 8 * (half + 1))

                def scores(bb):
                    b = b0 + bb
                    s = (b // BG) % 2
                    if b % BG == 0:
                        pe.wait_ge(keys_loaded[3][s], 16 * (b // BG // 2 + 1))
                    for j in range(2):
                        if b >= 1:
                            pe.wait_ge(d_exp, 2 * b - 1 + j)
                        for k in range(DT):
                            i = pe.matmul(bank[j][:, 0:NK], d_qk[:, k, bb, j * P:j * P + P], ringT[s][:, k, b % BG, :],
                                          start=(k == 0), stop=(k == DT - 1))
                        i.then_inc(d_s, 1)

                def turn(bb):
                    b = b0 + bb
                    pe.wait_ge(d_norm, 2 * b + 2)
                    if b >= 1:
                        pe.wait_ge(d_turned, b)
                    for j in range(2):
                        p = d_p[b % 2][j]
                        for k in range(2):
                            pe.transpose(bank[2 + b % 2][:, k * 256 + j * P:k * 256 + j * P + P],
                                         p[:, k * P:k * P + P], ident)
                        i = pe.transpose(bank[6][0:1, j * P:j * P + P], p[:, NK - 1:NK], ident)
                    i.then_inc(d_turn, 1)

                def values(bb):
                    b = b0 + bb
                    s = (b // BG) % 2
                    pe.wait_ge(d_turned, b + 1)
                    if b % BG == 0:
                        pe.wait_ge(rows_loaded[3][s], 32 * (b // BG // 2 + 1))
                    if b >= 2:
                        pe.wait_ge(d_a_out, b - 1)
                    for dt in range(DT):
                        o = bank[4 + b % 2][:, dt * 256:dt * 256 + 256]
                        for k in range(2):
                            pe.matmul(o, ringN[s][:, b % BG, k, dt * P:dt * P + P], d_pT[b % 2][:, k, :],
                                      start=(k == 0), stop=False)
                        c = (b % BG) * D + dt * P
                        i = pe.matmul(o, ringL[s][0:1, c:c + P], d_last[b % 2], start=False, stop=True)
                    i.then_inc(d_av, 1)

                staggered(B // 2, scores, turn, values)
                pe.wait_ge(d_a_out, (half + 1) * (B // 2))
                for m in range(XI // P):
                    if m >= 2:
                        pe.wait_ge(d_o_out, 4 * half + m - 1)
                    for h in (2 * m, 2 * m + 1):
                        r = (h % 2) * 64
                        for k in range(DT):
                            i = pe.matmul(bank[6 + m % 2][r:r + 64, :], w_d[2][:, k, h * XD:h * XD + XD],
                                          d_aT[:, k, :, h * L:h * L + L], start=(k == 0), stop=(k == DT - 1))
                    i.then_inc(d_o, 1)
                pe.wait_ge(d_o_out, 4 * (half + 1))
                for g in range(4 * half, 4 * half + 4):
                    if g % 4 >= 2:
                        pe.wait_ge(d_x, g - 1)
                    for m in range(XI // P):
                        pe.matmul(bank[g % 2][:, 0:D], d_oT[:, m, g * P:g * P + P], w_d[3][:, m, :],
                                  start=(m == 0), stop=False)
                    pe.matmul(bank[g % 2][:, 0:D], ones[0:1, :], brow[0:1, R_BO:R_BO + D],
                              start=False, stop=True).then_inc(d_y, 1)

        def act_stage_d(act):
            for c in range(8):
                m, n = c % 4, c // 4
                act.wait_ge(d_qd, c + 1)
                act.activation(d_q[:, m, n * 512:n * 512 + 512], bank[4 + c % 4][:, :], ACT.Copy).then_inc(d_q_out, 1)
            for half in range(2):
                for c in range(0, 16, 2):
                    act.wait_ge(d_qkd, 16 * half + c + 1)
                    act.activation(d_qk[:, 0, :, (c // 2) * L:(c // 2) * L + L],
                                   bank[c % 4][:, :].rearrange("p (b i) -> p b i", i=L), ACT.Copy).then_inc(d_qk_act, 1)

                def exps(bb):
                    b = half * (B // 2) + bb
                    for j in range(2):
                        t = 2 * b + j
                        act.wait_ge(d_nbias, t + 1)
                        if b >= 2:
                            act.wait_ge(d_turn, b - 1)
                        act.activation(d_p[b % 2][j], bank[j][:, 0:NK], ACT.Exp, bias=d_nb[:, t:t + 1],
                                       scale=XD ** -0.5, accum_out=d_sum[:, t:t + 1]).then_inc(d_exp, 1)

                def turned(bb):
                    b = half * (B // 2) + bb
                    act.wait_ge(d_turn, b + 1)
                    if b >= 2:
                        act.wait_ge(d_av, b - 1)
                    act.activation(d_pT[b % 2].rearrange("p k r -> p (k r)"), bank[2 + b % 2][:, :], ACT.Copy)
                    act.activation(d_last[b % 2], bank[6][0:1, 0:256], ACT.Copy).then_inc(d_turned, 1)

                staggered(B // 2, exps, turned)
                for m in range(XI // P):
                    act.wait_ge(d_o, 4 * half + m + 1)
                    act.activation(d_oT[:, m, half * 512:half * 512 + 512], bank[6 + m % 2][:, :], ACT.Copy).then_inc(d_o_out, 1)

        def dve_stage_d(dve):
            for half in range(2):
                for c in range(1, 16, 2):
                    dve.wait_ge(d_qkd, 16 * half + c + 1)
                    dve.tensor_copy(d_qk[:, 1, :, (c // 2) * L:(c // 2) * L + L],
                                    bank[c % 4][:, :].rearrange("p (b i) -> p b i", i=L)).then_inc(d_qk_dve, 1)

                def maxima(bb):
                    for j in range(2):
                        t = 2 * (half * (B // 2) + bb) + j
                        dve.wait_ge(d_s, t + 1)
                        link(dve, dve.tensor_reduce(d_mx[:, t:t + 1], bank[j][:, 0:NK], AX_X, ALU.max))
                        dve.tensor_scalar(d_nb[:, t:t + 1], d_mx[:, t:t + 1], -XD ** -0.5, None,
                                          ALU.mult).then_inc(d_nbias, 1)

                def normalize(bb):
                    b = half * (B // 2) + bb
                    dve.wait_ge(d_exp, 2 * b + 2)
                    link(dve, dve.reciprocal(d_inv[:, 2 * b:2 * b + 2], d_sum[:, 2 * b:2 * b + 2]))
                    for j in range(2):
                        p = d_p[b % 2][j]
                        dve.tensor_scalar(p, p, d_inv[:, 2 * b + j:2 * b + j + 1], None, ALU.mult).then_inc(d_norm, 1)

                def values_out(bb):
                    b = half * (B // 2) + bb
                    dve.wait_ge(d_av, b + 1)
                    dve.tensor_copy(d_aT[:, :, bb, :], bank[4 + b % 2][:, :].rearrange("p (k r) -> p k r", k=DT)).then_inc(d_a_out, 1)

                for t in range(B // 2 + 2):
                    if t >= 2:
                        values_out(t - 2)
                    if t < B // 2:
                        maxima(t)
                        normalize(t)
                for g in range(4 * half, 4 * half + 4):
                    dve.wait_ge(d_y, g + 1)
                    dve.tensor_tensor(x[:, g, :], bank[g % 2][:, 0:D], x[:, g, :], ALU.add).then_inc(d_x, 1)
            dve.wait_ge(d_x, G)

        f_z = split("f_z", 0, DT, T)
        f_w1 = split("f_w1", 4096, DT, I1)
        f_w2 = split("f_w2", 8192, I1 // P, D)
        f_hT = [split(f"f_hT{s}", 12288 + 8192 * s, I1 // P, 512) for s in range(2)]
        f_raw1, f_raw2 = area(28672, DT, I1), area(30720, I1 // P, D)
        f_tmp = [area(32768 + 512 * s, 512) for s in range(2)]
        f_r1 = w_odd[:, 0:1024].rearrange("p (k n) -> p k n", k=DT)
        f_r2 = w_odd[:, 1024:1024 + RH // P * E1].rearrange("p (k n) -> p k n", k=RH // P)
        f_rh = area(24576, RH // P, T)
        f_p, f_rank = area(33792, G, E1), area(33824, G, E1)
        f_cw = area(33856, G, E1)
        f_gt, f_eq = area(33888, G, E1, E1), area(34016, G, E1, E1)
        f_m, f_r = small[:, 0:G], small[:, 8:16]
        f_loaded = [sem("f_loaded_w1"), sem("f_loaded_w2")]
        f_split = [sem("f_split_w1"), sem("f_split_w2")]
        (f_rhd, f_rh_out, f_logit, f_sub, f_exp, f_cwd, f_h, f_gel, f_y, f_x, f_z_hi, f_z_lo, f_hi, f_lo) = (
            sem("f_" + n) for n in ("rh", "rh_out", "logit", "sub", "exp", "cw", "h", "gel", "y", "x",
                                    "z_hi", "z_lo", "hi", "lo"))
        NF = 2 * E1

        def sp_stage_f(sp):
            for e in range(E1):
                for j, (raw, name) in enumerate(((f_raw1, "f_w1"), (f_raw2, "f_w2"))):
                    if e == 0 and j == 0:
                        sp.wait_ge(x_done, 5)
                    if e >= 1:
                        sp.wait_ge(f_split[j], 2 * e)
                    sp.dma_start(raw.rearrange("p k n -> p (k n)"), a[name][e]).then_inc(f_loaded[j], 16)

        def pool_stage_f(pool):
            for e in range(E1):
                for j, (raw, (hi, lo)) in enumerate(((f_raw1, f_w1), (f_raw2, f_w2))):
                    pool.wait_ge(f_loaded[j], 16 * (e + 1))
                    if e >= 1:
                        pool.wait_ge(*((f_h, 16 * e), (f_y, 8 * e))[j])
                    pool.tensor_copy(hi, raw).then_inc(f_split[j], 1)
                    pool.wait_ge(f_split[j], 2 * e + 1)
                    pool.tensor_tensor(lo, raw, hi.bitcast(F32), ALU.subtract).then_inc(f_split[j], 1)

        def pe_stage_f(pe):
            pe.wait_ge(w_loaded[5], 16)
            for c in range(8):
                m, n = c % 4, c // 4
                if c >= 4:
                    pe.wait_ge(f_rh_out, c - 3)
                for k in range(DT):
                    i = pe.matmul(bank[c % 4][:, :], f_r1[:, k, m * P:m * P + P],
                                  zT[:, k, n * 512:n * 512 + 512], start=(k == 0), stop=(k == DT - 1))
                i.then_inc(f_rhd, 1)

            def first(i):
                e, n = i // 2, i % 2
                if n == 0:
                    pe.wait_ge(f_split[0], 2 * (e + 1))
                for m in range(I1 // P):
                    c = 8 * i + m
                    if c >= 4:
                        pe.wait_ge(f_gel, c - 3)
                    else:
                        pe.wait_ge(f_rh_out, 5 + c)
                    if c == 0:
                        pe.wait_ge(f_z_hi, 2)
                        pe.wait_ge(f_z_lo, 2)
                    for k in range(DT):
                        j = matmul3(pe, bank[c % 4][:, :], f_w1, f_z, (slice(None), k, slice(m * P, m * P + P)),
                                    (slice(None), k, slice(n * 512, n * 512 + 512)), k == 0, k == DT - 1)
                    j.then_inc(f_h, 1)

            def logits():
                pe.wait_ge(f_rh_out, 8)
                for g in range(G):
                    o = bank[4][:, g * E1:g * E1 + E1]
                    for m in range(RH // P):
                        pe.matmul(o, f_rh[:, m, g * P:g * P + P], f_r2[:, m, :], start=(m == 0), stop=False)
                    j = pe.matmul(o, ones[0:1, :], brow[0:1, R_RB2:R_RB2 + E1], start=False, stop=True)
                j.then_inc(f_logit, 1)

            def second(i):
                e, n = i // 2, i % 2
                pe.wait_ge(f_lo, 8 * (i + 1))
                if n == 0:
                    pe.wait_ge(f_split[1], 2 * (e + 1))
                if i == 0:
                    pe.wait_ge(f_sub, 1)
                for g in range(4):
                    if i >= 1:
                        pe.wait_ge(f_x, 4 * (i - 1) + g + 1)
                    o = bank[4 + g][:, 0:D]
                    for m in range(I1 // P):
                        matmul3(pe, o, f_hT[i % 2], f_w2, (slice(None), m, slice(g * P, g * P + P)),
                                (slice(None), m), m == 0, False)
                    pe.matmul(o, ones[0:1, :], brow[0:1, R_BE2 + e * D:R_BE2 + (e + 1) * D],
                              start=False, stop=True).then_inc(f_y, 1)

            logits()
            for e in range(E1):
                first(2 * e)
                first(2 * e + 1)
                second(2 * e)
                second(2 * e + 1)

        def act_stage_f(act):
            act.wait_ge(ln_zT_act, 12)
            act.wait_ge(ln_zT_dve, 12)
            for n in range(2):
                act.activation(f_z[0][:, :, n * 512:n * 512 + 512], zT[:, :, n * 512:n * 512 + 512],
                               ACT.Copy).then_inc(f_z_hi, 1)
            for c in range(8):
                m, n = c % 4, c // 4
                act.wait_ge(f_rhd, c + 1)
                act.activation(f_rh[:, m, n * 512:n * 512 + 512], bank[c % 4][:, :], ACT.Gelu,
                               bias=bcol[:, K_RB1 + m:K_RB1 + m + 1]).then_inc(f_rh_out, 1)
            act.wait_ge(f_sub, 1)
            act.activation(f_p, f_p, ACT.Exp).then_inc(f_exp, 1)
            for c in range(8 * NF):
                e, m = c // 16, c % 8
                act.wait_ge(f_h, c + 1)
                if c >= 2:
                    act.wait_ge(f_lo, c - 1)
                act.activation(f_tmp[c % 2], bank[c % 4][:, :], ACT.Gelu,
                               bias=bcol[:, K_BE1 + e * 8 + m:K_BE1 + e * 8 + m + 1]).then_inc(f_gel, 1)

        def dve_stage_f(dve):
            for n in range(2):
                dve.wait_ge(f_z_hi, n + 1)
                c = slice(n * 512, n * 512 + 512)
                dve.tensor_tensor(f_z[1][:, :, c], zT[:, :, c], f_z[0][:, :, c].bitcast(F32),
                                  ALU.subtract).then_inc(f_z_lo, 1)
            dve.wait_ge(f_logit, 1)
            lg = bank[4][:, 0:G * E1].rearrange("p (g e) -> p g e", g=G)
            m_b, r_b = (t[:, :, None].broadcast_to([P, G, E1]) for t in (f_m, f_r))
            link(dve, dve.tensor_reduce(f_m, lg, AX_X, ALU.max))
            dve.tensor_tensor(f_p, lg, m_b, ALU.subtract).then_inc(f_sub, 1)
            dve.wait_ge(f_exp, 1)
            link(dve, dve.tensor_reduce(f_r, f_p, AX_X, ALU.add))
            link(dve, dve.reciprocal(f_r, f_r))
            link(dve, dve.tensor_tensor(f_p, f_p, r_b, ALU.mult))
            other = f_p[:, :, None, :].broadcast_to([P, G, E1, E1])
            own = f_p[:, :, :, None].broadcast_to([P, G, E1, E1])
            tri = const[:, None, C_TRI:C_TRI + E1 * E1].broadcast_to([P, G, E1 * E1])
            dve.tensor_tensor(f_gt, other, own, ALU.is_gt)
            link(dve, dve.tensor_tensor(f_eq, other, own, ALU.is_equal))
            eq, gt = (t.rearrange("p g e f -> p g (e f)") for t in (f_eq, f_gt))
            link(dve, dve.tensor_tensor(eq, eq, tri, ALU.mult))
            link(dve, dve.tensor_tensor(gt, gt, eq, ALU.add))
            link(dve, dve.tensor_reduce(f_rank, f_gt, AX_X, ALU.add))
            dve.scalar_tensor_tensor(out=f_cw, in0=f_rank, scalar=2.0, in1=f_p, op0=ALU.is_lt,
                                     op1=ALU.mult).then_inc(f_cwd, 1)
            dve.wait_ge(f_cwd, 1)

            def parts(i):
                for m in range(I1 // P):
                    c = 8 * i + m
                    dve.wait_ge(f_gel, c + 1)
                    if m == 0 and i >= 2:
                        dve.wait_ge(f_y, 4 * (i - 1))
                    hi, lo = (t[:, m, :] for t in f_hT[i % 2])
                    dve.tensor_copy(hi, f_tmp[c % 2]).then_inc(f_hi, 1)
                    dve.wait_ge(f_hi, c + 1)
                    dve.tensor_tensor(lo, f_tmp[c % 2], hi.bitcast(F32), ALU.subtract).then_inc(f_lo, 1)

            def residual(i):
                e, n = i // 2, i % 2
                for g in range(4):
                    dve.wait_ge(f_y, 4 * i + g + 1)
                    if e:
                        dve.wait_ge(f_x, 4 * (i - 2) + g + 1)
                    xs = x[:, 4 * n + g, :]
                    dve.scalar_tensor_tensor(out=xs, in0=bank[4 + g][:, 0:D], scalar=f_cw[:, 4 * n + g, e:e + 1],
                                             in1=xs, op0=ALU.mult, op1=ALU.add).then_inc(f_x, 1)

            for e in range(E1):
                parts(2 * e)
                parts(2 * e + 1)
                residual(2 * e)
                residual(2 * e + 1)

        block = ctx.enter_context(nc.Block())
        last = 5 if stop is None else stop

        @block.sync
        def _(sp):
            sp.dma_start(x[:, :, :], a["x"].rearrange("(g p) d -> p g d", p=P)).then_inc(loaded_x, 16)
            sp.dma_start(const[:, :], a["const"]).then_inc(loaded_c, 16)
            sp.dma_start(bcol[:, :], a["bcol"]).then_inc(loaded_c, 16)
            sp.dma_start(brow[:, :], a["brow"]).then_inc(loaded_c, 16)

            def weights(k):
                w = w_odd if k % 2 else w_even
                if k >= 2:
                    sp.wait_ge(x_done, k - 1)
                v = a[f"w{k}"]
                sp.dma_start(w[:, 0:v.shape[1]], v).then_inc(w_loaded[k], 16)

            weights(0)
            weights(1)
            sp_stage_a(sp)
            for k, stage in ((2, sp_stage_c), (3, sp_stage_d), (4, None), (5, sp_stage_f)):
                if k > last:
                    break
                weights(k)
                if stage:
                    stage(sp)
            sp.wait_ge(x_done, last + 1)
            sp.dma_start(out.rearrange("(g p) d -> p g d", p=P), x[:, :, :]).then_inc(stored, 16)
            sp.wait_ge(stored, 16)

        stages = range(last + 1)

        @block.tensor
        def _(pe):
            for k in stages:
                pe_layernorm(k)
                (pe_stage_a, lambda e: pe_self(e, 1, w_b), pe_stage_c, pe_stage_d,
                 lambda e: pe_self(e, 4, w_e), pe_stage_f)[k](pe)

        @block.scalar
        def _(act):
            for k in stages:
                act_layernorm(k)
                (act_stage_a, lambda e: act_self(e, 1), act_stage_c, act_stage_d,
                 lambda e: act_self(e, 4), act_stage_f)[k](act)

        @block.vector
        def _(dve):
            dve.memset(ones[:, :], 1.0)
            for k in stages:
                dve_layernorm(k)
                (dve_stage_a, lambda e: dve_self(e, 1), dve_stage_c, dve_stage_d,
                 lambda e: dve_self(e, 4), dve_stage_f)[k](dve)
                if k == 5:
                    dve.wait_ge(f_x, 4 * NF)
                dve_end_stage(dve)

        @block.gpsimd
        def _(pool):
            if last >= 1:
                pool_self(pool, 1)
            if last >= 2:
                pool_stage_c(pool)
            if last >= 4:
                pool_self(pool, 4)
            if last >= 5:
                pool_stage_f(pool)


def constants():
    p = np.arange(P)
    c = np.zeros((P, C_END), np.float32)
    c[:, C_ID:C_ID + P] = np.eye(P)
    c[:, C_CAUSAL:C_CAUSAL + L] = np.where(np.arange(L)[None] <= (p % L)[:, None], 0.0, NEG)
    c[:, C_HEAD:C_HEAD + HPT] = (p // HD)[:, None] == np.arange(HPT)[None]
    c[:, C_BATCH:C_BATCH + BG] = (p // L)[:, None] == np.arange(BG)[None]
    c[:, C_INV:C_INV + L] = (1.0 / np.arange(1, L + 1))[None]
    exponent = np.arange(HD // 2, dtype=np.float32) * np.float32(2.0 / HD)
    inv_freq = np.float32(10000.0) ** (-exponent)
    angles = inv_freq[(p % HD) // 2][:, None] * np.arange(L, dtype=np.float32)[None]
    c[:, C_COS:C_COS + L] = np.cos(angles)
    c[:, C_SIN:C_SIN + L] = np.sin(angles) * np.where(p % 2 == 0, -1.0, 1.0)[:, None]
    e = np.arange(E1)
    c[:, C_TRI:C_TRI + E1 * E1] = (e[None, :] < e[:, None]).reshape(1, -1)
    return c


def tiled(w):
    k, n = w.shape
    return w.reshape(k // P, P, n).transpose(1, 0, 2).reshape(P, -1)


def lay_out(i):
    v = {}
    v["x"] = i["x"].reshape(T, D)
    v["const"] = constants()
    col = lambda w: w.reshape(-1, P).T
    ba = i["L0_attn_b_attn"]
    v["bcol"] = np.concatenate([col(i["L0_xattn_b"]), col(ba[0:D]), col(ba[D:2 * D]), col(i["L1_ffn_rb1"]),
                                col(i["L1_ffn_be1"])], 1)
    v["brow"] = np.concatenate([i["L0_xattn_b"], ba[2 * D:], i["L0_attn_b_proj"], i["L1_xattn_bo"],
                                i["L1_ffn_rb2"], i["L1_ffn_be2"].reshape(-1)])[None]
    c = i["ctx_1024"].reshape(G, BG, NK, D)
    v["ctxT"] = c.reshape(G, BG, NK, DT, P).transpose(0, 4, 3, 1, 2).reshape(G, P, -1)
    v["ctx"] = c[:, :, 0:2 * P].reshape(G, BG, 2, P, D).transpose(0, 3, 1, 2, 4).reshape(G, P, -1)
    v["ctx_last"] = c[:, :, 2 * P].reshape(B, D)
    w = i["L0_xattn_W"]
    v["w0"] = np.concatenate([tiled(w), tiled(w.T)], 1)
    w = i["L0_attn_w_attn"]
    v["w1"] = np.concatenate([tiled(w[:, 0:D]), tiled(w[:, D:2 * D]), tiled(w[:, 2 * D:]), tiled(i["L0_attn_w_proj"])], 1)
    v["w2"] = np.concatenate([tiled(i["L0_ffn_Sg"].T), tiled(i["L0_ffn_Su"].T), tiled(i["L0_ffn_Sd"].T),
                              tiled(i["L0_ffn_gate_w"].T)], 1)
    v["w3"] = np.concatenate([tiled(i["L1_xattn_Wq"]), tiled(i["L1_xattn_Wk"].T), tiled(i["L1_xattn_Wv"]),
                              tiled(i["L1_xattn_Wo"])], 1)
    v["w4"] = np.concatenate([tiled(i[f"L1_attn_{n}"].T) for n in ("Wq", "Wk", "Wv", "Wo")], 1)
    v["w5"] = np.concatenate([tiled(i["L1_ffn_rW1"]), tiled(i["L1_ffn_rW2"])], 1)
    for n, s in (("we_g", "L0_ffn_Wg"), ("we_u", "L0_ffn_Wu"), ("we_d", "L0_ffn_Wd")):
        w = i[s].transpose(0, 2, 1)
        v[n] = w.reshape(E0, w.shape[1] // P, P, w.shape[2]).transpose(0, 2, 1, 3).reshape(E0, P, -1)
    for n, s in (("f_w1", "L1_ffn_We1"), ("f_w2", "L1_ffn_We2")):
        w = i[s]
        v[n] = w.reshape(E1, w.shape[1] // P, P, w.shape[2]).transpose(0, 2, 1, 3).reshape(E1, P, -1)
    return {k: np.ascontiguousarray(t) for k, t in v.items()}


def kernel(**inputs):
    import concourse.bacc as bacc
    from concourse.bass_utils import run_bass_kernel_spmd

    arrays = lay_out({k: np.asarray(t) for k, t in inputs.items()})
    nc = bacc.Bacc("TRN2", target_bir_lowering=False, num_devices=1)
    ins = {k: nc.dram_tensor(f"in_{k}", t.shape, mybir.dt.from_np(t.dtype), kind="ExternalInput").ap()
           for k, t in arrays.items()}
    out = nc.dram_tensor("out", [T, D], F32, kind="ExternalOutput").ap()
    build(nc, ins, out)
    r = run_bass_kernel_spmd(nc, [{f"in_{k}": t for k, t in arrays.items()}], core_ids=[0])
    return r.results[0]["out"].reshape(B, L, D)
```

```python
from contextlib import ExitStack

import concourse.bass as bass
import numpy as np
from concourse import mybir

F32 = mybir.dt.float32
F32R = mybir.dt.float32r
U32 = mybir.dt.uint32
ALU = mybir.AluOpType
ACT = mybir.ActivationFunctionType
AX_X = mybir.AxisListType.X

B, L, D = 32, 32, 256
NK = 257
P = 128
T = B * L
G = T // P
BG = P // L
DT = D // P
H, HD = 16, 16
HPT = P // HD
QH = P // L
NQ = H // QH
E0, I0, C0 = 16, 1024, 128
IS = 512
XH, XD = 8, 64
XI = XH * XD
E1, I1 = 4, 1024
RH = 512
HALF = T // 2
EDGE_ROWS = (0, 32, 64)
BIAS_ROWS = 33
NEG = -1.0e30
EPS = 1e-5

C_ID, C_CAUSAL, C_HEAD, C_BATCH, C_INV, C_COS, C_SIN, C_TRI, C_END = np.cumsum(
    [0, P, L, HPT, BG, L, L, L, E1 * E1]).tolist()
K_B, K_BQ, K_BK, K_RB1, K_BE1, K_END = np.cumsum([0, DT, DT, DT, RH // P, E1 * I1 // P]).tolist()
R_B, R_BV, R_BP, R_BO, R_RB2, R_BE2, R_END = np.cumsum([0, D, D, D, D, E1, E1 * D]).tolist()


def sort_steps(n):
    p = 1
    while p < n:
        k = p
        while k >= 1:
            yield p, k
            k //= 2
        p *= 2


def build(nc, a, out, stop=None):
    with ExitStack() as ctx:
        def sb(name, shape, dt=F32):
            return ctx.enter_context(nc.sbuf_tensor(name, shape, dt))

        def sem(name):
            return ctx.enter_context(nc.semaphore(name))

        bank = [ctx.enter_context(nc.psum_tensor(f"bank{i}", [P, 512], F32)) for i in range(8)]

        x = sb("x", [P, G, D])
        z = sb("z", [P, G, D])
        zT = sb("zT", [P, DT, T])
        const = sb("const", [P, C_END])
        bcol = sb("bcol", [P, K_END])
        brow = sb("brow", [BIAS_ROWS, R_END], F32R)
        ones = sb("ones", [BIAS_ROWS, P], F32R)
        w_even = sb("w_even", [P, 3072 + E0 * DT])
        w_odd_at = nc.sbuf_base
        w_odd = sb("w_odd", [P, 4096 + 64])
        stats = sb("stats", [P, G, 6])
        mv = sb("mv", [P, G, 2])
        veps = sb("veps", [P, G])
        std = sb("std", [P, G])
        rstd = sb("rstd", [P, G])
        small = sb("small", [P, 1024])
        arena_at = nc.sbuf_base
        arena = sb("arena", [P, 35904])
        z_dram = nc.dram_tensor("z_rows", [T, D], F32)
        acc_dram = nc.dram_tensor("acc_rows", [T, D], F32)

        def shaped(v, dims):
            if len(dims) == 1:
                return v
            names = "abcdef"[:len(dims)]
            return v.rearrange(f"p ({' '.join(names)}) -> p {' '.join(names)}",
                               **{c: d for c, d in zip(names[1:], dims[1:])})

        def area(off, *dims):
            return shaped(arena[:, off:off + int(np.prod(dims))], dims)

        def rounded(name, off, *dims):
            n = int(np.prod(dims))
            t = nc.alloc_sbuf_tensor_at(name, [P, n], F32R, offset=arena_at + 4 * off)
            return shaped(t[:, :], dims)

        def split(name, off, *dims):
            return rounded(name + "_hi", off, *dims), rounded(name + "_lo", off + int(np.prod(dims)), *dims)

        def matmul3(pe, o, lhsT, rhs, at_l, at_r, start, stop):
            for n, (i, j) in enumerate(((0, 0), (0, 1), (1, 0))):
                r = pe.matmul(o, lhsT[i][at_l], rhs[j][at_r], start=(start and n == 0), stop=(stop and n == 2))
            return r

        ident = const[:, C_ID:C_ID + P]
        brow_raw = area(26000, R_END)[0:1, :]
        bias_zero = area(26000 + R_END, R_END)[0:BIAS_ROWS, :]
        bias_one = area(26000 + 2 * R_END, P)[0:BIAS_ROWS, :]

        ln_var, ln_std, ln_z = sem("ln_var"), sem("ln_std"), sem("ln_z")
        ln_turned, ln_zT_act, ln_zT_dve = sem("ln_turned"), sem("ln_zT_act"), sem("ln_zT_dve")
        dve_chain, act_chain = sem("dve_chain"), sem("act_chain")
        loaded_x = [sem(f"loaded_x{half}") for half in range(2)]
        loaded_c, bias_raw, bias_set = sem("loaded_c"), sem("bias_raw"), sem("bias_set")
        w_loaded = [sem("w_even_loaded"), sem("w_odd_loaded")]
        x_done = sem("x_done")
        stored = sem("stored")
        tick = sb("tick", [P, 1])
        chain = {"dve": 0, "act": 0}
        WARM_ROPE, WARM_SORT, WARM_SORTED, WARM_ADDED, WARM_LN = 12, 8, 14, 10, 5
        LN_BANK = (0, 4, 4, 0, 4, 4)

        def link(eng, ins):
            name, s = ("dve", dve_chain) if eng is nc.vector else ("act", act_chain)
            chain[name] += 1
            ins.then_inc(s, 1)
            eng.wait_ge(s, chain[name])

        def sp_weights(sp, k):
            if k >= 2:
                sp.wait_ge(x_done, k - 1)
            v = a[f"w{k}"]
            sp.dma_start((w_even, w_odd)[k % 2][:, 0:v.shape[1]], v).then_inc(w_loaded[k % 2], 16)

        def wait_weights(pe, k):
            pe.wait_ge(w_loaded[k % 2], 16 * (k // 2 + 1))

        def dve_stats(dve, g):
            return dve.bn_stats(stats[:, g, :], x[:, g, :])

        def dve_variances(dve, half):
            gs = slice(4 * half, 4 * half + 4)
            for g in range(4 * half, 4 * half + 4):
                i = dve.bn_aggr(mv[:, g, :], stats[:, g, :])
            link(dve, i)
            dve.tensor_scalar(veps[:, gs], mv[:, gs, 1], EPS, None, ALU.add).then_inc(ln_var, 1)

        def dve_scale(dve, k, half):
            gs = slice(4 * half, 4 * half + 4)
            dve.wait_ge(ln_std, 2 * k + half + 1)
            link(dve, dve.reciprocal(rstd[:, gs], std[:, gs]))
            for g in range(4 * half, 4 * half + 4):
                dve.tensor_scalar(z[:, g, :], x[:, g, :], mv[:, g, 0:1], rstd[:, g:g + 1],
                                  ALU.subtract, ALU.mult).then_inc(ln_z, 1)

        def zT_out(k, j):
            return zT[:, :, 256 * j:256 * j + 256], bank[LN_BANK[k] + j][:, :].rearrange("p (k t) -> p k t", k=DT)

        def dve_zT(dve, k, half):
            dve.wait_ge(ln_turned, 4 * k + 2 * half + 2)
            dve.tensor_copy(*zT_out(k, 2 * half + 1)).then_inc(ln_zT_dve, 1)

        def dve_layernorm_end(dve, k):
            dve_variances(dve, 1)
            dve_zT(dve, k, 0)
            dve_scale(dve, k, 1)
            dve_zT(dve, k, 1)

        def dve_layernorm_loaded(dve, k, count):
            for half in range(2):
                dve.wait_ge(loaded_x[half], count)
                for g in range(4 * half, 4 * half + 4):
                    i = dve_stats(dve, g)
                link(dve, i)
                if half == 0:
                    dve_variances(dve, 0)
                    dve_scale(dve, k, 0)
            dve_layernorm_end(dve, k)

        def dve_added(dve, k, g, added):
            if g >= 1:
                dve.wait_ge(added, g)
                dve_stats(dve, g - 1)
            if g == 4:
                link(dve, dve.memset(tick[:, :], 0.0))
                dve_variances(dve, 0)
            if g == 6:
                dve_scale(dve, k + 1, 0)
            if g == 7:
                dve.wait_ge(added, G)
                link(dve, dve_stats(dve, 7))
                dve.memset(tick[:, :], 0.0).then_inc(x_done, 1)
                dve_layernorm_end(dve, k + 1)

        def act_std(act, k, half):
            act.wait_ge(ln_var, 2 * k + half + 1)
            gs = slice(4 * half, 4 * half + 4)
            act.activation(std[:, gs], veps[:, gs], ACT.Sqrt).then_inc(ln_std, 1)

        def act_zT(act, k, half):
            act.wait_ge(ln_turned, 4 * k + 2 * half + 1)
            act.activation(*zT_out(k, 2 * half), ACT.Copy).then_inc(ln_zT_act, 1)

        def act_layernorm(act, k):
            for half in range(2):
                act_std(act, k, half)
                act_zT(act, k, half)

        def pe_turn_z(pe, k, half):
            for j in (2 * half, 2 * half + 1):
                pe.wait_ge(ln_z, G * k + 2 * j + 2)
                for g in (2 * j, 2 * j + 1):
                    for dt in range(DT):
                        c = dt * 256 + (g % 2) * P
                        i = pe.transpose(bank[LN_BANK[k] + j][:, c:c + P], z[:, g, dt * P:dt * P + P], ident)
                i.then_inc(ln_turned, 1)

        def pe_wait_zT(pe, k, half):
            pe.wait_ge(ln_zT_act, 2 * k + half + 1)
            pe.wait_ge(ln_zT_dve, 2 * k + half + 1)

        def pe_keep_warm(pe, n, bank_no):
            for _ in range(n):
                pe.matmul(bank[bank_no][:, 0:256], ident, const[:, 0:256], start=True, stop=True)

        def staggered(n, *steps):
            for t in range(n + len(steps) - 1):
                for lag, step in reversed(list(enumerate(steps))):
                    if step is not None and 0 <= t - lag < n:
                        step(t - lag)

        ctxT_v = a["ctxT"]
        ctx_v = a["ctx"]
        last_v = a["ctx_last"]
        SLOTS = {0: 4, 3: 2}
        ringT = [area(2056 * s, DT, BG, NK) for s in (0, 1)] + [area(16384 + 2056 * s, DT, BG, NK) for s in (0, 1)]
        ringN = [area(4112 + 2048 * s, BG, 2, D) for s in (0, 1)] + [area(20496 + 2048 * s, BG, 2, D) for s in (0, 1)]
        ringL = [area(8208 + 1024 * s, 1024) for s in (0, 1)] + [area(24592 + 256 * s, 256) for s in (0, 1)]
        RING_END = 10256
        keys_loaded, rows_loaded = ([sem(f"{n}_loaded{s}") for s in range(4)] for n in ("keys", "rows"))
        KEYS_A, ROWS_A = 16 * G // SLOTS[0], 32 * G // SLOTS[0]
        wa_o = w_even[:, 0:DT * D].rearrange("p (k n) -> p k n", k=DT)
        wa_T = w_even[:, DT * D:2 * DT * D].rearrange("p (k n) -> p k n", k=DT)
        zwT = area(RING_END, DT, T)
        a_p = [area(RING_END + 2048 + 272 * s, NK) for s in range(2)]
        a_pT = [area(RING_END + 2592 + 384 * s, 384) for s in range(2)]
        a_att = [area(RING_END + 3360 + 256 * s, D) for s in range(2)]
        a_attT = [area(RING_END + 3872 + 256 * s, D) for s in range(2)]
        zb = small[:, 0:G]
        a_max, a_top, a_nb = small[:, 8:16], small[:, 16:24], small[:, 24:32]
        a_sum, a_inv = small[:, 32:40], small[:, 40:48]
        a_edge = [small[:, 48 + 4 * s:52 + 4 * s] for s in range(2)]
        a_zw, a_zw_out, a_zb, a_zb_out = sem("a_zw"), sem("a_zw_out"), sem("a_zb"), sem("a_zb_out")
        a_s, a_nbias, a_exp, a_edged, a_turn, a_turned = (
            sem("a_s"), sem("a_nbias"), sem("a_exp"), sem("a_edged"), sem("a_turn"), sem("a_turned"))
        a_av, a_norm, a_attturn, a_attturned, a_y, a_x = (
            sem("a_av"), sem("a_norm"), sem("a_attturn"), sem("a_attturned"), sem("a_y"), sem("a_x"))

        def sp_context(sp, k, keys_used, rows_used):
            n = SLOTS[k]
            for g in range(G):
                s = g % n
                if g >= n:
                    sp.wait_ge(keys_used[0], keys_used[1] * (g - n + 1))
                sp.dma_start(ringT[s], ctxT_v[g].rearrange("p (k b n) -> p k b n", k=DT, b=BG)).then_inc(keys_loaded[s], 16)
                if g >= n:
                    sp.wait_ge(rows_used[0], rows_used[1] * (g - n + 1))
                sp.dma_start(ringN[s], ctx_v[g].rearrange("p (b k d) -> p b k d", b=BG, k=2)).then_inc(rows_loaded[s], 16)
                lasts = last_v[g * BG:g * BG + BG, :]
                if k == 0:
                    sp.dma_start(ringL[s][0:BG, 0:D], lasts).then_inc(rows_loaded[s], 16)
                else:
                    for r in EDGE_ROWS:
                        sp.dma_start(ringL[s][r:r + 1, :].rearrange("o (b d) -> o b d", b=BG),
                                     lasts[None]).then_inc(rows_loaded[s], 16)

        def sp_stage_a(sp):
            sp_context(sp, 0, (a_s, 1), (a_av, 1))

        def pe_stage_a(pe):
            wait_weights(pe, 0)
            for n in range(2):
                if n:
                    pe_turn_z(pe, 0, 1)
                pe_wait_zT(pe, 0, n)
                for m in range(DT):
                    for k in range(DT):
                        i = pe.matmul(bank[4 + 2 * n + m][:, :], wa_o[:, k, m * P:m * P + P],
                                      zT[:, k, n * 512:n * 512 + 512], start=(k == 0), stop=(k == DT - 1))
                    i.then_inc(a_zw, 1)
            for g in range(G):
                for k in range(DT):
                    i = pe.matmul(bank[0][:, g:g + 1], zT[:, k, g * P:g * P + P],
                                  bcol[:, K_B + k:K_B + k + 1], start=(k == 0), stop=(k == DT - 1))
            i.then_inc(a_zb, 1)
            pe.wait_ge(a_zw_out, 4)
            pe.wait_ge(a_zb_out, 1)

            def scores(g):
                pe.wait_ge(keys_loaded[g % 4], 16 * (g // 4 + 1))
                if g >= 2:
                    pe.wait_ge(a_exp, g - 1)
                for b in range(BG):
                    c = g * P + b * L
                    for k in range(DT):
                        i = pe.matmul(bank[g % 2][b * L:b * L + L, 0:NK], zwT[:, k, c:c + L],
                                      ringT[g % 4][:, k, b, :], start=(k == 0), stop=(k == DT - 1))
                i.then_inc(a_s, 1)

            def turn_p(g):
                pe.wait_ge(a_edged, g + 1)
                if g >= 2:
                    pe.wait_ge(a_turned, g - 1)
                bk, p = bank[2 + g % 2], a_p[g % 2]
                pe.transpose(bk[:, 0:P], p[:, 0:P], ident)
                pe.transpose(bk[:, P:2 * P], p[:, P:2 * P], ident)
                pe.transpose(bk[0:BG, 2 * P:3 * P], a_edge[g % 2], ident).then_inc(a_turn, 1)

            def values(g):
                pe.wait_ge(a_turned, g + 1)
                pe.wait_ge(rows_loaded[g % 4], 32 * (g // 4 + 1))
                if g >= 2:
                    pe.wait_ge(a_norm, g - 1)
                o, pT = bank[4 + g % 2], a_pT[g % 2]
                for b in range(BG):
                    for k in range(2):
                        pe.matmul(o[b * L:b * L + L, 0:D], pT[:, k * P + b * L:k * P + b * L + L],
                                  ringN[g % 4][:, b, k, :], start=(k == 0), stop=False, skip_group_check=True)
                pe.matmul(o[:, 0:D], pT[0:BG, 2 * P:3 * P], ringL[g % 4][0:BG, 0:D],
                          start=False, stop=True, skip_group_check=True).then_inc(a_av, 1)

            def turn_att(g):
                pe.wait_ge(a_norm, g + 1)
                if g >= 1:
                    pe.wait_ge(a_attturned, g)
                pe.transpose(bank[6][:, 0:P], a_att[g % 2][:, 0:P], ident)
                pe.transpose(bank[6][:, P:2 * P], a_att[g % 2][:, P:2 * P], ident).then_inc(a_attturn, 1)

            def project(g):
                pe.wait_ge(a_attturned, g + 1)
                if g == 0:
                    pe.wait_ge(bias_set, 3)
                if g >= 1:
                    pe.wait_ge(a_x, g)
                for k in range(DT):
                    pe.matmul(bank[7][:, 0:D], a_attT[g % 2][:, k * P:k * P + P], wa_T[:, k, :],
                              start=(k == 0), stop=False)
                pe.matmul(bank[7][:, 0:D], ones[:, :], brow[:, R_B:R_B + D],
                          start=False, stop=True).then_inc(a_y, 1)

            staggered(G, scores, turn_p, values, turn_att, project)

        def act_stage_a(act):
            for j in range(4):
                act.wait_ge(a_zw, j + 1)
                m, n = j % 2, j // 2
                act.activation(zwT[:, m, n * 512:n * 512 + 512], bank[4 + j][:, :], ACT.Copy).then_inc(a_zw_out, 1)

            def exps(g):
                act.wait_ge(a_nbias, g + 1)
                if g >= 2:
                    act.wait_ge(a_turn, g - 1)
                act.activation(a_p[g % 2], bank[g % 2][:, 0:NK], ACT.Exp, bias=a_nb[:, g:g + 1],
                               accum_out=a_sum[:, g:g + 1]).then_inc(a_exp, 1)

            def turned_p(g):
                act.wait_ge(a_turn, g + 1)
                if g >= 2:
                    act.wait_ge(a_av, g - 1)
                act.activation(a_pT[g % 2][:, 0:2 * P], bank[2 + g % 2][:, 0:2 * P], ACT.Copy)
                act.activation(a_pT[g % 2][0:BG, 2 * P:3 * P], bank[2 + g % 2][0:BG, 2 * P:3 * P],
                               ACT.Copy).then_inc(a_turned, 1)

            def turned_att(g):
                act.wait_ge(a_attturn, g + 1)
                if g >= 2:
                    act.wait_ge(a_y, g - 1)
                act.activation(a_attT[g % 2], bank[6][:, 0:D], ACT.Copy).then_inc(a_attturned, 1)

            staggered(G, exps, turned_p, None, turned_att)

        def dve_stage_a(dve):
            dve.wait_ge(a_zb, 1)
            dve.tensor_copy(zb, bank[0][:, 0:G]).then_inc(a_zb_out, 1)
            dve.wait_ge(a_zb_out, 1)

            def maxima(g):
                dve.wait_ge(a_s, g + 1)
                c = slice(g, g + 1)
                link(dve, dve.tensor_reduce(a_max[:, c], bank[g % 2][:, 0:NK], AX_X, ALU.max))
                link(dve, dve.tensor_tensor(a_top[:, c], a_max[:, c], zb[:, c], ALU.add))
                dve.tensor_tensor(a_nb[:, c], zb[:, c], a_top[:, c], ALU.subtract).then_inc(a_nbias, 1)

            def edges(g):
                dve.wait_ge(a_exp, g + 1)
                dve.reciprocal(a_inv[:, g:g + 1], a_sum[:, g:g + 1])
                dve.tensor_scalar(a_edge[g % 2], const[:, C_BATCH:C_BATCH + BG], a_p[g % 2][:, NK - 1:NK], None,
                                  ALU.mult).then_inc(a_edged, 1)

            def normalize(g):
                dve.wait_ge(a_av, g + 1)
                dve.wait_ge(a_edged, g + 1)
                if g >= 2:
                    dve.wait_ge(a_attturn, g - 1)
                dve.tensor_scalar(a_att[g % 2], bank[4 + g % 2][:, 0:D], a_inv[:, g:g + 1], None,
                                  ALU.mult).then_inc(a_norm, 1)

            def residual(g):
                dve.wait_ge(a_y, g + 1)
                dve.scalar_tensor_tensor(out=x[:, g, :], in0=bank[7][:, 0:D], scalar=0.0, in1=x[:, g, :],
                                         op0=ALU.max, op1=ALU.add).then_inc(a_x, 1)
                dve_added(dve, 0, g, a_x)

            def maxima_edges(g):
                maxima(g)
                edges(g)

            staggered(G, maxima_edges, None, normalize, None, residual)

        Kx = area(0, 2, DT, B // 2, HPT, L)
        Vx = area(16384, B, NQ, QH, HD)
        S = area(24576, G, H * L)
        S_rows = S.rearrange("p g (h j) -> p (g h) j", j=L)
        qT = area(28672, DT, T)
        kT = area(30720, DT, T)
        pT = [area(32768 + 512 * s, NQ, P) for s in range(2)]
        vrow = area(33792, G, D)
        yT = area(28672, DT, T)
        HR = G * H // 2
        sort_a, sort_b = area(0, HR, L), area(2048, HR, L)
        notfirst = area(4096, HR, L)
        sums = area(6144, HR, L)
        rot = z[:, :, :].rearrange("p g d -> p (g d)")[:, 0:DT * HALF].rearrange("p (k t) -> p k t", k=DT)
        SELF_SEMS = ("proj", "k_out", "q_out", "v", "v_out", "vx", "kx_act", "kx_dve", "masked", "s",
                     "lowered", "probs", "turn", "turned", "av", "y", "out", "added")
        self_sems = {k: {s: sem(f"{n}_{s}") for s in SELF_SEMS + more}
                     for k, n, more in ((1, "b", ("kx_pool", "s_out", "sorted", "carried", "flagged")), (4, "e", ("rope", "exp")))}
        stat = small[:, 0:G * H]
        bq_scaled = small[:, 128:128 + DT]
        stat_b = stat[:, :, None].broadcast_to([P, G * H, L])
        mask_of = {k: (nc.alloc_sbuf_tensor_at(f"mask{k}", [P, H * L], F32R, offset=w_odd_at + 4 * 2560),
                       nc.alloc_sbuf_tensor_at(f"mask_ident{k}", [P, P], F32R, offset=w_odd_at + 4 * (2560 + H * L)))
                   for k in (1, 4)}

        def halves(t, m, n):
            return t[:, m, n * HALF:n * HALF + HALF].rearrange("p (b j) -> p b j", j=L)

        def pe_self(pe, k, w):
            q = self_sems[k]
            logits_gone = q["s_out" if k == 1 else "lowered"]
            wait_weights(pe, k)

            def project_in(n):
                for c in range(4):
                    j, m = 1 - c // 2, c % 2
                    if n:
                        pe.wait_ge(logits_gone, c + 1)
                    elif k == 4 and c >= 2:
                        pe.wait_ge(d_x, G - 3 + c)
                    for kk in range(DT):
                        i = pe.matmul(bank[c][:, :], w(j)[:, kk, m * P:m * P + P],
                                      zT[:, kk, n * HALF:n * HALF + HALF], start=(kk == 0), stop=(kk == DT - 1))
                    i.then_inc(q["proj"], 1)

            def values_in(g):
                if g >= 4:
                    pe.wait_ge(q["v_out"], g - 3)
                o = bank[4 + g % 4][:, 0:D]
                for kk in range(DT):
                    i = pe.matmul(o, zT[:, kk, g * P:g * P + P], w(2)[:, kk, :], start=(kk == 0),
                                  stop=(kk == DT - 1 and k == 4))
                if k == 1:
                    i = pe.matmul(o, ones[:, :], brow[:, R_BV:R_BV + D], start=False, stop=True)
                i.then_inc(q["v"], 1)

            def scores(g):
                half = g // 4
                if g % 4 == 0:
                    if k == 4 and half:
                        pe.wait_ge(q["added"], 4)
                    pe.wait_ge(q["k_out"], 2 * (half + 1))
                    pe.wait_ge(q["q_out"], 2 * (half + 1))
                    if k == 1:
                        pe.wait_ge(q["kx_act"], 8 * (half + 1))
                        pe.wait_ge(*((q["kx_pool"], 8) if half else (q["kx_dve"], 8)))
                    else:
                        pe.wait_ge(q["kx_act"], 8 * (half + 1))
                        pe.wait_ge(q["kx_dve"], 8 * (half + 1))
                        pe.wait_ge(q["rope"], 8 * (half + 1))
                if g == 0:
                    pe.wait_ge(q["masked"], 2)
                mask, mask_ident = mask_of[k]
                pe.matmul(bank[g % 4][:, :], mask_ident[:, :], mask[:, :], start=True, stop=False, skip_group_check=True)
                for b in range(BG):
                    c = g * P + b * L
                    for kk in range(DT):
                        i = pe.matmul(bank[g % 4][b * L:b * L + L, kk * 256:kk * 256 + 256], qT[:, kk, c:c + L],
                                      Kx[:, half, kk, g % 4 * BG + b, :, :].rearrange("p h j -> p (h j)"),
                                      start=False, stop=(b == BG - 1 and kk == DT - 1), skip_group_check=True)
                i.then_inc(q["s"], 1)

            def turn(g):
                pe.wait_ge(q["probs"], g + 1)
                if g == 0:
                    pe.wait_ge(q["v_out"], G)
                if g >= 2:
                    pe.wait_ge(q["turned"], g - 1)
                for m in range(NQ):
                    i = pe.transpose(bank[4 + g % 2][:, m * P:m * P + P], S[:, g, m * P:m * P + P], ident)
                i.then_inc(q["turn"], 1)

            def values(g):
                pe.wait_ge(q["turned"], g + 1)
                if g % 4 == 0:
                    pe.wait_ge(q["vx"], g // 4 + 2)
                if g >= 1:
                    pe.wait_ge(q["y"], g)
                for b in range(BG):
                    for m in range(NQ):
                        r, kk = (m % 2) * 64, m // 2
                        c = kk * P + b * L
                        i = pe.matmul(bank[6][r:r + 64, c:c + L],
                                      Vx[:, g * BG + b, m, :, :].rearrange("p h d -> p (h d)"),
                                      pT[g % 2][:, m, b * L:b * L + L], start=True, stop=True)
                i.then_inc(q["av"], 1)

            def project(g):
                pe.wait_ge(q["y"], g + 1)
                if k == 4 and g == 0:
                    pe.wait_ge(q["k_out"], 4)
                    pe.wait_ge(q["q_out"], 4)
                elif k == 1 and g < 4 or k == 4 and g >= 4:
                    pe.wait_ge(logits_gone, g % 4 + 5)
                elif k == 1:
                    pe.wait_ge(q["added"], g - 3)
                o = bank[g % 4][:, 0:D]
                for kk in range(DT):
                    i = pe.matmul(o, yT[:, kk, g * P:g * P + P], w(3)[:, kk, :], start=(kk == 0),
                                  stop=(kk == DT - 1 and k == 4))
                if k == 1:
                    i = pe.matmul(o, ones[:, :], brow[:, R_BP:R_BP + D], start=False, stop=True)
                i.then_inc(q["out"], 1)

            def attend(first, end):
                for g in range(first, end + 2):
                    if g < end:
                        turn(g)
                    if first <= g - 1 < end:
                        values(g - 1)
                    if first <= g - 2:
                        project(g - 2)

            pe_wait_zT(pe, k, 0)
            project_in(0)
            pe_turn_z(pe, k, 1)
            pe_wait_zT(pe, k, 1)
            for g in range(G if k == 4 else 4):
                values_in(g)
            if k == 4:
                pe.wait_ge(q["q_out"], 2)
                pe_keep_warm(pe, WARM_ROPE, 3)
            for g in range(4):
                scores(g)
            for g in range(G if k == 4 else 4, G):
                values_in(g)
            project_in(1)
            if k == 1:
                pe.wait_ge(q["v_out"], G)
                pe.wait_ge(q["sorted"], 26)
                pe_keep_warm(pe, WARM_SORT, 7)
                for g in range(4, G):
                    scores(g)
            attend(0, 4)
            if k == 4:
                pe_keep_warm(pe, WARM_ROPE, 7)
                for g in range(4, G):
                    scores(g)
            else:
                pe.wait_ge(q["sorted"], 60)
                pe_keep_warm(pe, WARM_SORTED, 7)
            attend(4, G)

        def act_spread_keys(act, q, m, n, heads=range(HPT)):
            for h in heads:
                act.activation(Kx[:, n, m, :, h, :], halves(kT, m, n), ACT.Copy,
                               scale=const[:, C_HEAD + h:C_HEAD + h + 1]).then_inc(q["kx_act"], 1)

        def act_turned(act, q, g):
            act.wait_ge(q["turn"], g + 1)
            if g >= 2:
                act.wait_ge(q["av"], g - 1)
            act.activation(pT[g % 2].rearrange("p m t -> p (m t)"), bank[4 + g % 2][:, :],
                           ACT.Copy).then_inc(q["turned"], 1)

        def act_values_out(act, q, g):
            act.wait_ge(q["av"], g + 1)
            act.activation(yT[:, :, g * P:g * P + P], bank[6][:, 0:D].rearrange("p (k t) -> p k t", k=DT),
                           ACT.Copy).then_inc(q["y"], 1)

        def act_attend(act, q, first, end):
            for g in range(first, end + 1):
                if g < end:
                    act_turned(act, q, g)
                if g > first:
                    act_values_out(act, q, g - 1)

        def act_stage_b(act):
            q = self_sems[1]

            def keys(n):
                for m in range(DT):
                    act.wait_ge(q["proj"], 4 * n + m + 1)
                    act.activation(kT[:, m, n * HALF:n * HALF + HALF], bank[m][:, :], ACT.Identity,
                                   bias=bcol[:, K_BK + m:K_BK + m + 1]).then_inc(q["k_out"], 1)
                act.wait_ge(q["k_out"], 2 * n + 2)

            def values_in(g):
                act.wait_ge(q["v"], g + 1)
                act.activation(vrow[:, g, :], bank[4 + g % 4][:, 0:D], ACT.Copy).then_inc(q["v_out"], 1)

            def logits_out(g):
                act.wait_ge(q["s"], g + 1)
                act.activation(S[:, g, :], bank[g % 4][:, :], ACT.Copy).then_inc(q["s_out"], 1)

            keys(0)
            act_spread_keys(act, q, 0, 0)
            for g in range(4):
                values_in(g)
            for g in range(4):
                logits_out(g)

            def prepare(t):
                if t < 4:
                    values_in(4 + t)
                elif t == 4:
                    keys(1)
                elif t == 5:
                    for m in range(DT):
                        act.wait_ge(q["proj"], 7 + m)
                        act.activation(qT[:, m, HALF:T], bank[2 + m][:, :], ACT.Identity, scale=HD ** -0.5,
                                       bias=bq_scaled[:, m:m + 1]).then_inc(q["q_out"], 1)
                else:
                    act_spread_keys(act, q, 0, 1, range(2 * (t - 6), 2 * (t - 5)))

            carried = 0

            def attend(t):
                if t < 4:
                    act_turned(act, q, t)
                if t >= 1:
                    act_values_out(act, q, t - 1)

            for half in range(2):
                src, dst = None, sort_a
                steps = 0
                for s, (p_, k_) in enumerate(sort_steps(L)):
                    if k_ < p_:
                        act.wait_ge(q["sorted"], 30 * half + 2 * s)
                        if carried:
                            act.wait_ge(q["carried"], carried)
                        c = 2 * p_ // k_
                        u = [t.rearrange("p r (c i) -> p r c i", i=k_) if c == L // k_ else
                             t.rearrange("p r (b c i) -> p (r b) c i", c=c, i=k_) for t in (src, dst)]
                        act.activation(u[1][:, :, 0:c:c - 1, :], u[0][:, :, 0:c:c - 1, :],
                                       ACT.Copy).then_inc(q["carried"], 1)
                        carried += 1
                        if half == 0:
                            prepare(steps)
                        elif steps in (0, 1, 3, 5, 7):
                            attend((0, 1, 3, 5, 7).index(steps))
                        steps += 1
                    src, dst = dst, (sort_b if dst is sort_a else sort_a)
                if half == 0:
                    for g in range(4, G):
                        logits_out(g)
                for g in range(4 * half, 4 * half + 4):
                    act.wait_ge(q["lowered"], g + 1)
                    act.activation(S[:, g, :], S[:, g, :], ACT.Relu).then_inc(q["probs"], 1)
            act_attend(act, q, 4, G)

        def act_stage_e(act):
            q = self_sems[4]

            def keys_queries(n):
                for c in range(4):
                    act.wait_ge(q["proj"], 4 * n + c + 1)
                    dst = (kT, qT)[c // 2]
                    act.activation(dst[:, c % 2, n * HALF:n * HALF + HALF], bank[c][:, :],
                                   ACT.Copy).then_inc(q[("k_out", "q_out")[c // 2]], 1)

            keys_queries(0)
            for g in range(G):
                act.wait_ge(q["v"], g + 1)
                act.activation(vrow[:, g, :], bank[4 + g % 4][:, 0:D], ACT.Copy).then_inc(q["v_out"], 1)
            act.wait_ge(q["rope"], 4)
            act_spread_keys(act, q, 0, 0)

            def exps(g):
                act.wait_ge(q["lowered"], g + 1)
                act.activation(S[:, g, :], S[:, g, :], ACT.Exp, scale=HD ** -0.5).then_inc(q["exp"], 1)

            for g in range(4):
                exps(g)
            keys_queries(1)
            act_attend(act, q, 0, 4)
            act.wait_ge(q["rope"], 12)
            act_spread_keys(act, q, 0, 1)
            for g in range(4, G + 3):
                if g < G:
                    exps(g)
                if 4 <= g - 2 < G:
                    act_turned(act, q, g - 2)
                if 4 <= g - 3:
                    act_values_out(act, q, g - 3)

        def pool_self(pool, k):
            q = self_sems[k]
            pool.wait_ge(x_done, k)
            mask, mask_ident = mask_of[k]
            pool.tensor_copy(mask[:, :].rearrange("p (h j) -> p h j", j=L),
                             const[:, None, C_CAUSAL:C_CAUSAL + L].broadcast_to([P, H, L])).then_inc(q["masked"], 1)
            pool.tensor_copy(mask_ident[:, :], ident).then_inc(q["masked"], 1)
            pool.memset(arena[:, 16384:24576], 0.0).then_inc(q["vx"], 1)
            pool.wait_ge(q["vx"], 1)
            if k == 1:
                pool.wait_ge(q["s"], 4)
                pool.memset(notfirst, 1.0).then_inc(q["flagged"], 1)
                pool.wait_ge(q["flagged"], 1)
                pool.memset(notfirst[:, :, 0:1], 0.0).then_inc(q["flagged"], 1)
                pool.wait_ge(q["flagged"], 2)
                pool.wait_ge(q["k_out"], 4)
                for h in range(HPT):
                    pool.tensor_scalar(Kx[:, 1, 1, :, h, :], halves(kT, 1, 1), const[:, C_HEAD + h:C_HEAD + h + 1],
                                       None, ALU.mult).then_inc(q["kx_pool"], 1)
                pool.wait_ge(q["kx_pool"], HPT)
            vx = Vx.rearrange("p (g b) m h d -> p g b m h d", b=BG)
            vr = vrow.rearrange("p g (m h d) -> p g m h d", m=NQ, h=QH)
            for half in range(2):
                gs = slice(4 * half, 4 * half + 4)
                pool.wait_ge(q["v_out"], 4 * half + 4)
                for b in range(BG):
                    for h in range(QH):
                        i = pool.tensor_copy(vx[h * L:h * L + L, gs, b, :, h, :], vr[b * L:b * L + L, gs, :, h, :])
                i.then_inc(q["vx"], 1)

        def dve_spread_keys(dve, q, m, n):
            for h in range(HPT):
                dve.tensor_scalar(Kx[:, n, m, :, h, :], halves(kT, m, n), const[:, C_HEAD + h:C_HEAD + h + 1], None,
                                  ALU.mult).then_inc(q["kx_dve"], 1)

        def dve_residual(dve, k, g):
            q = self_sems[k]
            dve.wait_ge(q["out"], g + 1)
            dve.tensor_tensor(x[:, g, :], bank[g % 4][:, 0:D], x[:, g, :], ALU.add).then_inc(q["added"], 1)
            dve_added(dve, k, g, q["added"])

        def dve_stage_b(dve):
            q = self_sems[1]

            def queries(n):
                for m in range(DT):
                    dve.wait_ge(q["proj"], 4 * n + 3 + m)
                    dve.tensor_scalar(qT[:, m, n * HALF:n * HALF + HALF], bank[2 + m][:, :],
                                      bcol[:, K_BQ + m:K_BQ + m + 1], HD ** -0.5, ALU.add,
                                      ALU.mult).then_inc(q["q_out"], 1)

            dve.tensor_scalar(bq_scaled, bcol[:, K_BQ:K_BQ + DT], HD ** -0.5, None, ALU.mult)
            queries(0)
            dve.wait_ge(q["k_out"], 2)
            dve_spread_keys(dve, q, 1, 0)
            carried = 0
            for half in range(2):
                dve.wait_ge(q["s_out"], 4 * half + 4)
                mine = slice(HR * half, HR * half + HR)
                src, dst = S_rows[:, mine, :], sort_a
                for s, (p_, k_) in enumerate(sort_steps(L)):
                    if s:
                        dve.wait_ge(q["sorted"], 30 * half + 2 * s)
                    if carried:
                        dve.wait_ge(q["carried"], carried)
                    u, v = (t.rearrange("p r (b n) -> p (r b) n", n=2 * p_) for t in (src, dst))
                    if k_ < p_:
                        u, v = (t[:, :, k_:2 * p_ - k_] for t in (u, v))
                        carried += 1
                    u, v = (t.rearrange("p r (m c i) -> p r m c i", c=2, i=k_) for t in (u, v))
                    lo, hi = u[:, :, :, 0, :], u[:, :, :, 1, :]
                    dve.tensor_tensor(v[:, :, :, 0, :], lo, hi, ALU.max).then_inc(q["sorted"], 1)
                    dve.tensor_tensor(v[:, :, :, 1, :], lo, hi, ALU.min).then_inc(q["sorted"], 1)
                    src, dst = dst, (sort_b if dst is sort_a else sort_a)
                dve.wait_ge(q["sorted"], 30 * half + 30)
                dve.wait_ge(q["carried"], carried)
                dve.wait_ge(q["flagged"], 2)
                flat = [t.rearrange("p r j -> p (r j)") for t in (sums, notfirst, src)]
                link(dve, dve.tensor_tensor_scan(flat[0], flat[1], flat[2], 0.0, ALU.mult, ALU.add))
                inv = const[:, None, C_INV:C_INV + L].broadcast_to([P, HR, L])
                link(dve, dve.scalar_tensor_tensor(out=sums, in0=sums, scalar=-1.0, in1=inv,
                                                   op0=ALU.add, op1=ALU.mult))
                link(dve, dve.tensor_reduce(stat[:, mine], sums, AX_X, ALU.max))
                for g in range(4 * half, 4 * half + 4):
                    r = slice(g * H, g * H + H)
                    dve.tensor_tensor(S_rows[:, r, :], S_rows[:, r, :], stat_b[:, r, :],
                                      ALU.subtract).then_inc(q["lowered"], 1)
            for g in range(G):
                dve_residual(dve, 1, g)

        def dve_stage_e(dve):
            q = self_sems[4]
            swap = [i ^ 1 for i in range(32)]
            cos, sin = (const[:, None, c:c + L].broadcast_to([P, B // 2, L]) for c in (C_COS, C_SIN))

            def rope(t, s, n):
                done = 8 * n + (0 if t is kT else 4)
                dve.wait_ge(q[s], 2 * n + 2)
                c = slice(n * HALF, n * HALF + HALF)
                for m in range(DT):
                    i = dve.stream_shuffle(rot[:, m, :], t[:, m, c], swap)
                link(dve, i)
                for m in range(DT):
                    r = rot[:, m, :].rearrange("p (b j) -> p b j", j=L)
                    dve.tensor_tensor(r, r, sin, ALU.mult)
                    i = dve.tensor_tensor(halves(t, m, n), halves(t, m, n), cos, ALU.mult)
                link(dve, i)
                for m in range(DT):
                    dve.tensor_tensor(t[:, m, c], t[:, m, c], rot[:, m, :], ALU.add).then_inc(q["rope"], 2)
                dve.wait_ge(q["rope"], done + 4)


            def lower(g):
                dve.wait_ge(q["s"], g + 1)
                r = slice(g * H, g * H + H)
                logits = bank[g % 4][:, :].rearrange("p (h j) -> p h j", j=L)
                link(dve, dve.tensor_reduce(stat[:, r], logits, AX_X, ALU.max))
                dve.tensor_tensor(S_rows[:, r, :], logits, stat_b[:, r, :],
                                  ALU.subtract).then_inc(q["lowered"], 1)

            def normalize(g):
                r = slice(g * H, g * H + H)
                dve.wait_ge(q["exp"], g + 1)
                link(dve, dve.tensor_reduce(stat[:, r], S_rows[:, r, :], AX_X, ALU.add))
                link(dve, dve.reciprocal(stat[:, r], stat[:, r]))
                dve.tensor_tensor(S_rows[:, r, :], S_rows[:, r, :], stat_b[:, r, :], ALU.mult).then_inc(q["probs"], 1)

            rope(kT, "k_out", 0)
            rope(qT, "q_out", 0)
            dve_spread_keys(dve, q, 1, 0)
            for g in range(4):
                lower(g)
            for g in range(4):
                normalize(g)
            rope(kT, "k_out", 1)
            for g in range(2):
                dve_residual(dve, 4, g)
            rope(qT, "q_out", 1)
            dve_spread_keys(dve, q, 1, 1)
            for g in range(2, 4):
                dve_residual(dve, 4, g)
            staggered(4, lambda g: lower(4 + g), lambda g: normalize(4 + g))
            for g in range(4, G):
                dve_residual(dve, 4, g)

        def w_b(j):
            return w_odd[:, j * DT * D:(j + 1) * DT * D].rearrange("p (k n) -> p k n", k=DT)

        def w_e(j):
            return w_even[:, j * DT * D:(j + 1) * DT * D].rearrange("p (k n) -> p k n", k=DT)

        we = [[area(6144 * s, DT, I0), area(6144 * s + 2048, DT, I0), area(6144 * s + 4096, I0 // P, D)]
              for s in range(3)]
        c_gate = w_even[:, 3072:3072 + DT * E0].rearrange("p (k n) -> p k n", k=DT)
        c_sg, c_su = (w_even[:, j * 1024:(j + 1) * 1024].rearrange("p (k n) -> p k n", k=DT) for j in range(2))
        c_sd = w_even[:, 2048:3072].rearrange("p (k n) -> p k n", k=IS // P)
        c_sT = area(18432, IS // P, T)
        c_tmp = [area(22528 + 512 * s, 512) for s in range(2)]
        c_up = [area(30624 + 512 * s, 512) for s in range(2)]
        c_sc = area(23552, T // 2)[0:32 + E0, :]
        c_val = area(24064, C0)[0:32 + E0, :]
        c_idx = area(24192, C0)[0:32 + E0, :].bitcast(U32)
        c_idxf = area(24320, C0)[0:32 + E0, :]
        c_val2, c_idx2 = area(24448, C0)[0:E0, :], area(24576, C0)[0:E0, :]
        c_first = area(24704, C0)[0:E0, :]
        c_p = area(24832, G, E0)
        c_valT = area(24960, E0)
        c_idxT = area(24976, E0).bitcast(U32)
        c_xg = area(24992, E0, D)
        c_xgT = [area(29088 + 256 * s, DT, C0) for s in range(2)]
        c_hg = area(29600, 2, 512)
        c_h = area(30624, 2, 512)
        c_hT = [area(31648 + 1024 * s, I0 // P, C0) for s in range(2)]
        c_eo = [area(33696 + 256 * s, D) for s in range(2)]
        c_m, c_r = small[:, 0:G], small[:, 8:16]
        we_loaded = [sem(f"we_loaded{s}") for s in range(3)]
        z_stored, acc_stored = sem("z_stored"), sem("acc_stored")
        c_logit, c_sub, c_exp, c_prob, c_scT, c_sc_out = (
            sem("c_logit"), sem("c_sub"), sem("c_exp"), sem("c_prob"), sem("c_scT"), sem("c_sc_out"))
        c_sgu, c_sgel, c_sh, c_sy, c_sx = sem("c_sgu"), sem("c_sgel"), sem("c_sh"), sem("c_sy"), sem("c_sx")
        c_top, c_topT, c_pick = sem("c_top"), sem("c_topT"), sem("c_pick")
        GOT_FIRST = (0, 1, 4, 8, E0)
        c_got = [sem(f"c_got{s}") for s in range(4)]
        S_BANK = (6, 7, 0, 1, 2, 3, 5, 6)

        def got_by(e):
            return max(s for s in range(4) if GOT_FIRST[s] <= e)

        c_xt, c_xt_out, c_gu, c_gel, c_hm = sem("c_xt"), sem("c_xt_out"), sem("c_gu"), sem("c_gel"), sem("c_hm")
        c_ht, c_hT_act, c_hT_dve, c_down, c_eo_out, c_added = (
            sem("c_ht"), sem("c_hT_act"), sem("c_hT_dve"), sem("c_down"), sem("c_eo_out"), sem("c_added"))

        N_TOP = 3 * (C0 // 8) + 2

        def sp_stage_c(sp):
            sp_weights(sp, 2)
            sp.wait_ge(ln_z, 3 * G)
            sp.dma_start(z_dram.rearrange("(g p) d -> p g d", p=P), z[:, :, :]).then_inc(z_stored, 16)
            for e in range(E0):
                s = e % 3
                if e == 0:
                    sp.wait_ge(x_done, 2)
                if e == 2:
                    sp_weights(sp, 3)
                if e == 3:
                    sp.wait_ge(c_sx, G)
                    sp.dma_start(acc_dram.rearrange("(g p) d -> p g d", p=P), x[:, :, :]).then_inc(acc_stored, 16)
                if e >= 3:
                    sp.wait_ge(c_down, e - 2)
                for j, name in enumerate(("we_g", "we_u", "we_d")):
                    sp.dma_start(we[s][j].rearrange("p k n -> p (k n)"), a[name][e]).then_inc(we_loaded[s], 16)
            sp.wait_ge(c_added, 16 * E0)
            for half in range(2):
                gs = slice(4 * half, 4 * half + 4)
                sp.dma_start(x[:, gs, :], acc_dram.rearrange("(g p) d -> p g d", p=P)[:, gs, :]).then_inc(loaded_x[half], 16)

        def pe_stage_c(pe):
            wait_weights(pe, 2)
            pe_turn_z(pe, 2, 1)
            pe_wait_zT(pe, 2, 0)
            pe_wait_zT(pe, 2, 1)
            for g in range(G):
                for k in range(DT):
                    i = pe.matmul(bank[4][:, g * E0:g * E0 + E0], zT[:, k, g * P:g * P + P], c_gate[:, k, :],
                                  start=(k == 0), stop=(k == DT - 1))
            i.then_inc(c_logit, 1)

            def shared(c):
                m, n = c // 2, c % 2
                if c >= 2:
                    pe.wait_ge(c_sgel, c - 1)
                for w, o in ((c_sg, bank[c % 2]), (c_su, bank[2 + c % 2])):
                    for k in range(DT):
                        i = pe.matmul(o[:, :], w[:, k, m * P:m * P + P], zT[:, k, n * 512:n * 512 + 512],
                                      start=(k == 0), stop=(k == DT - 1))
                i.then_inc(c_sgu, 1)

            pe.wait_ge(c_prob, 1)
            for g in range(G):
                i = pe.transpose(bank[5 + g // 4][0:E0, (g % 4) * P:(g % 4) * P + P], c_p[:, g, :], ident)
            i.then_inc(c_scT, 1)
            for c in range(8):
                shared(c)
            pe.wait_ge(c_sh, 8)
            for g in range(G):
                if g == 0:
                    pe.wait_ge(c_sc_out, 2)
                if g == 7:
                    pe.wait_ge(c_top, N_TOP)
                    pe.transpose(bank[4][:, 128:128 + E0], c_val[0:E0, :], ident[0:E0, 0:E0])
                    pe.transpose(bank[4][:, 144:144 + E0], c_idxf[0:E0, :], ident[0:E0, 0:E0]).then_inc(c_topT, 1)
                    pe.wait_ge(c_sx, 1)
                for m in range(IS // P):
                    i = pe.matmul(bank[S_BANK[g]][:, 0:D], c_sT[:, m, g * P:g * P + P], c_sd[:, m, :],
                                  start=(m == 0), stop=(m == IS // P - 1))
                i.then_inc(c_sy, 1)

            def turn_x(e):
                if e == GOT_FIRST[got_by(e)]:
                    pe.wait_ge(c_got[got_by(e)], 16 * (GOT_FIRST[got_by(e) + 1] - e))
                if e >= 1:
                    pe.wait_ge(c_xt_out, e)
                for k in range(DT):
                    i = pe.transpose(bank[0][:, k * P:k * P + P], c_xg[:, e, k * P:k * P + P], ident)
                i.then_inc(c_xt, 1)

            def gate_up(e, c):
                if c == 0:
                    pe.wait_ge(c_xt_out, e + 1)
                    pe.wait_ge(we_loaded[e % 3], 48 * (e // 3 + 1))
                if e >= 1:
                    pe.wait_ge(c_hm, 2 * e - 1 + c)
                elif c == 0:
                    pe.wait_ge(c_pick, 2)
                for j in range(2):
                    for k in range(DT):
                        i = pe.matmul(bank[1 + 2 * j + c][:, :], c_xgT[e % 2][:, k, :],
                                      we[e % 3][j][:, k, c * 512:c * 512 + 512], start=(k == 0), stop=(k == DT - 1))
                i.then_inc(c_gu, 1)

            def turn_h(e, c):
                pe.wait_ge(c_hm, 2 * e + c + 1)
                if e >= 1:
                    pe.wait_ge((c_hT_act, c_hT_dve)[c], e)
                for m in range(4):
                    i = pe.transpose(bank[5 + c][:, m * P:m * P + P], c_h[:, c, m * P:m * P + P], ident)
                i.then_inc(c_ht, 1)

            def down(e):
                pe.wait_ge(c_hT_act, e + 1)
                pe.wait_ge(c_hT_dve, e + 1)
                if e >= 1:
                    pe.wait_ge(c_eo_out, e)
                for m in range(I0 // P):
                    i = pe.matmul(bank[7][:, 0:D], c_hT[e % 2][:, m, :], we[e % 3][2][:, m, :],
                                  start=(m == 0), stop=(m == I0 // P - 1))
                i.then_inc(c_down, 1)

            pe.wait_ge(c_sx, G)
            turn_x(0)
            for e in range(E0 + 1):
                if e < E0:
                    gate_up(e, 0)
                if e >= 1:
                    turn_h(e - 1, 1)
                if e < E0:
                    gate_up(e, 1)
                if e + 1 < E0:
                    turn_x(e + 1)
                if e >= 1:
                    down(e - 1)
                if e < E0:
                    turn_h(e, 0)

        def act_stage_c(act):
            act.wait_ge(c_sub, 1)
            act.activation(c_p, c_p, ACT.Exp).then_inc(c_exp, 1)
            for c in range(8):
                act.wait_ge(c_sgu, c + 1)
                if c >= 2:
                    act.wait_ge(c_sh, c - 1)
                act.activation(c_tmp[c % 2], bank[c % 2][:, :], ACT.Gelu)
                act.activation(c_up[c % 2], bank[2 + c % 2][:, :], ACT.Copy).then_inc(c_sgel, 1)

            def x_out(e):
                act.wait_ge(c_xt, e + 1)
                if e >= 2:
                    act.wait_ge(c_gu, 2 * (e - 1))
                act.activation(c_xgT[e % 2].rearrange("p k t -> p (k t)"), bank[0][:, 0:D], ACT.Copy).then_inc(c_xt_out, 1)

            x_out(0)
            for e in range(E0):
                for c in range(2):
                    act.wait_ge(c_gu, 2 * e + c + 1)
                    act.activation(c_hg[:, c, :], bank[1 + c][:, :], ACT.Gelu).then_inc(c_gel, 1)
                if e + 1 < E0:
                    x_out(e + 1)
                act.wait_ge(c_ht, 2 * e + 1)
                if e >= 2:
                    act.wait_ge(c_down, e - 1)
                act.activation(c_hT[e % 2][:, 0:4, :].rearrange("p m t -> p (m t)"), bank[5][:, :],
                               ACT.Copy).then_inc(c_hT_act, 1)

        def dve_stage_c(dve):
            def picks():
                dve.wait_ge(c_topT, 1)
                dve.tensor_copy(c_idxT, bank[4][:, 144:144 + E0]).then_inc(c_pick, 1)
                dve.tensor_copy(c_valT, bank[4][:, 128:128 + E0]).then_inc(c_pick, 1)

            link(dve, dve.memset(c_sc[0:32, :], 0.0))
            dve.wait_ge(c_logit, 1)
            logits = bank[4][:, 0:P].rearrange("p (g e) -> p g e", g=G)
            m_b, r_b = (t[:, :, None].broadcast_to([P, G, E0]) for t in (c_m, c_r))
            link(dve, dve.tensor_reduce(c_m, logits, AX_X, ALU.max))
            dve.tensor_tensor(c_p, logits, m_b, ALU.subtract).then_inc(c_sub, 1)
            dve.wait_ge(c_exp, 1)
            link(dve, dve.tensor_reduce(c_r, c_p, AX_X, ALU.add))
            link(dve, dve.reciprocal(c_r, c_r))
            dve.tensor_tensor(c_p, c_p, r_b, ALU.mult).then_inc(c_prob, 1)

            dve.wait_ge(c_scT, 1)
            for j in range(2):
                dve.tensor_copy(c_sc[32 * j:32 * j + E0, :], bank[5 + j][0:E0, :]).then_inc(c_sc_out, 1)
            dve.wait_ge(c_sc_out, 2)
            for r in range(C0 // 8):
                v, ix = c_val[:, 8 * r:8 * r + 8], c_idx[:, 8 * r:8 * r + 8]
                dve.max(v, c_sc).then_inc(c_top, 1)
                dve.wait_ge(c_top, 3 * r + 1)
                dve.max_index(ix, v, c_sc).then_inc(c_top, 1)
                dve.wait_ge(c_top, 3 * r + 2)
                dve.match_replace(c_sc, v, c_sc, -1.0).then_inc(c_top, 1)
                dve.wait_ge(c_top, 3 * r + 3)
            up = slice(C0 - 1, None, -1)
            dve.tensor_copy(c_val2, c_val[32:32 + E0, up])
            link(dve, dve.tensor_copy(c_idxf, c_idx))
            dve.tensor_scalar(c_idx2, c_idxf[32:32 + E0, up], float(T // 2), None, ALU.add)
            link(dve, dve.tensor_tensor(c_first, c_val[0:E0, :], c_val2, ALU.is_ge))
            link(dve, dve.tensor_tensor(c_idxf[0:E0, :], c_idxf[0:E0, :], c_idx2, ALU.subtract))
            link(dve, dve.tensor_tensor(c_idxf[0:E0, :], c_idxf[0:E0, :], c_first, ALU.mult))
            dve.tensor_tensor(c_idxf[0:E0, :], c_idxf[0:E0, :], c_idx2, ALU.add).then_inc(c_top, 1)
            dve.tensor_tensor(c_val[0:E0, :], c_val[0:E0, :], c_val2, ALU.max).then_inc(c_top, 1)
            for g in range(G):
                if g == 1:
                    picks()
                dve.wait_ge(c_sy, g + 1)
                dve.tensor_tensor(x[:, g, :], bank[S_BANK[g]][:, 0:D], x[:, g, :], ALU.add).then_inc(c_sx, 1)
            dve.wait_ge(c_pick, 2)

            def hidden(e, c):
                dve.wait_ge(c_gel, 2 * e + c + 1)
                if e >= 1:
                    dve.wait_ge(c_ht, 2 * e - 1 + c)
                dve.tensor_tensor(c_h[:, c, :], bank[3 + c][:, :], c_hg[:, c, :], ALU.mult).then_inc(c_hm, 1)

            def h_out(e):
                dve.wait_ge(c_ht, 2 * e + 2)
                if e >= 2:
                    dve.wait_ge(c_down, e - 1)
                dve.tensor_copy(c_hT[e % 2][:, 4:8, :].rearrange("p m t -> p (m t)"), bank[6][:, :]).then_inc(c_hT_dve, 1)

            def weigh(e):
                dve.wait_ge(c_down, e + 1)
                if e >= 2:
                    dve.wait_ge(c_added, 16 * (e - 1))
                dve.tensor_scalar(c_eo[e % 2], bank[7][:, 0:D], c_valT[:, e:e + 1], None, ALU.mult).then_inc(c_eo_out, 1)

            for e in range(E0 + 1):
                if e < E0:
                    hidden(e, 0)
                if e >= 1:
                    h_out(e - 1)
                if e < E0:
                    hidden(e, 1)
                if e >= 1:
                    weigh(e - 1)
            dve.wait_ge(loaded_x[0], 32)
            dve.memset(tick[:, :], 0.0).then_inc(x_done, 1)
            dve_layernorm_loaded(dve, 3, 32)

        def pool_stage_c(pool):
            def gather(e):
                pool.indirect_dma_start(c_xg[:, e, :], None, z_dram[:, :], bass.IndirectOffsetOnAxis(
                    ap=c_idxT[:, e:e + 1], axis=0)).then_inc(c_got[got_by(e)], 16)

            for c in range(8):
                m, n = c // 2, c % 2
                pool.wait_ge(c_sgel, c + 1)
                if c >= 1:
                    pool.wait_ge(c_sh, c)
                pool.tensor_tensor(c_sT[:, m, n * 512:n * 512 + 512], c_up[c % 2], c_tmp[c % 2], ALU.mult).then_inc(c_sh, 1)
            pool.wait_ge(c_pick, 1)
            pool.wait_ge(z_stored, 16)
            for e in range(E0):
                gather(e)
            pool.wait_ge(acc_stored, 16)
            for e in range(E0):
                pool.wait_ge(c_eo_out, e + 1)
                if e >= 1:
                    pool.wait_ge(c_added, 16 * e)
                pool.indirect_dma_start(acc_dram[:, :], bass.IndirectOffsetOnAxis(ap=c_idxT[:, e:e + 1], axis=0),
                                        c_eo[e % 2], None, compute_op=ALU.add).then_inc(c_added, 16)

        w_d = [w_odd[:, j * 1024:(j + 1) * 1024].rearrange("p (k n) -> p k n", k=k)
               for j, k in enumerate((DT, XI // P, DT, XI // P))]
        d_qk = area(10256, DT, B // 2, XH * L)
        d_aT = d_qk
        d_q = area(18448, XI // P, T)
        d_oT = area(22544, XI // P, HALF)
        d_p = [[area(24592 + 260 * (2 * s + j), NK) for j in range(2)] for s in range(2)]
        d_n = [split(f"d_n{s}", 25632 + 1024 * s, 2, D) for s in range(3)]
        d_pT = [split(f"d_pT{s}", 28704 + 1024 * s, 2, XH * L) for s in range(2)]
        EDGE = EDGE_ROWS[-1] + 1
        d_nl = [rounded(f"d_nl{s}", 30752 + 256 * s, D)[0:EDGE, :] for s in range(3)]
        d_pl = [rounded(f"d_pl{s}", 31520 + 256 * s, XH * L)[0:EDGE, :] for s in range(2)]
        d_mx, d_nb, d_sum, d_inv = (small[:, 64 * j:64 * j + 64] for j in range(4))
        (d_qd, d_q_out, d_qkd, d_qk_act, d_qk_dve, d_s, d_nbias, d_exp, d_norm, d_turn, d_turned, d_av, d_a_out,
         d_o, d_o_out, d_y, d_x, d_clear, d_nhi, d_nlo, d_phi) = (sem("d_" + n) for n in (
             "q", "q_out", "qk", "qk_act", "qk_dve", "s", "nbias", "exp", "norm", "turn", "turned", "av", "a_out",
             "o", "o_out", "y", "x", "clear", "rows_hi", "rows_lo", "p_hi"))

        def sp_stage_d(sp):
            sp.wait_ge(x_done, 3)
            sp.wait_ge(d_clear, 1)
            sp_context(sp, 3, (d_s, 2 * BG), (d_nlo, 2 * BG))
            sp_weights(sp, 4)
            sp_weights(sp, 5)

        def pe_stage_d(pe):
            wait_weights(pe, 3)
            for c in range(8):
                m, n = c % 4, c // 4
                if c == 4:
                    pe_turn_z(pe, 3, 1)
                if m == 0:
                    pe_wait_zT(pe, 3, n)
                if c >= 4:
                    pe.wait_ge(d_q_out, c - 3)
                for k in range(DT):
                    i = pe.matmul(bank[4 + c % 4][:, :], w_d[0][:, k, m * P:m * P + P],
                                  zT[:, k, n * 512:n * 512 + 512], start=(k == 0), stop=(k == DT - 1))
                i.then_inc(d_qd, 1)
            pe.wait_ge(d_q_out, 8)
            for half in range(2):
                b0 = half * (B // 2)
                for c in range(16):
                    h, dt = c // 2, c % 2
                    r = (h % 2) * 64
                    if c >= 4:
                        pe.wait_ge((d_qk_act, d_qk_dve)[c % 2], 8 * half + (c - 4) // 2 + 1)
                    elif half:
                        pe.wait_ge(d_x, 4)
                    pe.matmul(bank[c % 4][:, :], w_d[1][r:r + 64, h // 2, dt * P:dt * P + P],
                              d_q[r:r + 64, h // 2, half * 512:half * 512 + 512], start=True, stop=True).then_inc(d_qkd, 1)
                pe.wait_ge(d_qk_act, 8 * (half + 1))
                pe.wait_ge(d_qk_dve, 8 * (half + 1))

                def scores(bb):
                    b = b0 + bb
                    s = (b // BG) % 2
                    if b % BG == 0:
                        pe.wait_ge(keys_loaded[s], KEYS_A + 16 * (b // BG // 2 + 1))
                    for j in range(2):
                        if b >= 1:
                            pe.wait_ge(d_exp, 2 * b - 1 + j)
                        for k in range(DT):
                            i = pe.matmul(bank[j][:, 0:NK], d_qk[:, k, bb, j * P:j * P + P], ringT[s][:, k, b % BG, :],
                                          start=(k == 0), stop=(k == DT - 1))
                        i.then_inc(d_s, 1)

                def turn(bb):
                    b = b0 + bb
                    pe.wait_ge(d_norm, 2 * b + 2)
                    if b >= 1:
                        pe.wait_ge(d_turned, 2 * b)
                    for j in range(2):
                        p = d_p[b % 2][j]
                        for k in range(2):
                            pe.transpose(bank[2 + b % 2][:, k * 256 + j * P:k * 256 + j * P + P],
                                         p[:, k * P:k * P + P], ident)
                        i = pe.transpose(bank[6][0:EDGE, j * P:j * P + P], p[:, NK - 1:NK].broadcast_to([P, EDGE]), ident)
                    i.then_inc(d_turn, 1)

                def values(bb):
                    b = b0 + bb
                    pe.wait_ge(d_turned, 2 * b + 1)
                    pe.wait_ge(d_nlo, 2 * b + 2)
                    if b >= 2:
                        pe.wait_ge(d_a_out, b - 1)
                    for dt in range(DT):
                        o = bank[4 + b % 2][:, dt * 256:dt * 256 + 256]
                        for k in range(2):
                            matmul3(pe, o, d_n[b % 3], d_pT[b % 2], (slice(None), k, slice(dt * P, dt * P + P)),
                                    (slice(None), k), k == 0, False)
                        if dt == 0:
                            pe.wait_ge(d_turned, 2 * b + 2)
                        i = pe.matmul(o, d_nl[b % 3][:, dt * P:dt * P + P], d_pl[b % 2], start=False, stop=True)
                    i.then_inc(d_av, 1)

                for t in range(B // 2 + 2):
                    if t < B // 2:
                        scores(t)
                    if t >= 2:
                        values(t - 2)
                    if 1 <= t <= B // 2:
                        turn(t - 1)
                pe.wait_ge(d_a_out, (half + 1) * (B // 2))
                if half:
                    pe_turn_z(pe, 4, 0)
                for m in range(XI // P):
                    if m >= 2:
                        pe.wait_ge(d_o_out, 4 * half + m - 1)
                    for h in (2 * m, 2 * m + 1):
                        r = (h % 2) * 64
                        for k in range(DT):
                            i = pe.matmul(bank[6 + m % 2][r:r + 64, :], w_d[2][:, k, h * XD:h * XD + XD],
                                          d_aT[:, k, :, h * L:h * L + L], start=(k == 0), stop=(k == DT - 1))
                    i.then_inc(d_o, 1)
                pe.wait_ge(d_o_out, 4 * (half + 1))
                for g in range(4 * half, 4 * half + 4):
                    if g % 4 >= 2:
                        pe.wait_ge(d_x, g - 1)
                    for m in range(XI // P):
                        pe.matmul(bank[2 + g % 2][:, 0:D], d_oT[:, m, g % 4 * P:g % 4 * P + P], w_d[3][:, m, :],
                                  start=(m == 0), stop=False)
                    pe.matmul(bank[2 + g % 2][:, 0:D], ones[:, :], brow[:, R_BO:R_BO + D],
                              start=False, stop=True).then_inc(d_y, 1)

        def act_stage_d(act):
            for c in range(8):
                m, n = c % 4, c // 4
                act.wait_ge(d_qd, c + 1)
                act.activation(d_q[:, m, n * 512:n * 512 + 512], bank[4 + c % 4][:, :], ACT.Copy).then_inc(d_q_out, 1)
            for half in range(2):
                for c in range(0, 16, 2):
                    act.wait_ge(d_qkd, 16 * half + c + 1)
                    act.activation(d_qk[:, 0, :, (c // 2) * L:(c // 2) * L + L],
                                   bank[c % 4][:, :].rearrange("p (b i) -> p b i", i=L), ACT.Copy).then_inc(d_qk_act, 1)

                def exps(bb):
                    b = half * (B // 2) + bb
                    for j in range(2):
                        t = 2 * b + j
                        act.wait_ge(d_nbias, b + 1)
                        if b >= 2:
                            act.wait_ge(d_turn, b - 1)
                        act.activation(d_p[b % 2][j], bank[j][:, 0:NK], ACT.Exp, bias=d_nb[:, t:t + 1],
                                       scale=XD ** -0.5, accum_out=d_sum[:, t:t + 1]).then_inc(d_exp, 1)

                def turned(bb):
                    b = half * (B // 2) + bb
                    act.wait_ge(d_turn, b + 1)
                    if b >= 2:
                        act.wait_ge(d_av, b - 1)
                    act.activation(d_pT[b % 2][0].rearrange("p k r -> p (k r)"), bank[2 + b % 2][:, :],
                                   ACT.Copy).then_inc(d_phi, 1)
                    act.activation(d_pl[b % 2], bank[6][0:EDGE, 0:256], ACT.Copy).then_inc(d_phi, 1)

                def rows(bb):
                    b = half * (B // 2) + bb
                    s = (b // BG) % 2
                    if b % BG == 0:
                        act.wait_ge(rows_loaded[s], ROWS_A + 64 * (b // BG // 2 + 1))
                    if b >= 3:
                        act.wait_ge(d_av, b - 2)
                    act.activation(d_n[b % 3][0], ringN[s][:, b % BG], ACT.Copy).then_inc(d_nhi, 1)
                    act.activation(d_nl[b % 3], ringL[s][0:EDGE, b % BG * D:b % BG * D + D], ACT.Copy).then_inc(d_nhi, 1)

                if half:
                    act_std(act, 4, 0)
                for t in range(B // 2 + 1):
                    if t < B // 2:
                        exps(t)
                    if t >= 1:
                        turned(t - 1)
                    if t < B // 2:
                        rows(t)
                if half:
                    act_zT(act, 4, 0)
                for m in range(XI // P):
                    act.wait_ge(d_o, 4 * half + m + 1)
                    act.activation(d_oT[:, m, :], bank[6 + m % 2][:, :], ACT.Copy).then_inc(d_o_out, 1)
            act_std(act, 4, 1)
            act_zT(act, 4, 1)

        def dve_stage_d(dve):
            for half in range(2):
                for c in range(1, 16, 2):
                    dve.wait_ge(d_qkd, 16 * half + c + 1)
                    dve.tensor_copy(d_qk[:, 1, :, (c // 2) * L:(c // 2) * L + L],
                                    bank[c % 4][:, :].rearrange("p (b i) -> p b i", i=L)).then_inc(d_qk_dve, 1)

                def maxima(bb):
                    t = 2 * (half * (B // 2) + bb)
                    for j in range(2):
                        dve.wait_ge(d_s, t + j + 1)
                        i = dve.tensor_reduce(d_mx[:, t + j:t + j + 1], bank[j][:, 0:NK], AX_X, ALU.max)
                    link(dve, i)
                    dve.tensor_scalar(d_nb[:, t:t + 2], d_mx[:, t:t + 2], -XD ** -0.5, None,
                                      ALU.mult).then_inc(d_nbias, 1)

                def normalize(bb):
                    b = half * (B // 2) + bb
                    dve.wait_ge(d_exp, 2 * b + 2)
                    link(dve, dve.reciprocal(d_inv[:, 2 * b:2 * b + 2], d_sum[:, 2 * b:2 * b + 2]))
                    for j in range(2):
                        p = d_p[b % 2][j]
                        dve.tensor_scalar(p, p, d_inv[:, 2 * b + j:2 * b + j + 1], None, ALU.mult).then_inc(d_norm, 1)

                def lows(bb):
                    b = half * (B // 2) + bb
                    dve.wait_ge(d_phi, 2 * b + 1)
                    hi, lo = d_pT[b % 2]
                    dve.tensor_tensor(lo.rearrange("p k r -> p (k r)"), bank[2 + b % 2][:, :],
                                      hi.bitcast(F32).rearrange("p k r -> p (k r)"), ALU.subtract).then_inc(d_turned, 1)
                    r = EDGE_ROWS[2]
                    pl = d_pl[b % 2][r:r + 1, :]
                    dve.wait_ge(d_phi, 2 * b + 2)
                    dve.tensor_tensor(pl, bank[6][r:r + 1, 0:256], pl.bitcast(F32), ALU.subtract).then_inc(d_turned, 1)

                def values_out(bb):
                    b = half * (B // 2) + bb
                    dve.wait_ge(d_av, b + 1)
                    dve.tensor_copy(d_aT[:, :, bb, :], bank[4 + b % 2][:, :].rearrange("p (k r) -> p k r", k=DT)).then_inc(d_a_out, 1)

                for t in range(B // 2 + 2):
                    if t < B // 2:
                        maxima(t)
                    if 1 <= t <= B // 2:
                        normalize(t - 1)
                    if t >= 2:
                        values_out(t - 2)
                    if 1 <= t <= B // 2:
                        lows(t - 1)
                    if half and t == 2:
                        dve_scale(dve, 4, 0)
                if half:
                    dve_zT(dve, 4, 0)
                for g in range(4 * half, 4 * half + 4):
                    dve.wait_ge(d_y, g + 1)
                    dve.tensor_tensor(x[:, g, :], bank[2 + g % 2][:, 0:D], x[:, g, :], ALU.add).then_inc(d_x, 1)
                    dve.wait_ge(d_x, g + 1)
                    i = dve_stats(dve, g)
                link(dve, i)
                if half == 0:
                    dve_variances(dve, 0)
            dve.memset(tick[:, :], 0.0).then_inc(x_done, 1)
            dve_variances(dve, 1)
            dve_scale(dve, 4, 1)
            dve_zT(dve, 4, 1)

        def pool_stage_d(pool):
            pool.wait_ge(x_done, 3)
            pool.memset(arena[0:EDGE, 8208:10256], 0.0).then_inc(d_clear, 1)
            for b in range(B):
                s = (b // BG) % 2
                pool.wait_ge(d_nhi, 2 * b + 2)
                if b >= 1:
                    pool.wait_ge(d_nlo, 2 * b)
                if b % BG == 0:
                    pool.wait_ge(rows_loaded[s], ROWS_A + 64 * (b // BG // 2 + 1))
                hi, lo = d_n[b % 3]
                pool.tensor_tensor(lo, ringN[s][:, b % BG], hi.bitcast(F32), ALU.subtract).then_inc(d_nlo, 1)
                pool.wait_ge(d_nlo, 2 * b + 1)
                r = EDGE_ROWS[1]
                nl = d_nl[b % 3][r:r + 1, :]
                pool.tensor_tensor(nl, ringL[s][r:r + 1, b % BG * D:b % BG * D + D], nl.bitcast(F32),
                                   ALU.subtract).then_inc(d_nlo, 1)

        f_z = split("f_z", 0, DT, T)
        f_w1 = split("f_w1", 4096, DT, I1)
        f_w2 = split("f_w2", 8192, I1 // P, D)
        f_hT = [split(f"f_hT{s}", 12288 + 8192 * s, I1 // P, 512) for s in range(2)]
        f_raw1, f_raw2 = area(28672, DT, I1), area(30720, I1 // P, D)
        f_tmp = [area(32768 + 512 * s, 512) for s in range(2)]
        f_r1 = w_odd[:, 0:1024].rearrange("p (k n) -> p k n", k=DT)
        f_r2 = w_odd[:, 1024:1024 + RH // P * E1].rearrange("p (k n) -> p k n", k=RH // P)
        f_rh = area(24576, RH // P, T)
        f_p, f_rank = area(33792, G, E1), area(33824, G, E1)
        f_cw = area(33856, G, E1)
        f_gt, f_eq = area(33888, G, E1, E1), area(34016, G, E1, E1)
        f_m, f_r = small[:, 0:G], small[:, 8:16]
        f_loaded = [sem("f_loaded_w1"), sem("f_loaded_w2")]
        f_split = [sem("f_split_w1"), sem("f_split_w2")]
        (f_rhd, f_rh_out, f_logit, f_sub, f_exp, f_h, f_gel, f_y, f_x, f_z_hi, f_z_lo, f_hi, f_lo) = (
            sem("f_" + n) for n in ("rh", "rh_out", "logit", "sub", "exp", "h", "gel", "y", "x",
                                    "z_hi", "z_lo", "hi", "lo"))
        NF = 2 * E1

        def sp_stage_f(sp):
            for e in range(E1):
                for j, (raw, name) in enumerate(((f_raw1, "f_w1"), (f_raw2, "f_w2"))):
                    if e == 0 and j == 0:
                        sp.wait_ge(x_done, 5)
                    if e >= 1:
                        sp.wait_ge(f_split[j], 2 * e)
                    sp.dma_start(raw.rearrange("p k n -> p (k n)"), a[name][e]).then_inc(f_loaded[j], 16)

        def pool_stage_f(pool):
            for e in range(E1):
                for j, (raw, (hi, lo)) in enumerate(((f_raw1, f_w1), (f_raw2, f_w2))):
                    pool.wait_ge(f_loaded[j], 16 * (e + 1))
                    if e >= 1:
                        pool.wait_ge(*((f_h, 16 * e), (f_y, 8 * e))[j])
                    pool.tensor_copy(hi, raw).then_inc(f_split[j], 1)
                    pool.wait_ge(f_split[j], 2 * e + 1)
                    pool.tensor_tensor(lo, raw, hi.bitcast(F32), ALU.subtract).then_inc(f_split[j], 1)

        def pe_stage_f(pe):
            wait_weights(pe, 5)
            for c in range(8):
                m, n = c % 4, c // 4
                if c == 4:
                    pe_turn_z(pe, 5, 1)
                if m == 0:
                    pe_wait_zT(pe, 5, n)
                if c >= 4:
                    pe.wait_ge(f_rh_out, c - 3)
                for k in range(DT):
                    i = pe.matmul(bank[c % 4][:, :], f_r1[:, k, m * P:m * P + P],
                                  zT[:, k, n * 512:n * 512 + 512], start=(k == 0), stop=(k == DT - 1))
                i.then_inc(f_rhd, 1)

            def first(i):
                e, n = i // 2, i % 2
                if n == 0:
                    pe.wait_ge(f_split[0], 2 * (e + 1))
                for m in range(I1 // P):
                    c = 8 * i + m
                    if c >= 4:
                        pe.wait_ge(f_gel, c - 3)
                    else:
                        pe.wait_ge(f_rh_out, 5 + c)
                    if c == 0:
                        pe.wait_ge(f_z_hi, 2)
                        pe.wait_ge(f_z_lo, 2)
                    for k in range(DT):
                        j = matmul3(pe, bank[c % 4][:, :], f_w1, f_z, (slice(None), k, slice(m * P, m * P + P)),
                                    (slice(None), k, slice(n * 512, n * 512 + 512)), k == 0, k == DT - 1)
                    j.then_inc(f_h, 1)

            def logits():
                pe.wait_ge(f_rh_out, 8)
                for g in range(G):
                    o = bank[4][:, g * E1:g * E1 + E1]
                    for m in range(RH // P):
                        pe.matmul(o, f_rh[:, m, g * P:g * P + P], f_r2[:, m, :], start=(m == 0), stop=False)
                    j = pe.matmul(o, ones[:, :], brow[:, R_RB2:R_RB2 + E1], start=False, stop=True)
                j.then_inc(f_logit, 1)

            def second(i):
                e, n = i // 2, i % 2
                pe.wait_ge(f_lo, 8 * (i + 1))
                if n == 0:
                    pe.wait_ge(f_split[1], 2 * (e + 1))
                if i == 0:
                    pe.wait_ge(f_sub, 1)
                for g in range(4):
                    if i >= 1:
                        pe.wait_ge(f_x, 4 * (i - 1) + g + 1)
                    o = bank[4 + g][:, 0:D]
                    for m in range(I1 // P):
                        matmul3(pe, o, f_hT[i % 2], f_w2, (slice(None), m, slice(g * P, g * P + P)),
                                (slice(None), m), m == 0, False)
                    pe.matmul(o, ones[:, :], brow[:, R_BE2 + e * D:R_BE2 + (e + 1) * D],
                              start=False, stop=True).then_inc(f_y, 1)

            logits()
            for e in range(E1):
                first(2 * e)
                first(2 * e + 1)
                second(2 * e)
                second(2 * e + 1)

        def act_stage_f(act):
            act.wait_ge(ln_zT_act, 12)
            act.wait_ge(ln_zT_dve, 12)
            for n in range(2):
                act.activation(f_z[0][:, :, n * 512:n * 512 + 512], zT[:, :, n * 512:n * 512 + 512],
                               ACT.Copy).then_inc(f_z_hi, 1)
            for c in range(8):
                m, n = c % 4, c // 4
                act.wait_ge(f_rhd, c + 1)
                act.activation(f_rh[:, m, n * 512:n * 512 + 512], bank[c % 4][:, :], ACT.Gelu,
                               bias=bcol[:, K_RB1 + m:K_RB1 + m + 1]).then_inc(f_rh_out, 1)
            act.wait_ge(f_sub, 1)
            act.activation(f_p, f_p, ACT.Exp).then_inc(f_exp, 1)
            for c in range(8 * NF):
                e, m = c // 16, c % 8
                act.wait_ge(f_h, c + 1)
                if c >= 2:
                    act.wait_ge(f_lo, c - 1)
                act.activation(f_tmp[c % 2], bank[c % 4][:, :], ACT.Gelu,
                               bias=bcol[:, K_BE1 + e * 8 + m:K_BE1 + e * 8 + m + 1]).then_inc(f_gel, 1)

        def dve_stage_f(dve):
            for n in range(2):
                dve.wait_ge(f_z_hi, n + 1)
                c = slice(n * 512, n * 512 + 512)
                dve.tensor_tensor(f_z[1][:, :, c], zT[:, :, c], f_z[0][:, :, c].bitcast(F32),
                                  ALU.subtract).then_inc(f_z_lo, 1)
            dve.wait_ge(f_logit, 1)
            lg = bank[4][:, 0:G * E1].rearrange("p (g e) -> p g e", g=G)
            m_b, r_b = (t[:, :, None].broadcast_to([P, G, E1]) for t in (f_m, f_r))
            link(dve, dve.tensor_reduce(f_m, lg, AX_X, ALU.max))
            dve.tensor_tensor(f_p, lg, m_b, ALU.subtract).then_inc(f_sub, 1)
            dve.wait_ge(f_exp, 1)
            link(dve, dve.tensor_reduce(f_r, f_p, AX_X, ALU.add))
            link(dve, dve.reciprocal(f_r, f_r))
            link(dve, dve.tensor_tensor(f_p, f_p, r_b, ALU.mult))
            other = f_p[:, :, None, :].broadcast_to([P, G, E1, E1])
            own = f_p[:, :, :, None].broadcast_to([P, G, E1, E1])
            tri = const[:, None, C_TRI:C_TRI + E1 * E1].broadcast_to([P, G, E1 * E1])
            dve.tensor_tensor(f_gt, other, own, ALU.is_gt)
            link(dve, dve.tensor_tensor(f_eq, other, own, ALU.is_equal))
            eq, gt = (t.rearrange("p g e f -> p g (e f)") for t in (f_eq, f_gt))
            link(dve, dve.tensor_tensor(eq, eq, tri, ALU.mult))
            link(dve, dve.tensor_tensor(gt, gt, eq, ALU.add))
            link(dve, dve.tensor_reduce(f_rank, f_gt, AX_X, ALU.add))
            link(dve, dve.scalar_tensor_tensor(out=f_cw, in0=f_rank, scalar=2.0, in1=f_p, op0=ALU.is_lt,
                                     op1=ALU.mult))

            def parts(i):
                for m in range(I1 // P):
                    c = 8 * i + m
                    dve.wait_ge(f_gel, c + 1)
                    if m == 0 and i >= 2:
                        dve.wait_ge(f_y, 4 * (i - 1))
                    hi, lo = (t[:, m, :] for t in f_hT[i % 2])
                    dve.tensor_copy(hi, f_tmp[c % 2]).then_inc(f_hi, 1)
                    dve.wait_ge(f_hi, c + 1)
                    dve.tensor_tensor(lo, f_tmp[c % 2], hi.bitcast(F32), ALU.subtract).then_inc(f_lo, 1)

            def residual(i):
                e, n = i // 2, i % 2
                for g in range(4):
                    dve.wait_ge(f_y, 4 * i + g + 1)
                    if e:
                        dve.wait_ge(f_x, 4 * (i - 2) + g + 1)
                    xs = x[:, 4 * n + g, :]
                    dve.scalar_tensor_tensor(out=xs, in0=bank[4 + g][:, 0:D], scalar=f_cw[:, 4 * n + g, e:e + 1],
                                             in1=xs, op0=ALU.mult, op1=ALU.add).then_inc(f_x, 1)

            for e in range(E1):
                parts(2 * e)
                parts(2 * e + 1)
                residual(2 * e)
                residual(2 * e + 1)

        block = ctx.enter_context(nc.Block())
        last = 5 if stop is None else stop

        @block.sync
        def _(sp):
            for half in range(2):
                gs = slice(4 * half, 4 * half + 4)
                sp.dma_start(x[:, gs, :], a["x"].rearrange("(g p) d -> p g d", p=P)[:, gs, :]).then_inc(loaded_x[half], 16)
                if half == 0:
                    sp.dma_start(const[:, :], a["const"]).then_inc(loaded_c, 16)
            sp_weights(sp, 0)
            sp.dma_start(bcol[:, :], a["bcol"]).then_inc(loaded_c, 16)
            sp.dma_start(brow_raw, a["brow"]).then_inc(bias_raw, 16)

            sp_stage_a(sp)
            sp_weights(sp, 1)
            if last >= 2:
                sp_stage_c(sp)
            if last >= 3:
                sp_stage_d(sp)
            if last >= 5:
                sp_stage_f(sp)
            if last == 2:
                sp.wait_ge(loaded_x[1], 32)
            sp.wait_ge(x_done, last + 1)
            sp.dma_start(out.rearrange("(g p) d -> p g d", p=P), x[:, :, :]).then_inc(stored, 16)
            sp.wait_ge(stored, 16)

        stages = range(last + 1)

        @block.tensor
        def _(pe):
            for k in stages:
                if k == 0:
                    pe.wait_ge(loaded_c, 32)
                    pe_turn_z(pe, 0, 0)
                (pe_stage_a, lambda e: pe_self(e, 1, w_b), pe_stage_c, pe_stage_d,
                 lambda e: pe_self(e, 4, w_e), pe_stage_f)[k](pe)
                if k == 2:
                    pe.wait_ge(c_added, 16 * E0)
                    pe_keep_warm(pe, WARM_ADDED, 1)
                if k in (0, 1, 2, 4):
                    pe_turn_z(pe, k + 1, 0)
                    if k in (1, 4):
                        pe_keep_warm(pe, WARM_LN, LN_BANK[k + 1] + 3)
                if k == last and k < 5:
                    pe_turn_z(pe, k + 1, 1)

        @block.scalar
        def _(act):
            act_layernorm(act, 0)
            act.wait_ge(bias_set, 1)
            act.wait_ge(bias_raw, 16)
            act.activation(brow[0:1, :], brow_raw, ACT.Copy).then_inc(bias_set, 1)
            for k in stages:
                (act_stage_a, act_stage_b, act_stage_c, act_stage_d, act_stage_e, act_stage_f)[k](act)
                if k in (0, 1, 2, 4):
                    act_layernorm(act, k + 1)

        @block.vector
        def _(dve):
            dve.memset(bias_one, 1.0)
            link(dve, dve.memset(bias_zero, 0.0))
            dve.tensor_copy(ones[:, :], bias_one)
            dve.tensor_copy(brow[:, :], bias_zero).then_inc(bias_set, 1)
            dve_layernorm_loaded(dve, 0, 16)
            for k in stages:
                (dve_stage_a, dve_stage_b, dve_stage_c, dve_stage_d, dve_stage_e, dve_stage_f)[k](dve)
            if last == 5:
                dve.wait_ge(f_x, 4 * NF)
                dve.memset(tick[:, :], 0.0).then_inc(x_done, 1)

        @block.gpsimd
        def _(pool):
            pool.wait_ge(bias_set, 2)
            pool.tensor_tensor(brow[BIAS_ROWS - 1:BIAS_ROWS, :], brow_raw, brow[0:1, :].bitcast(F32),
                               ALU.subtract).then_inc(bias_set, 1)
            if last >= 1:
                pool_self(pool, 1)
            if last >= 2:
                pool_stage_c(pool)
            if last >= 3:
                pool_stage_d(pool)
            if last >= 4:
                pool_self(pool, 4)
            if last >= 5:
                pool_stage_f(pool)


def constants():
    p = np.arange(P)
    c = np.zeros((P, C_END), np.float32)
    c[:, C_ID:C_ID + P] = np.eye(P)
    c[:, C_CAUSAL:C_CAUSAL + L] = np.where(np.arange(L)[None] <= (p % L)[:, None], 0.0, NEG)
    c[:, C_HEAD:C_HEAD + HPT] = (p // HD)[:, None] == np.arange(HPT)[None]
    c[:, C_BATCH:C_BATCH + BG] = (p // L)[:, None] == np.arange(BG)[None]
    c[:, C_INV:C_INV + L] = (1.0 / np.arange(1, L + 1))[None]
    exponent = np.arange(HD // 2, dtype=np.float32) * np.float32(2.0 / HD)
    inv_freq = np.float32(10000.0) ** (-exponent)
    angles = inv_freq[(p % HD) // 2][:, None] * np.arange(L, dtype=np.float32)[None]
    c[:, C_COS:C_COS + L] = np.cos(angles)
    c[:, C_SIN:C_SIN + L] = np.sin(angles) * np.where(p % 2 == 0, -1.0, 1.0)[:, None]
    e = np.arange(E1)
    c[:, C_TRI:C_TRI + E1 * E1] = (e[None, :] < e[:, None]).reshape(1, -1)
    return c


def tiled(w):
    k, n = w.shape
    return w.reshape(k // P, P, n).transpose(1, 0, 2).reshape(P, -1)


def lay_out(i):
    v = {}
    v["x"] = i["x"].reshape(T, D)
    v["const"] = constants()
    col = lambda w: w.reshape(-1, P).T
    ba = i["L0_attn_b_attn"]
    v["bcol"] = np.concatenate([col(i["L0_xattn_b"]), col(ba[0:D]), col(ba[D:2 * D]), col(i["L1_ffn_rb1"]),
                                col(i["L1_ffn_be1"])], 1)
    v["brow"] = np.concatenate([i["L0_xattn_b"], ba[2 * D:], i["L0_attn_b_proj"], i["L1_xattn_bo"],
                                i["L1_ffn_rb2"], i["L1_ffn_be2"].reshape(-1)])[None]
    c = i["ctx_1024"].reshape(G, BG, NK, D)
    v["ctxT"] = c.reshape(G, BG, NK, DT, P).transpose(0, 4, 3, 1, 2).reshape(G, P, -1)
    v["ctx"] = c[:, :, 0:2 * P].reshape(G, BG, 2, P, D).transpose(0, 3, 1, 2, 4).reshape(G, P, -1)
    v["ctx_last"] = c[:, :, 2 * P].reshape(B, D)
    w = i["L0_xattn_W"]
    v["w0"] = np.concatenate([tiled(w), tiled(w.T)], 1)
    w = i["L0_attn_w_attn"]
    v["w1"] = np.concatenate([tiled(w[:, 0:D]), tiled(w[:, D:2 * D]), tiled(w[:, 2 * D:]), tiled(i["L0_attn_w_proj"])], 1)
    v["w2"] = np.concatenate([tiled(i["L0_ffn_Sg"].T), tiled(i["L0_ffn_Su"].T), tiled(i["L0_ffn_Sd"].T),
                              tiled(i["L0_ffn_gate_w"].T)], 1)
    v["w3"] = np.concatenate([tiled(i["L1_xattn_Wq"]), tiled(i["L1_xattn_Wk"].T), tiled(i["L1_xattn_Wv"]),
                              tiled(i["L1_xattn_Wo"])], 1)
    v["w4"] = np.concatenate([tiled(i[f"L1_attn_{n}"].T) for n in ("Wq", "Wk", "Wv", "Wo")], 1)
    v["w5"] = np.concatenate([tiled(i["L1_ffn_rW1"]), tiled(i["L1_ffn_rW2"])], 1)
    for n, s in (("we_g", "L0_ffn_Wg"), ("we_u", "L0_ffn_Wu"), ("we_d", "L0_ffn_Wd")):
        w = i[s].transpose(0, 2, 1)
        v[n] = w.reshape(E0, w.shape[1] // P, P, w.shape[2]).transpose(0, 2, 1, 3).reshape(E0, P, -1)
    for n, s in (("f_w1", "L1_ffn_We1"), ("f_w2", "L1_ffn_We2")):
        w = i[s]
        v[n] = w.reshape(E1, w.shape[1] // P, P, w.shape[2]).transpose(0, 2, 1, 3).reshape(E1, P, -1)
    return {k: np.ascontiguousarray(t) for k, t in v.items()}


def kernel(**inputs):
    import concourse.bacc as bacc
    from concourse.bass_utils import run_bass_kernel_spmd

    arrays = lay_out({k: np.asarray(t) for k, t in inputs.items()})
    nc = bacc.Bacc("TRN2", target_bir_lowering=False, num_devices=1)
    ins = {k: nc.dram_tensor(f"in_{k}", t.shape, mybir.dt.from_np(t.dtype), kind="ExternalInput").ap()
           for k, t in arrays.items()}
    out = nc.dram_tensor("out", [T, D], F32, kind="ExternalOutput").ap()
    build(nc, ins, out)
    r = run_bass_kernel_spmd(nc, [{f"in_{k}": t for k, t in arrays.items()}], core_ids=[0])
    return r.results[0]["out"].reshape(B, L, D)
```

```python
from contextlib import ExitStack

import concourse.bass as bass
import numpy as np
from concourse import mybir

F32 = mybir.dt.float32
F32R = mybir.dt.float32r
U32 = mybir.dt.uint32
ALU = mybir.AluOpType
ACT = mybir.ActivationFunctionType
AX_X = mybir.AxisListType.X

B, L, D = 32, 32, 256
NK = 257
P = 128
T = B * L
G = T // P
BG = P // L
DT = D // P
H, HD = 16, 16
HPT = P // HD
QH = P // L
NQ = H // QH
E0, I0, C0 = 16, 1024, 128
IS = 512
XH, XD = 8, 64
XI = XH * XD
E1, I1 = 4, 1024
RH = 512
HALF = T // 2
EDGE_ROWS = (0, 32, 64)
BIAS_ROWS = 33
NEG = -1.0e30
EPS = 1e-5

C_ID, C_CAUSAL, C_HEAD, C_BATCH, C_INV, C_COS, C_SIN, C_TRI, C_END = np.cumsum(
    [0, P, L, HPT, BG, L, L, L, E1 * E1]).tolist()
K_B, K_BQ, K_BK, K_RB1, K_BE1, K_END = np.cumsum([0, DT, DT, DT, RH // P, E1 * I1 // P]).tolist()
R_B, R_BV, R_BP, R_BO, R_RB2, R_BE2, R_END = np.cumsum([0, D, D, D, D, E1, E1 * D]).tolist()


def sort_steps(n):
    p = 1
    while p < n:
        k = p
        while k >= 1:
            yield p, k
            k //= 2
        p *= 2


def build(nc, a, out, stop=None):
    with ExitStack() as ctx:
        def sb(name, shape, dt=F32):
            return ctx.enter_context(nc.sbuf_tensor(name, shape, dt))

        def sem(name):
            return ctx.enter_context(nc.semaphore(name))

        bank = [ctx.enter_context(nc.psum_tensor(f"bank{i}", [P, 512], F32)) for i in range(8)]

        x_at = -(-nc.sbuf_base // 32) * 32
        x = sb("x", [P, G, D])
        z = sb("z", [P, G, D])
        zT = sb("zT", [P, DT, T])
        const = sb("const", [P, C_END])
        bcol = sb("bcol", [P, K_END])
        brow = sb("brow", [BIAS_ROWS, R_END], F32R)
        ones = sb("ones", [BIAS_ROWS, P], F32R)
        w_even = sb("w_even", [P, 3072 + E0 * DT])
        w_odd_at = nc.sbuf_base
        w_odd = sb("w_odd", [P, 4096 + 64])
        stats = sb("stats", [P, G, 6])
        mv = sb("mv", [P, G, 2])
        veps = sb("veps", [P, G])
        std = sb("std", [P, G])
        rstd = sb("rstd", [P, G])
        small = sb("small", [P, 1024])
        arena_at = nc.sbuf_base
        arena = sb("arena", [P, 35904])
        z_dram = nc.dram_tensor("z_rows", [T, D], F32)
        acc_dram = nc.dram_tensor("acc_rows", [T, D], F32)

        def shaped(v, dims):
            if len(dims) == 1:
                return v
            names = "abcdef"[:len(dims)]
            return v.rearrange(f"p ({' '.join(names)}) -> p {' '.join(names)}",
                               **{c: d for c, d in zip(names[1:], dims[1:])})

        def area(off, *dims):
            return shaped(arena[:, off:off + int(np.prod(dims))], dims)

        def rounded(name, off, *dims, at=arena_at):
            n = int(np.prod(dims))
            t = nc.alloc_sbuf_tensor_at(name, [P, n], F32R, offset=at + 4 * off)
            return shaped(t[:, :], dims)

        def split(name, off, *dims, at=arena_at):
            return rounded(name + "_hi", off, *dims, at=at), rounded(name + "_lo", off + int(np.prod(dims)), *dims, at=at)

        def matmul3(pe, o, lhsT, rhs, at_l, at_r, start, stop):
            for n, (i, j) in enumerate(((0, 0), (0, 1), (1, 0))):
                r = pe.matmul(o, lhsT[i][at_l], rhs[j][at_r], start=(start and n == 0), stop=(stop and n == 2))
            return r

        ident = const[:, C_ID:C_ID + P]
        brow_raw = area(26000, R_END)[0:1, :]
        bias_zero = area(26000 + R_END, R_END)[0:BIAS_ROWS, :]
        bias_one = area(26000 + 2 * R_END, P)[0:BIAS_ROWS, :]

        ln_var, ln_std, ln_z = sem("ln_var"), sem("ln_std"), sem("ln_z")
        ln_turned, ln_zT_act, ln_zT_dve = sem("ln_turned"), sem("ln_zT_act"), sem("ln_zT_dve")
        dve_chain = sem("dve_chain")
        loaded_x = [sem(f"loaded_x{half}") for half in range(2)]
        loaded_c, bias_raw, bias_set = sem("loaded_c"), sem("bias_raw"), sem("bias_set")
        w_loaded = [sem("w_even_loaded"), sem("w_odd_loaded")]
        x_done = sem("x_done")
        stored = sem("stored")
        tick = sb("tick", [P, 1])
        links = [0]
        WARM_ROPE, WARM_SORT, WARM_SORTED, WARM_ADDED, WARM_LN = 16, 8, 14, 10, 8
        LN_BANK = (0, 4, 4, 0, 4, 4)

        def link(eng, ins):
            links[0] += 1
            ins.then_inc(dve_chain, 1)
            eng.wait_ge(dve_chain, links[0])

        def sp_weights(sp, k):
            if k >= 2:
                sp.wait_ge(x_done, k - 1)
            v = a[f"w{k}"]
            sp.dma_start((w_even, w_odd)[k % 2][:, 0:v.shape[1]], v).then_inc(w_loaded[k % 2], 16)

        def wait_weights(pe, k):
            pe.wait_ge(w_loaded[k % 2], 16 * (k // 2 + 1))

        def dve_stats(dve, g):
            return dve.bn_stats(stats[:, g, :], x[:, g, :])

        def dve_variances(dve, half):
            gs = slice(4 * half, 4 * half + 4)
            for g in range(4 * half, 4 * half + 4):
                i = dve.bn_aggr(mv[:, g, :], stats[:, g, :])
            link(dve, i)
            dve.tensor_scalar(veps[:, gs], mv[:, gs, 1], EPS, None, ALU.add).then_inc(ln_var, 1)

        def dve_scale(dve, k, half):
            gs = slice(4 * half, 4 * half + 4)
            dve.wait_ge(ln_std, 2 * k + half + 1)
            link(dve, dve.reciprocal(rstd[:, gs], std[:, gs]))
            for g in range(4 * half, 4 * half + 4):
                dve.tensor_scalar(z[:, g, :], x[:, g, :], mv[:, g, 0:1], rstd[:, g:g + 1],
                                  ALU.subtract, ALU.mult).then_inc(ln_z, 1)

        def zT_out(k, j):
            return zT[:, :, 256 * j:256 * j + 256], bank[LN_BANK[k] + j][:, :].rearrange("p (k t) -> p k t", k=DT)

        def dve_zT(dve, k, half):
            dve.wait_ge(ln_turned, 4 * k + 2 * half + 2)
            dve.tensor_copy(*zT_out(k, 2 * half + 1)).then_inc(ln_zT_dve, 1)

        def dve_layernorm_end(dve, k):
            dve_variances(dve, 1)
            dve_zT(dve, k, 0)
            dve_scale(dve, k, 1)
            dve_zT(dve, k, 1)

        def dve_layernorm_loaded(dve, k, count):
            for half in range(2):
                dve.wait_ge(loaded_x[half], count)
                for g in range(4 * half, 4 * half + 4):
                    i = dve_stats(dve, g)
                link(dve, i)
                if half == 0:
                    dve_variances(dve, 0)
                    dve_scale(dve, k, 0)
            dve_layernorm_end(dve, k)

        def dve_added(dve, k, g, added):
            if g >= 1:
                dve.wait_ge(added, g)
                dve_stats(dve, g - 1)
            if g == 4:
                link(dve, dve.memset(tick[:, :], 0.0))
                dve_variances(dve, 0)
            if g == 6:
                dve_scale(dve, k + 1, 0)
            if g == 7:
                dve.wait_ge(added, G)
                link(dve, dve_stats(dve, 7))
                dve.memset(tick[:, :], 0.0).then_inc(x_done, 1)
                dve_layernorm_end(dve, k + 1)

        def act_std(act, k, half):
            act.wait_ge(ln_var, 2 * k + half + 1)
            gs = slice(4 * half, 4 * half + 4)
            act.activation(std[:, gs], veps[:, gs], ACT.Sqrt).then_inc(ln_std, 1)

        def act_zT(act, k, half):
            act.wait_ge(ln_turned, 4 * k + 2 * half + 1)
            act.activation(*zT_out(k, 2 * half), ACT.Copy).then_inc(ln_zT_act, 1)

        def act_layernorm(act, k):
            for half in range(2):
                act_std(act, k, half)
                act_zT(act, k, half)

        def pe_turn_z(pe, k, half):
            for j in (2 * half, 2 * half + 1):
                pe.wait_ge(ln_z, G * k + 2 * j + 2)
                for g in (2 * j, 2 * j + 1):
                    for dt in range(DT):
                        c = dt * 256 + (g % 2) * P
                        i = pe.transpose(bank[LN_BANK[k] + j][:, c:c + P], z[:, g, dt * P:dt * P + P], ident)
                i.then_inc(ln_turned, 1)

        def pe_wait_zT(pe, k, half):
            pe.wait_ge(ln_zT_act, 2 * k + half + 1)
            pe.wait_ge(ln_zT_dve, 2 * k + half + 1)

        def pe_keep_warm(pe, n, bank_no):
            for _ in range(n):
                pe.matmul(bank[bank_no][:, 0:256], ident, const[:, 0:256], start=True, stop=True)

        def staggered(n, *steps):
            for t in range(n + len(steps) - 1):
                for lag, step in reversed(list(enumerate(steps))):
                    if step is not None and 0 <= t - lag < n:
                        step(t - lag)

        ctxT_v = a["ctxT"]
        ctx_v = a["ctx"]
        last_v = a["ctx_last"]
        SLOTS = {0: 4, 3: 2}
        ringT = [area(2056 * s, DT, BG, NK) for s in (0, 1)] + [area(16384 + 2056 * s, DT, BG, NK) for s in (0, 1)]
        ringN = [area(4112 + 2048 * s, BG, 2, D) for s in (0, 1)] + [area(20496 + 2048 * s, BG, 2, D) for s in (0, 1)]
        ringL = [area(8208 + 1024 * s, 1024) for s in (0, 1)] + [area(24592 + 256 * s, 256) for s in (0, 1)]
        RING_END = 10256
        keys_loaded, rows_loaded = ([sem(f"{n}_loaded{s}") for s in range(4)] for n in ("keys", "rows"))
        KEYS_A, ROWS_A = 16 * G // SLOTS[0], 32 * G // SLOTS[0]
        wa_o = w_even[:, 0:DT * D].rearrange("p (k n) -> p k n", k=DT)
        wa_T = w_even[:, DT * D:2 * DT * D].rearrange("p (k n) -> p k n", k=DT)
        zwT = area(RING_END, DT, T)
        a_p = [area(RING_END + 2048 + 272 * s, NK) for s in range(2)]
        a_pT = [area(RING_END + 2592 + 384 * s, 384) for s in range(2)]
        a_att = [area(RING_END + 3360 + 256 * s, D) for s in range(2)]
        a_attT = [area(RING_END + 3872 + 256 * s, D) for s in range(2)]
        zb = small[:, 0:G]
        a_max, a_top, a_nb = small[:, 8:16], small[:, 16:24], small[:, 24:32]
        a_sum, a_inv = small[:, 32:40], small[:, 40:48]
        a_edge = [small[:, 48 + 4 * s:52 + 4 * s] for s in range(2)]
        a_zw, a_zw_out, a_zb, a_zb_out = sem("a_zw"), sem("a_zw_out"), sem("a_zb"), sem("a_zb_out")
        a_s, a_nbias, a_exp, a_edged, a_turn, a_turned = (
            sem("a_s"), sem("a_nbias"), sem("a_exp"), sem("a_edged"), sem("a_turn"), sem("a_turned"))
        a_av, a_norm, a_attturn, a_attturned, a_y, a_x = (
            sem("a_av"), sem("a_norm"), sem("a_attturn"), sem("a_attturned"), sem("a_y"), sem("a_x"))

        def sp_context(sp, k, keys_used, rows_used):
            n = SLOTS[k]
            for g in range(G):
                s = g % n
                if g >= n:
                    sp.wait_ge(keys_used[0], keys_used[1] * (g - n + 1))
                sp.dma_start(ringT[s], ctxT_v[g].rearrange("p (k b n) -> p k b n", k=DT, b=BG)).then_inc(keys_loaded[s], 16)
                if g >= n:
                    sp.wait_ge(rows_used[0], rows_used[1] * (g - n + 1))
                sp.dma_start(ringN[s], ctx_v[g].rearrange("p (b k d) -> p b k d", b=BG, k=2)).then_inc(rows_loaded[s], 16)
                lasts = last_v[g * BG:g * BG + BG, :]
                if k == 0:
                    sp.dma_start(ringL[s][0:BG, 0:D], lasts).then_inc(rows_loaded[s], 16)
                else:
                    for r in EDGE_ROWS:
                        sp.dma_start(ringL[s][r:r + 1, :].rearrange("o (b d) -> o b d", b=BG),
                                     lasts[None]).then_inc(rows_loaded[s], 16)

        def sp_stage_a(sp):
            sp_context(sp, 0, (a_s, 1), (a_av, 1))

        def pe_stage_a(pe):
            wait_weights(pe, 0)
            for n in range(2):
                if n:
                    pe_turn_z(pe, 0, 1)
                pe_wait_zT(pe, 0, n)
                for m in range(DT):
                    for k in range(DT):
                        i = pe.matmul(bank[4 + 2 * n + m][:, :], wa_o[:, k, m * P:m * P + P],
                                      zT[:, k, n * 512:n * 512 + 512], start=(k == 0), stop=(k == DT - 1))
                    i.then_inc(a_zw, 1)
            for g in range(G):
                for k in range(DT):
                    i = pe.matmul(bank[0][:, g:g + 1], zT[:, k, g * P:g * P + P],
                                  bcol[:, K_B + k:K_B + k + 1], start=(k == 0), stop=(k == DT - 1))
            i.then_inc(a_zb, 1)
            pe.wait_ge(a_zw_out, 4)
            pe.wait_ge(a_zb_out, 1)

            def scores(g):
                pe.wait_ge(keys_loaded[g % 4], 16 * (g // 4 + 1))
                if g >= 2:
                    pe.wait_ge(a_exp, g - 1)
                for b in range(BG):
                    c = g * P + b * L
                    for k in range(DT):
                        i = pe.matmul(bank[g % 2][b * L:b * L + L, 0:NK], zwT[:, k, c:c + L],
                                      ringT[g % 4][:, k, b, :], start=(k == 0), stop=(k == DT - 1))
                i.then_inc(a_s, 1)

            def turn_p(g):
                pe.wait_ge(a_edged, g + 1)
                if g >= 2:
                    pe.wait_ge(a_turned, g - 1)
                bk, p = bank[2 + g % 2], a_p[g % 2]
                pe.transpose(bk[:, 0:P], p[:, 0:P], ident)
                pe.transpose(bk[:, P:2 * P], p[:, P:2 * P], ident)
                pe.transpose(bk[0:BG, 2 * P:3 * P], a_edge[g % 2], ident).then_inc(a_turn, 1)

            def values(g):
                pe.wait_ge(a_turned, g + 1)
                pe.wait_ge(rows_loaded[g % 4], 32 * (g // 4 + 1))
                if g >= 2:
                    pe.wait_ge(a_norm, g - 1)
                o, pT = bank[4 + g % 2], a_pT[g % 2]
                for b in range(BG):
                    for k in range(2):
                        pe.matmul(o[b * L:b * L + L, 0:D], pT[:, k * P + b * L:k * P + b * L + L],
                                  ringN[g % 4][:, b, k, :], start=(k == 0), stop=False, skip_group_check=True)
                pe.matmul(o[:, 0:D], pT[0:BG, 2 * P:3 * P], ringL[g % 4][0:BG, 0:D],
                          start=False, stop=True, skip_group_check=True).then_inc(a_av, 1)

            def turn_att(g):
                pe.wait_ge(a_norm, g + 1)
                if g >= 1:
                    pe.wait_ge(a_attturned, g)
                pe.transpose(bank[6][:, 0:P], a_att[g % 2][:, 0:P], ident)
                pe.transpose(bank[6][:, P:2 * P], a_att[g % 2][:, P:2 * P], ident).then_inc(a_attturn, 1)

            def project(g):
                pe.wait_ge(a_attturned, g + 1)
                if g == 0:
                    pe.wait_ge(bias_set, 3)
                if g >= 1:
                    pe.wait_ge(a_x, g)
                for k in range(DT):
                    pe.matmul(bank[7][:, 0:D], a_attT[g % 2][:, k * P:k * P + P], wa_T[:, k, :],
                              start=(k == 0), stop=False)
                pe.matmul(bank[7][:, 0:D], ones[:, :], brow[:, R_B:R_B + D],
                          start=False, stop=True).then_inc(a_y, 1)

            staggered(G, scores, turn_p, values, turn_att, project)

        def act_stage_a(act):
            for j in range(4):
                act.wait_ge(a_zw, j + 1)
                m, n = j % 2, j // 2
                act.activation(zwT[:, m, n * 512:n * 512 + 512], bank[4 + j][:, :], ACT.Copy).then_inc(a_zw_out, 1)

            def exps(g):
                act.wait_ge(a_nbias, g + 1)
                if g >= 2:
                    act.wait_ge(a_turn, g - 1)
                act.activation(a_p[g % 2], bank[g % 2][:, 0:NK], ACT.Exp, bias=a_nb[:, g:g + 1],
                               accum_out=a_sum[:, g:g + 1]).then_inc(a_exp, 1)

            def turned_p(g):
                act.wait_ge(a_turn, g + 1)
                if g >= 2:
                    act.wait_ge(a_av, g - 1)
                act.activation(a_pT[g % 2][:, 0:2 * P], bank[2 + g % 2][:, 0:2 * P], ACT.Copy)
                act.activation(a_pT[g % 2][0:BG, 2 * P:3 * P], bank[2 + g % 2][0:BG, 2 * P:3 * P],
                               ACT.Copy).then_inc(a_turned, 1)

            def turned_att(g):
                act.wait_ge(a_attturn, g + 1)
                if g >= 2:
                    act.wait_ge(a_y, g - 1)
                act.activation(a_attT[g % 2], bank[6][:, 0:D], ACT.Copy).then_inc(a_attturned, 1)

            staggered(G, exps, turned_p, None, turned_att)

        def dve_stage_a(dve):
            dve.wait_ge(a_zb, 1)
            dve.tensor_copy(zb, bank[0][:, 0:G]).then_inc(a_zb_out, 1)
            dve.wait_ge(a_zb_out, 1)

            def maxima(g):
                dve.wait_ge(a_s, g + 1)
                c = slice(g, g + 1)
                link(dve, dve.tensor_reduce(a_max[:, c], bank[g % 2][:, 0:NK], AX_X, ALU.max))
                link(dve, dve.tensor_tensor(a_top[:, c], a_max[:, c], zb[:, c], ALU.add))
                dve.tensor_tensor(a_nb[:, c], zb[:, c], a_top[:, c], ALU.subtract).then_inc(a_nbias, 1)

            def edges(g):
                dve.wait_ge(a_exp, g + 1)
                dve.reciprocal(a_inv[:, g:g + 1], a_sum[:, g:g + 1])
                dve.tensor_scalar(a_edge[g % 2], const[:, C_BATCH:C_BATCH + BG], a_p[g % 2][:, NK - 1:NK], None,
                                  ALU.mult).then_inc(a_edged, 1)

            def normalize(g):
                dve.wait_ge(a_av, g + 1)
                dve.wait_ge(a_edged, g + 1)
                if g >= 2:
                    dve.wait_ge(a_attturn, g - 1)
                dve.tensor_scalar(a_att[g % 2], bank[4 + g % 2][:, 0:D], a_inv[:, g:g + 1], None,
                                  ALU.mult).then_inc(a_norm, 1)

            def residual(g):
                dve.wait_ge(a_y, g + 1)
                dve.scalar_tensor_tensor(out=x[:, g, :], in0=bank[7][:, 0:D], scalar=0.0, in1=x[:, g, :],
                                         op0=ALU.max, op1=ALU.add).then_inc(a_x, 1)
                dve_added(dve, 0, g, a_x)

            def maxima_edges(g):
                maxima(g)
                edges(g)

            staggered(G, maxima_edges, None, normalize, None, residual)

        Kx = area(0, 2, DT, B // 2, HPT, L)
        Vx = area(16384, B, NQ, QH, HD)
        S = area(24576, G, H * L)
        S_rows = S.rearrange("p g (h j) -> p (g h) j", j=L)
        qT = area(28672, DT, T)
        kT = area(30720, DT, T)
        pT = [area(32768 + 512 * s, NQ, P) for s in range(2)]
        vrow = area(33792, G, D)
        yT = area(28672, DT, T)
        HR = G * H // 2
        sort_a, sort_b = area(0, HR, L), area(2048, HR, L)
        notfirst = area(4096, HR, L)
        sums = area(6144, HR, L)
        rot = z[:, :, :].rearrange("p g d -> p (g d)")[:, 0:DT * HALF].rearrange("p (k t) -> p k t", k=DT)
        SELF_SEMS = ("proj", "k_out", "q_out", "v", "v_out", "vx", "kx_act", "kx_dve", "s",
                     "lowered", "probs", "turn", "turned", "av", "y", "out", "added")
        self_sems = {k: {s: sem(f"{n}_{s}") for s in SELF_SEMS + more}
                     for k, n, more in ((1, "b", ("s_out", "sorted", "carried", "flagged")), (4, "e", ("rope", "exp")))}
        stat = small[:, 0:G * H]
        bq_scaled = small[:, 128:128 + DT]
        stat_b = stat[:, :, None].broadcast_to([P, G * H, L])
        mask_of = {k: (nc.alloc_sbuf_tensor_at(f"mask{k}", [P, H * L], F32R, offset=w_odd_at + 4 * 2560),
                       nc.alloc_sbuf_tensor_at(f"mask_ident{k}", [P, P], F32R, offset=w_odd_at + 4 * (2560 + H * L)))
                   for k in (1, 4)}

        def halves(t, m, n):
            return t[:, m, n * HALF:n * HALF + HALF].rearrange("p (b j) -> p b j", j=L)

        def pe_self(pe, k, w):
            q = self_sems[k]
            logits_gone = q["s_out" if k == 1 else "lowered"]
            wait_weights(pe, k)

            def project_in(n):
                for c in range(4):
                    j, m = 1 - c // 2, c % 2
                    if n:
                        pe.wait_ge(logits_gone, c + 1)
                    elif k == 4 and c >= 2:
                        pe.wait_ge(d_x, G - 3 + c)
                    for kk in range(DT):
                        i = pe.matmul(bank[c][:, :], w(j)[:, kk, m * P:m * P + P],
                                      zT[:, kk, n * HALF:n * HALF + HALF], start=(kk == 0), stop=(kk == DT - 1))
                    i.then_inc(q["proj"], 1)

            def values_in(g):
                if g >= 4:
                    pe.wait_ge(q["v_out"], g - 3)
                o = bank[4 + g % 4][:, 0:D]
                for kk in range(DT):
                    i = pe.matmul(o, zT[:, kk, g * P:g * P + P], w(2)[:, kk, :], start=(kk == 0),
                                  stop=(kk == DT - 1 and k == 4))
                if k == 1:
                    i = pe.matmul(o, ones[:, :], brow[:, R_BV:R_BV + D], start=False, stop=True)
                i.then_inc(q["v"], 1)

            def scores(g):
                half = g // 4
                if g % 4 == 0:
                    if k == 4 and half:
                        pe.wait_ge(q["added"], 4)
                    pe.wait_ge(q["k_out"], 2 * (half + 1))
                    pe.wait_ge(q["q_out"], 2 * (half + 1))
                    if k == 1:
                        pe.wait_ge(q["kx_act"], 8 * (half + 1))
                        pe.wait_ge(*((q["flagged"], 2 + HPT) if half else (q["kx_dve"], 8)))
                    else:
                        pe.wait_ge(q["kx_act"], 8 * (half + 1))
                        pe.wait_ge(q["kx_dve"], 8 * (half + 1))
                        pe.wait_ge(q["rope"], 8 * (half + 1))
                if g == 0:
                    pe.wait_ge(q["vx"], 2)
                mask, mask_ident = mask_of[k]
                pe.matmul(bank[g % 4][:, :], mask_ident[:, :], mask[:, :], start=True, stop=False, skip_group_check=True)
                for b in range(BG):
                    c = g * P + b * L
                    for kk in range(DT):
                        i = pe.matmul(bank[g % 4][b * L:b * L + L, kk * 256:kk * 256 + 256], qT[:, kk, c:c + L],
                                      Kx[:, half, kk, g % 4 * BG + b, :, :].rearrange("p h j -> p (h j)"),
                                      start=False, stop=(b == BG - 1 and kk == DT - 1), skip_group_check=True)
                i.then_inc(q["s"], 1)

            def turn(g):
                pe.wait_ge(q["probs"], g + 1)
                if g == 0:
                    pe.wait_ge(q["v_out"], G)
                if g >= 2:
                    pe.wait_ge(q["turned"], g - 1)
                for m in range(NQ):
                    i = pe.transpose(bank[4 + g % 2][:, m * P:m * P + P], S[:, g, m * P:m * P + P], ident)
                i.then_inc(q["turn"], 1)

            def values(g):
                pe.wait_ge(q["turned"], g + 1)
                if g % 4 == 0:
                    pe.wait_ge(q["vx"], g // 4 + 4)
                if g >= 1:
                    pe.wait_ge(q["y"], g)
                for b in range(BG):
                    for m in range(NQ):
                        r, kk = (m % 2) * 64, m // 2
                        c = kk * P + b * L
                        i = pe.matmul(bank[6][r:r + 64, c:c + L],
                                      Vx[:, g * BG + b, m, :, :].rearrange("p h d -> p (h d)"),
                                      pT[g % 2][:, m, b * L:b * L + L], start=True, stop=True)
                i.then_inc(q["av"], 1)

            def project(g):
                pe.wait_ge(q["y"], g + 1)
                if k == 4 and g == 0:
                    pe.wait_ge(q["k_out"], 4)
                    pe.wait_ge(q["q_out"], 4)
                elif k == 1 and g < 4 or k == 4 and g >= 4:
                    pe.wait_ge(logits_gone, g % 4 + 5)
                elif k == 1:
                    pe.wait_ge(q["added"], g - 3)
                o = bank[g % 4][:, 0:D]
                for kk in range(DT):
                    i = pe.matmul(o, yT[:, kk, g * P:g * P + P], w(3)[:, kk, :], start=(kk == 0),
                                  stop=(kk == DT - 1 and k == 4))
                if k == 1:
                    i = pe.matmul(o, ones[:, :], brow[:, R_BP:R_BP + D], start=False, stop=True)
                i.then_inc(q["out"], 1)

            def attend(first, end):
                for g in range(first, end + 2):
                    if g < end:
                        turn(g)
                    if first <= g - 1 < end:
                        values(g - 1)
                    if first <= g - 2:
                        project(g - 2)

            pe_wait_zT(pe, k, 0)
            project_in(0)
            pe_turn_z(pe, k, 1)
            pe_wait_zT(pe, k, 1)
            for g in range(G if k == 4 else 4):
                values_in(g)
            if k == 4:
                pe.wait_ge(q["q_out"], 2)
                pe_keep_warm(pe, WARM_ROPE, 3)
            for g in range(4):
                scores(g)
            for g in range(G if k == 4 else 4, G):
                values_in(g)
            project_in(1)
            if k == 1:
                pe.wait_ge(q["v_out"], G)
                pe.wait_ge(q["sorted"], 26)
                pe_keep_warm(pe, WARM_SORT, 7)
                for g in range(4, G):
                    scores(g)
            attend(0, 4)
            if k == 4:
                pe_keep_warm(pe, WARM_ROPE, 7)
                for g in range(4, G):
                    scores(g)
            else:
                pe.wait_ge(q["sorted"], 60)
                pe_keep_warm(pe, WARM_SORTED, 7)
            attend(4, G)

        def act_spread_keys(act, q, m, n, heads=range(HPT)):
            for h in heads:
                act.activation(Kx[:, n, m, :, h, :], halves(kT, m, n), ACT.Copy,
                               scale=const[:, C_HEAD + h:C_HEAD + h + 1]).then_inc(q["kx_act"], 1)

        def act_turned(act, q, g):
            act.wait_ge(q["turn"], g + 1)
            if g >= 2:
                act.wait_ge(q["av"], g - 1)
            act.activation(pT[g % 2].rearrange("p m t -> p (m t)"), bank[4 + g % 2][:, :],
                           ACT.Copy).then_inc(q["turned"], 1)

        def act_values_out(act, q, g):
            act.wait_ge(q["av"], g + 1)
            act.activation(yT[:, :, g * P:g * P + P], bank[6][:, 0:D].rearrange("p (k t) -> p k t", k=DT),
                           ACT.Copy).then_inc(q["y"], 1)

        def act_attend(act, q, first, end):
            for g in range(first, end + 1):
                if g < end:
                    act_turned(act, q, g)
                if g > first:
                    act_values_out(act, q, g - 1)

        def act_stage_b(act):
            q = self_sems[1]

            def keys(n):
                for m in range(DT):
                    act.wait_ge(q["proj"], 4 * n + m + 1)
                    act.activation(kT[:, m, n * HALF:n * HALF + HALF], bank[m][:, :], ACT.Identity,
                                   bias=bcol[:, K_BK + m:K_BK + m + 1]).then_inc(q["k_out"], 1)
                act.wait_ge(q["k_out"], 2 * n + 2)

            def values_in(g):
                act.wait_ge(q["v"], g + 1)
                act.activation(vrow[:, g, :], bank[4 + g % 4][:, 0:D], ACT.Copy).then_inc(q["v_out"], 1)

            def logits_out(g):
                act.wait_ge(q["s"], g + 1)
                act.activation(S[:, g, :], bank[g % 4][:, :], ACT.Copy).then_inc(q["s_out"], 1)

            keys(0)
            act_spread_keys(act, q, 0, 0)
            for g in range(4):
                values_in(g)
            for g in range(4):
                logits_out(g)

            def prepare(t):
                if t < 4:
                    values_in(4 + t)
                elif t == 4:
                    keys(1)
                elif t == 5:
                    for m in range(DT):
                        act.wait_ge(q["proj"], 7 + m)
                        act.activation(qT[:, m, HALF:T], bank[2 + m][:, :], ACT.Identity, scale=HD ** -0.5,
                                       bias=bq_scaled[:, m:m + 1]).then_inc(q["q_out"], 1)
                else:
                    act_spread_keys(act, q, 0, 1, range(2 * (t - 6), 2 * (t - 5)))

            carried = 0

            ATTEND_AT = (0, 1, 3, 5, 7)

            def attend(t):
                if t < 4:
                    act_turned(act, q, t)
                if t >= 1:
                    act_values_out(act, q, t - 1)

            for half in range(2):
                src, dst = None, sort_a
                steps = 0
                for s, (p_, k_) in enumerate(sort_steps(L)):
                    if k_ < p_:
                        act.wait_ge(q["sorted"], 30 * half + 2 * s)
                        if carried:
                            act.wait_ge(q["carried"], carried)
                        c = 2 * p_ // k_
                        u = [t.rearrange("p r (c i) -> p r c i", i=k_) if c == L // k_ else
                             t.rearrange("p r (b c i) -> p (r b) c i", c=c, i=k_) for t in (src, dst)]
                        act.activation(u[1][:, :, 0:c:c - 1, :], u[0][:, :, 0:c:c - 1, :],
                                       ACT.Copy).then_inc(q["carried"], 1)
                        carried += 1
                        if half == 0:
                            prepare(steps)
                        elif steps in ATTEND_AT:
                            attend(ATTEND_AT.index(steps))
                        steps += 1
                    src, dst = dst, (sort_b if dst is sort_a else sort_a)
                if half == 0:
                    for g in range(4, G):
                        logits_out(g)
                for g in range(4 * half, 4 * half + 4):
                    act.wait_ge(q["lowered"], g + 1)
                    act.activation(S[:, g, :], S[:, g, :], ACT.Relu).then_inc(q["probs"], 1)
            act_attend(act, q, 4, G)

        def act_stage_e(act):
            q = self_sems[4]

            def keys_queries(n):
                for c in range(4):
                    act.wait_ge(q["proj"], 4 * n + c + 1)
                    dst = (kT, qT)[c // 2]
                    act.activation(dst[:, c % 2, n * HALF:n * HALF + HALF], bank[c][:, :],
                                   ACT.Copy).then_inc(q[("k_out", "q_out")[c // 2]], 1)

            keys_queries(0)
            for g in range(G):
                act.wait_ge(q["v"], g + 1)
                act.activation(vrow[:, g, :], bank[4 + g % 4][:, 0:D], ACT.Copy).then_inc(q["v_out"], 1)
            act.wait_ge(q["rope"], 4)
            act_spread_keys(act, q, 0, 0)

            def exps(g):
                act.wait_ge(q["lowered"], g + 1)
                act.activation(S[:, g, :], S[:, g, :], ACT.Exp, scale=HD ** -0.5).then_inc(q["exp"], 1)

            for g in range(4):
                exps(g)
            keys_queries(1)
            act_attend(act, q, 0, 4)
            act.wait_ge(q["rope"], 12)
            act_spread_keys(act, q, 0, 1)
            for g in range(4, G + 3):
                if g < G:
                    exps(g)
                if 4 <= g - 2 < G:
                    act_turned(act, q, g - 2)
                if 4 <= g - 3:
                    act_values_out(act, q, g - 3)

        def pool_self(pool, k):
            q = self_sems[k]
            pool.wait_ge(x_done, k)
            mask, mask_ident = mask_of[k]
            pool.tensor_copy(mask[:, :].rearrange("p (h j) -> p h j", j=L),
                             const[:, None, C_CAUSAL:C_CAUSAL + L].broadcast_to([P, H, L])).then_inc(q["vx"], 1)
            pool.tensor_copy(mask_ident[:, :], ident).then_inc(q["vx"], 1)
            pool.memset(arena[:, 16384:24576], 0.0).then_inc(q["vx"], 1)
            pool.wait_ge(q["vx"], 3)
            if k == 1:
                pool.wait_ge(q["s"], 4)
                pool.memset(notfirst, 1.0).then_inc(q["flagged"], 1)
                pool.wait_ge(q["flagged"], 1)
                pool.memset(notfirst[:, :, 0:1], 0.0).then_inc(q["flagged"], 1)
                pool.wait_ge(q["flagged"], 2)
                pool.wait_ge(q["k_out"], 4)
                for h in range(HPT):
                    pool.tensor_scalar(Kx[:, 1, 1, :, h, :], halves(kT, 1, 1), const[:, C_HEAD + h:C_HEAD + h + 1],
                                       None, ALU.mult).then_inc(q["flagged"], 1)
                pool.wait_ge(q["flagged"], 2 + HPT)
            vx = Vx.rearrange("p (g b) m h d -> p g b m h d", b=BG)
            vr = vrow.rearrange("p g (m h d) -> p g m h d", m=NQ, h=QH)
            for half in range(2):
                gs = slice(4 * half, 4 * half + 4)
                pool.wait_ge(q["v_out"], 4 * half + 4)
                for b in range(BG):
                    for h in range(QH):
                        i = pool.tensor_copy(vx[h * L:h * L + L, gs, b, :, h, :], vr[b * L:b * L + L, gs, :, h, :])
                i.then_inc(q["vx"], 1)

        def dve_spread_keys(dve, q, m, n):
            for h in range(HPT):
                dve.tensor_scalar(Kx[:, n, m, :, h, :], halves(kT, m, n), const[:, C_HEAD + h:C_HEAD + h + 1], None,
                                  ALU.mult).then_inc(q["kx_dve"], 1)

        def dve_residual(dve, k, g):
            q = self_sems[k]
            dve.wait_ge(q["out"], g + 1)
            dve.tensor_tensor(x[:, g, :], bank[g % 4][:, 0:D], x[:, g, :], ALU.add).then_inc(q["added"], 1)
            dve_added(dve, k, g, q["added"])

        def dve_stage_b(dve):
            q = self_sems[1]

            def queries(n):
                for m in range(DT):
                    dve.wait_ge(q["proj"], 4 * n + 3 + m)
                    dve.tensor_scalar(qT[:, m, n * HALF:n * HALF + HALF], bank[2 + m][:, :],
                                      bcol[:, K_BQ + m:K_BQ + m + 1], HD ** -0.5, ALU.add,
                                      ALU.mult).then_inc(q["q_out"], 1)

            dve.tensor_scalar(bq_scaled, bcol[:, K_BQ:K_BQ + DT], HD ** -0.5, None, ALU.mult)
            queries(0)
            dve.wait_ge(q["k_out"], 2)
            dve_spread_keys(dve, q, 1, 0)
            carried = 0
            for half in range(2):
                dve.wait_ge(q["s_out"], 4 * half + 4)
                mine = slice(HR * half, HR * half + HR)
                src, dst = S_rows[:, mine, :], sort_a
                for s, (p_, k_) in enumerate(sort_steps(L)):
                    if s:
                        dve.wait_ge(q["sorted"], 30 * half + 2 * s)
                    if carried:
                        dve.wait_ge(q["carried"], carried)
                    u, v = (t.rearrange("p r (b n) -> p (r b) n", n=2 * p_) for t in (src, dst))
                    if k_ < p_:
                        u, v = (t[:, :, k_:2 * p_ - k_] for t in (u, v))
                        carried += 1
                    u, v = (t.rearrange("p r (m c i) -> p r m c i", c=2, i=k_) for t in (u, v))
                    lo, hi = u[:, :, :, 0, :], u[:, :, :, 1, :]
                    dve.tensor_tensor(v[:, :, :, 0, :], lo, hi, ALU.max).then_inc(q["sorted"], 1)
                    dve.tensor_tensor(v[:, :, :, 1, :], lo, hi, ALU.min).then_inc(q["sorted"], 1)
                    src, dst = dst, (sort_b if dst is sort_a else sort_a)
                dve.wait_ge(q["sorted"], 30 * half + 30)
                dve.wait_ge(q["carried"], carried)
                dve.wait_ge(q["flagged"], 2)
                flat = [t.rearrange("p r j -> p (r j)") for t in (sums, notfirst, src)]
                link(dve, dve.tensor_tensor_scan(flat[0], flat[1], flat[2], 0.0, ALU.mult, ALU.add))
                inv = const[:, None, C_INV:C_INV + L].broadcast_to([P, HR, L])
                link(dve, dve.scalar_tensor_tensor(out=sums, in0=sums, scalar=-1.0, in1=inv,
                                                   op0=ALU.add, op1=ALU.mult))
                link(dve, dve.tensor_reduce(stat[:, mine], sums, AX_X, ALU.max))
                for g in range(4 * half, 4 * half + 4):
                    r = slice(g * H, g * H + H)
                    dve.tensor_tensor(S_rows[:, r, :], S_rows[:, r, :], stat_b[:, r, :],
                                      ALU.subtract).then_inc(q["lowered"], 1)
            for g in range(G):
                dve_residual(dve, 1, g)

        def dve_stage_e(dve):
            q = self_sems[4]
            swap = [i ^ 1 for i in range(32)]
            cos, sin = (const[:, None, c:c + L].broadcast_to([P, B // 2, L]) for c in (C_COS, C_SIN))

            def rope(t, s, n):
                done = 8 * n + (0 if t is kT else 4)
                dve.wait_ge(q[s], 2 * n + 2)
                c = slice(n * HALF, n * HALF + HALF)
                for m in range(DT):
                    i = dve.stream_shuffle(rot[:, m, :], t[:, m, c], swap)
                link(dve, i)
                for m in range(DT):
                    r = rot[:, m, :].rearrange("p (b j) -> p b j", j=L)
                    dve.tensor_tensor(r, r, sin, ALU.mult)
                    i = dve.tensor_tensor(halves(t, m, n), halves(t, m, n), cos, ALU.mult)
                link(dve, i)
                for m in range(DT):
                    dve.tensor_tensor(t[:, m, c], t[:, m, c], rot[:, m, :], ALU.add).then_inc(q["rope"], 2)
                dve.wait_ge(q["rope"], done + 4)


            def lower(g):
                dve.wait_ge(q["s"], g + 1)
                r = slice(g * H, g * H + H)
                logits = bank[g % 4][:, :].rearrange("p (h j) -> p h j", j=L)
                link(dve, dve.tensor_reduce(stat[:, r], logits, AX_X, ALU.max))
                dve.tensor_tensor(S_rows[:, r, :], logits, stat_b[:, r, :],
                                  ALU.subtract).then_inc(q["lowered"], 1)

            def normalize(g):
                r = slice(g * H, g * H + H)
                dve.wait_ge(q["exp"], g + 1)
                link(dve, dve.tensor_reduce(stat[:, r], S_rows[:, r, :], AX_X, ALU.add))
                link(dve, dve.reciprocal(stat[:, r], stat[:, r]))
                dve.tensor_tensor(S_rows[:, r, :], S_rows[:, r, :], stat_b[:, r, :], ALU.mult).then_inc(q["probs"], 1)

            rope(kT, "k_out", 0)
            rope(qT, "q_out", 0)
            dve_spread_keys(dve, q, 1, 0)
            for g in range(4):
                lower(g)
            for g in range(4):
                normalize(g)
            rope(kT, "k_out", 1)
            for g in range(2):
                dve_residual(dve, 4, g)
            rope(qT, "q_out", 1)
            dve_spread_keys(dve, q, 1, 1)
            for g in range(2, 4):
                dve_residual(dve, 4, g)
            staggered(4, lambda g: lower(4 + g), lambda g: normalize(4 + g))
            for g in range(4, G):
                dve_residual(dve, 4, g)

        def w_b(j):
            return w_odd[:, j * DT * D:(j + 1) * DT * D].rearrange("p (k n) -> p k n", k=DT)

        def w_e(j):
            return w_even[:, j * DT * D:(j + 1) * DT * D].rearrange("p (k n) -> p k n", k=DT)

        WE_DIMS = ((DT, I0), (DT, I0), (I0 // P, D))
        WE = DT * I0
        we = [[area(3 * WE * s + WE * j, *d) for j, d in enumerate(WE_DIMS)] for s in range(3)]
        we_lo = [[rounded(f"we_lo{s}{j}", 3 * WE * s + WE * j, *d) for j, d in enumerate(WE_DIMS)] for s in range(3)]
        we_hi = [[rounded(f"we_hi{s}{j}", at + WE * j, *d) for j, d in enumerate(WE_DIMS)]
                 for s, at in enumerate((12 * WE, 9 * WE))]
        c_gate = w_even[:, 3072:3072 + DT * E0].rearrange("p (k n) -> p k n", k=DT)
        c_sg, c_su = (w_even[:, j * 1024:(j + 1) * 1024].rearrange("p (k n) -> p k n", k=DT) for j in range(2))
        c_sd = w_even[:, 2048:3072].rearrange("p (k n) -> p k n", k=IS // P)
        c_sT = area(18432, IS // P, T)
        c_sc = area(22528, T // 2)[0:32 + E0, :]
        c_sc2 = area(23936, T // 2)[0:32 + E0, :]
        c_val = area(23040, C0)[0:32 + E0, :]
        c_idx = area(23168, C0)[0:32 + E0, :].bitcast(U32)
        c_idxf = area(23296, C0)[0:32 + E0, :]
        c_val2, c_idx2 = area(23424, C0)[0:E0, :], area(23552, C0)[0:E0, :]
        c_first = area(23680, C0)[0:E0, :]
        c_p = area(23808, G, E0)
        c_xgT = [split(f"c_xgT{s}", 30720 + 512 * s, DT, C0) for s in range(2)]
        c_hg = area(31744, 2, 512)
        c_h = area(32768, 2, 512)
        c_tmp, c_up = ([area(at + 512 * s, 512) for s in range(2)] for at in (31744, 32768))
        c_hT = [split("c_hT0", 33792, I0 // P, C0), split("c_hT1", 0, I0 // P, C0, at=x_at)]
        c_idxT = area(35840, E0).bitcast(U32)
        c_valT = area(35856, E0)
        zT_flat = zT.rearrange("p k t -> p (k t)")
        c_xg = [z[:, e, :] if e < G else zT_flat[:, (e - G) * D:(e - G + 1) * D] for e in range(E0)]
        c_eo = [w_even[:, D * s:D * s + D] for s in range(2)]
        c_m, c_r = small[:, 0:G], small[:, 8:16]
        we_loaded, wd_loaded = ([sem(f"{n}_loaded{s}") for s in range(3)] for n in ("gate_up", "down"))
        z_stored, acc_stored = sem("z_stored"), sem("acc_stored")
        r_logit, r_sub, r_exp = sem("router_logit"), sem("router_sub"), sem("router_exp")
        c_prob, c_scT, c_sc_out = sem("c_prob"), sem("c_scT"), sem("c_sc_out")
        c_sgu, c_sgel, c_sh, c_sy, c_sx = sem("c_sgu"), sem("c_sgel"), sem("c_sh"), sem("c_sy"), sem("c_sx")
        c_top, c_topT, c_pick = sem("c_top"), sem("c_topT"), sem("c_pick")
        GOT_FIRST = (0, 1, 4, 8, E0)
        c_got = [sem(f"c_got{s}") for s in range(4)]
        S_BANK = (6, 7, 0, 1, 2, 3, 5, 6)

        def got_by(e):
            return max(s for s in range(4) if GOT_FIRST[s] <= e)

        c_xt, c_xt_hi, c_gu, c_gel, c_hm = sem("c_xt"), sem("c_xt_hi"), sem("c_gu"), sem("c_gel"), sem("c_hm")
        c_ht, c_hT_hi, c_hT_lo, c_down, c_eo_out, c_added = (
            sem("c_ht"), sem("c_hT_hi"), sem("c_hT_lo"), sem("c_down"), sem("c_eo_out"), sem("c_added"))

        c_whi, c_wlo_dve, c_wlo_pool, c_xt_lo = (
            sem("c_weights_hi"), sem("c_weights_lo_dve"), sem("c_weights_lo_pool"), sem("c_xt_lo"))

        WE_ORDER = ((0, 0), (1, 0), (0, 1), (1, 1), (2, 0), (2, 1))

        def we_part(t, i):
            j, c = WE_ORDER[i]
            return t[j][:, :, c * 512:c * 512 + 512] if j < 2 else t[j][:, 4 * c:4 * c + 4, :]

        N_TOP = 3 * (C0 // 8) + 2

        def sp_stage_c(sp):
            sp_weights(sp, 2)
            sp.wait_ge(ln_z, 3 * G)
            sp.dma_start(z_dram.rearrange("(g p) d -> p g d", p=P), z[:, :, :]).then_inc(z_stored, 16)
            for e in range(E0):
                s = e % 3
                if e == 0:
                    sp.wait_ge(x_done, 2)
                if e == 2:
                    sp_weights(sp, 3)
                if e == 3:
                    sp.wait_ge(c_sx, G)
                    sp.dma_start(acc_dram.rearrange("(g p) d -> p g d", p=P), x[:, :, :]).then_inc(acc_stored, 16)
                if e >= 3:
                    sp.wait_ge(c_gu, 2 * (e - 2))
                for j, name in enumerate(("we_g", "we_u")):
                    sp.dma_start(we[s][j].rearrange("p k n -> p (k n)"), a[name][e]).then_inc(we_loaded[s], 16)
                if e >= 3:
                    sp.wait_ge(c_down, e - 2)
                sp.dma_start(we[s][2].rearrange("p k n -> p (k n)"), a["we_d"][e]).then_inc(wd_loaded[s], 16)
            sp.wait_ge(c_added, 16 * E0)
            for half in range(2):
                gs = slice(4 * half, 4 * half + 4)
                sp.dma_start(x[:, gs, :], acc_dram.rearrange("(g p) d -> p g d", p=P)[:, gs, :]).then_inc(loaded_x[half], 16)

        def pe_stage_c(pe):
            wait_weights(pe, 2)
            pe_turn_z(pe, 2, 1)
            pe_wait_zT(pe, 2, 0)
            pe_wait_zT(pe, 2, 1)
            for g in range(G):
                for k in range(DT):
                    i = pe.matmul(bank[4][:, g * E0:g * E0 + E0], zT[:, k, g * P:g * P + P], c_gate[:, k, :],
                                  start=(k == 0), stop=(k == DT - 1))
            i.then_inc(r_logit, 1)

            def shared(c):
                m, n = c // 2, c % 2
                if c >= 2:
                    pe.wait_ge(c_sgel, c - 1)
                for w, o in ((c_sg, bank[c % 2]), (c_su, bank[2 + c % 2])):
                    for k in range(DT):
                        i = pe.matmul(o[:, :], w[:, k, m * P:m * P + P], zT[:, k, n * 512:n * 512 + 512],
                                      start=(k == 0), stop=(k == DT - 1))
                i.then_inc(c_sgu, 1)

            pe.wait_ge(c_prob, 1)
            for g in range(G):
                i = pe.transpose(bank[5 + g // 4][0:E0, (g % 4) * P:(g % 4) * P + P], c_p[:, g, :], ident)
            i.then_inc(c_scT, 1)
            for c in range(8):
                shared(c)
            pe.wait_ge(c_sh, 8)
            for g in range(G):
                if g == 0:
                    pe.wait_ge(c_sc_out, 2)
                if g == 2:
                    pe.wait_ge(c_top, N_TOP)
                    pe.transpose(bank[4][:, 128:128 + E0], c_val[0:E0, :], ident[0:E0, 0:E0])
                    pe.transpose(bank[4][:, 144:144 + E0], c_idxf[0:E0, :], ident[0:E0, 0:E0]).then_inc(c_topT, 1)
                if g == 7:
                    pe.wait_ge(c_sx, 1)
                for m in range(IS // P):
                    i = pe.matmul(bank[S_BANK[g]][:, 0:D], c_sT[:, m, g * P:g * P + P], c_sd[:, m, :],
                                  start=(m == 0), stop=(m == IS // P - 1))
                i.then_inc(c_sy, 1)

            def turn_x(e):
                if e == GOT_FIRST[got_by(e)]:
                    pe.wait_ge(c_got[got_by(e)], 16 * (GOT_FIRST[got_by(e) + 1] - e))
                if e >= 1:
                    pe.wait_ge(c_xt_lo, e)
                for k in range(DT):
                    i = pe.transpose(bank[0][:, k * P:k * P + P], c_xg[e][:, k * P:k * P + P], ident)
                i.then_inc(c_xt, 1)

            def gate_up(e, c):
                if c == 0:
                    pe.wait_ge(c_xt_lo, e + 1)
                pe.wait_ge(c_wlo_dve, 4 * e + 2 * (c + 1))
                if e >= 1:
                    pe.wait_ge(c_hm, 2 * e - 1 + c)
                elif c == 0:
                    pe.wait_ge(c_pick, 2)
                for j in range(2):
                    for k in range(DT):
                        i = matmul3(pe, bank[1 + 2 * j + c][:, :], c_xgT[e % 2], (we_hi[e % 2][j], we_lo[e % 3][j]),
                                    (slice(None), k), (slice(None), k, slice(c * 512, c * 512 + 512)),
                                    k == 0, k == DT - 1)
                i.then_inc(c_gu, 1)

            def turn_h(e, c):
                pe.wait_ge(c_hm, 2 * e + c + 1)
                if e >= 1:
                    pe.wait_ge(c_hT_lo, 2 * e - 1 + c)
                for m in range(4):
                    i = pe.transpose(bank[5 + c][:, m * P:m * P + P], c_h[:, c, m * P:m * P + P], ident)
                i.then_inc(c_ht, 1)

            def down(e):
                pe.wait_ge(c_hT_lo, 2 * e + 2)
                pe.wait_ge(c_wlo_pool, 2 * (e + 1))
                if e >= 1:
                    pe.wait_ge(c_eo_out, e)
                for m in range(I0 // P):
                    i = matmul3(pe, bank[7][:, 0:D], c_hT[e % 2], (we_hi[e % 2][2], we_lo[e % 3][2]),
                                (slice(None), m), (slice(None), m), m == 0, m == I0 // P - 1)
                i.then_inc(c_down, 1)

            pe.wait_ge(c_sx, G)
            turn_x(0)
            for e in range(E0 + 1):
                if e < E0:
                    gate_up(e, 0)
                if e >= 1:
                    turn_h(e - 1, 1)
                if e < E0:
                    gate_up(e, 1)
                if e + 1 < E0:
                    turn_x(e + 1)
                if e >= 1:
                    down(e - 1)
                if e < E0:
                    turn_h(e, 0)

        def act_stage_c(act):
            act.wait_ge(r_sub, 1)
            act.activation(c_p, c_p, ACT.Exp).then_inc(r_exp, 1)
            for c in range(8):
                act.wait_ge(c_sgu, c + 1)
                if c >= 2:
                    act.wait_ge(c_sh, c - 1)
                act.activation(c_tmp[c % 2], bank[c % 2][:, :], ACT.Gelu)
                act.activation(c_up[c % 2], bank[2 + c % 2][:, :], ACT.Copy).then_inc(c_sgel, 1)

            def x_out(e):
                act.wait_ge(c_xt, e + 1)
                if e >= 2:
                    act.wait_ge(c_gu, 2 * (e - 1))
                act.activation(c_xgT[e % 2][0].rearrange("p k t -> p (k t)"), bank[0][:, 0:D], ACT.Copy).then_inc(c_xt_hi, 1)

            def weights_hi(e, first, end):
                if first == 0:
                    act.wait_ge(we_loaded[e % 3], 32 * (e // 3 + 1))
                    if e == 1:
                        act.wait_ge(c_sx, G)
                        act.wait_ge(c_pick, 2)
                    elif e >= 2:
                        act.wait_ge(c_gu, 2 * (e - 1))
                if end == 6:
                    act.wait_ge(wd_loaded[e % 3], 16 * (e // 3 + 1))
                    if e >= 2:
                        act.wait_ge(c_down, e - 1)
                for i in range(first, end):
                    act.activation(we_part(we_hi[e % 2], i), we_part(we[e % 3], i), ACT.Copy).then_inc(c_whi, 1)

            def h_hi(e, c):
                act.wait_ge(c_ht, 2 * e + c + 1)
                if e == 1:
                    act.wait_ge(acc_stored, 16)
                elif e >= 2:
                    act.wait_ge(c_down, e - 1)
                act.activation(c_hT[e % 2][0][:, 4 * c:4 * c + 4, :].rearrange("p m t -> p (m t)"), bank[5 + c][:, :],
                               ACT.Copy).then_inc(c_hT_hi, 1)

            def gelu(e, c):
                act.wait_ge(c_gu, 2 * e + c + 1)
                act.activation(c_hg[:, c, :], bank[1 + c][:, :], ACT.Gelu).then_inc(c_gel, 1)

            weights_hi(0, 0, 6)
            x_out(0)
            for e in range(E0 + 1):
                more = e + 1 < E0
                if e < E0:
                    gelu(e, 0)
                if e >= 1:
                    h_hi(e - 1, 1)
                if more:
                    weights_hi(e + 1, 0, 2)
                if e < E0:
                    gelu(e, 1)
                if more:
                    weights_hi(e + 1, 2, 3)
                    x_out(e + 1)
                if e < E0:
                    h_hi(e, 0)
                if more:
                    weights_hi(e + 1, 3, 4)
                    weights_hi(e + 1, 4, 6)

        def dve_stage_c(dve):
            def picks():
                dve.wait_ge(c_topT, 1)
                dve.tensor_copy(c_idxT, bank[4][:, 144:144 + E0]).then_inc(c_pick, 1)
                dve.tensor_copy(c_valT, bank[4][:, 128:128 + E0]).then_inc(c_pick, 1)

            def weights_lo(e, first, end):
                for i in range(first, end):
                    dve.wait_ge(c_whi, 6 * e + i + 1)
                    dve.tensor_tensor(we_part(we_lo[e % 3], i), we_part(we[e % 3], i),
                                      we_part(we_hi[e % 2], i).bitcast(F32), ALU.subtract).then_inc(c_wlo_dve, 1)

            link(dve, dve.memset(c_sc[0:32, :], 0.0))
            dve.wait_ge(r_logit, 1)
            logits = bank[4][:, 0:P].rearrange("p (g e) -> p g e", g=G)
            m_b, r_b = (t[:, :, None].broadcast_to([P, G, E0]) for t in (c_m, c_r))
            link(dve, dve.tensor_reduce(c_m, logits, AX_X, ALU.max))
            dve.tensor_tensor(c_p, logits, m_b, ALU.subtract).then_inc(r_sub, 1)
            dve.wait_ge(r_exp, 1)
            link(dve, dve.tensor_reduce(c_r, c_p, AX_X, ALU.add))
            link(dve, dve.reciprocal(c_r, c_r))
            dve.tensor_tensor(c_p, c_p, r_b, ALU.mult).then_inc(c_prob, 1)

            dve.wait_ge(c_scT, 1)
            for j in range(2):
                dve.tensor_copy(c_sc[32 * j:32 * j + E0, :], bank[5 + j][0:E0, :]).then_inc(c_sc_out, 1)
            dve.wait_ge(c_sc_out, 2)
            for r in range(C0 // 8):
                v, ix = c_val[:, 8 * r:8 * r + 8], c_idx[:, 8 * r:8 * r + 8]
                left, then = (c_sc, c_sc2) if r % 2 == 0 else (c_sc2, c_sc)
                if r:
                    dve.wait_ge(c_top, 3 * r - 1)
                dve.max(v, left).then_inc(c_top, 1)
                dve.wait_ge(c_top, 3 * r + 1)
                dve.match_replace(then, v, left, -1.0).then_inc(c_top, 1)
                dve.max_index(ix, v, left).then_inc(c_top, 1)
            dve.wait_ge(c_top, 3 * (C0 // 8))
            up = slice(C0 - 1, None, -1)
            dve.tensor_copy(c_val2, c_val[32:32 + E0, up])
            link(dve, dve.tensor_copy(c_idxf, c_idx))
            dve.tensor_scalar(c_idx2, c_idxf[32:32 + E0, up], float(T // 2), None, ALU.add)
            link(dve, dve.tensor_tensor(c_first, c_val[0:E0, :], c_val2, ALU.is_ge))
            link(dve, dve.tensor_tensor(c_idxf[0:E0, :], c_idxf[0:E0, :], c_idx2, ALU.subtract))
            link(dve, dve.tensor_tensor(c_idxf[0:E0, :], c_idxf[0:E0, :], c_first, ALU.mult))
            dve.tensor_tensor(c_idxf[0:E0, :], c_idxf[0:E0, :], c_idx2, ALU.add).then_inc(c_top, 1)
            dve.tensor_tensor(c_val[0:E0, :], c_val[0:E0, :], c_val2, ALU.max).then_inc(c_top, 1)
            for g in range(G):
                if g == 0:
                    picks()
                dve.wait_ge(c_sy, g + 1)
                dve.tensor_tensor(x[:, g, :], bank[S_BANK[g]][:, 0:D], x[:, g, :], ALU.add).then_inc(c_sx, 1)
                if 1 <= g <= 4:
                    weights_lo(0, g - 1, g)
            dve.wait_ge(c_pick, 2)

            def x_lo(e):
                dve.wait_ge(c_xt_hi, e + 1)
                hi, lo = (t.rearrange("p k t -> p (k t)") for t in c_xgT[e % 2])
                dve.tensor_tensor(lo, bank[0][:, 0:D], hi.bitcast(F32), ALU.subtract).then_inc(c_xt_lo, 1)

            def hidden(e, c):
                dve.wait_ge(c_gel, 2 * e + c + 1)
                if e >= 1:
                    dve.wait_ge(c_ht, 2 * e - 1 + c)
                dve.tensor_tensor(c_h[:, c, :], bank[3 + c][:, :], c_hg[:, c, :], ALU.mult).then_inc(c_hm, 1)

            def h_lo(e, c):
                dve.wait_ge(c_hT_hi, 2 * e + c + 1)
                hi, lo = (t[:, 4 * c:4 * c + 4, :].rearrange("p m t -> p (m t)") for t in c_hT[e % 2])
                dve.tensor_tensor(lo, bank[5 + c][:, :], hi.bitcast(F32), ALU.subtract).then_inc(c_hT_lo, 1)

            def weigh(e):
                dve.wait_ge(c_down, e + 1)
                if e >= 2:
                    dve.wait_ge(c_added, 16 * (e - 1))
                dve.tensor_scalar(c_eo[e % 2], bank[7][:, 0:D], c_valT[:, e:e + 1], None, ALU.mult).then_inc(c_eo_out, 1)

            x_lo(0)
            for e in range(E0 + 1):
                more = e + 1 < E0
                if e < E0:
                    hidden(e, 0)
                if e >= 1:
                    h_lo(e - 1, 1)
                if more:
                    weights_lo(e + 1, 0, 2)
                if e < E0:
                    hidden(e, 1)
                if more:
                    x_lo(e + 1)
                    weights_lo(e + 1, 2, 3)
                if e >= 1:
                    weigh(e - 1)
                if more:
                    weights_lo(e + 1, 3, 4)
                if e < E0:
                    h_lo(e, 0)
            dve.wait_ge(loaded_x[0], 32)
            dve.memset(tick[:, :], 0.0).then_inc(x_done, 1)
            dve_layernorm_loaded(dve, 3, 32)

        def pool_stage_c(pool):
            def gather(e):
                pool.indirect_dma_start(c_xg[e], None, z_dram[:, :], bass.IndirectOffsetOnAxis(
                    ap=c_idxT[:, e:e + 1], axis=0)).then_inc(c_got[got_by(e)], 16)

            for c in range(8):
                m, n = c // 2, c % 2
                pool.wait_ge(c_sgel, c + 1)
                if c >= 1:
                    pool.wait_ge(c_sh, c)
                pool.tensor_tensor(c_sT[:, m, n * 512:n * 512 + 512], c_up[c % 2], c_tmp[c % 2], ALU.mult).then_inc(c_sh, 1)
            pool.wait_ge(c_pick, 1)
            pool.wait_ge(z_stored, 16)
            def weights_lo(e):
                for i in (4, 5):
                    pool.wait_ge(c_whi, 6 * e + i + 1)
                    pool.tensor_tensor(we_part(we_lo[e % 3], i), we_part(we[e % 3], i),
                                       we_part(we_hi[e % 2], i).bitcast(F32), ALU.subtract).then_inc(c_wlo_pool, 1)

            for e in range(E0):
                gather(e)
                if e == 3:
                    weights_lo(0)

            pool.wait_ge(acc_stored, 16)
            for e in range(E0):
                if e + 1 < E0:
                    weights_lo(e + 1)
                pool.wait_ge(c_eo_out, e + 1)
                if e >= 1:
                    pool.wait_ge(c_added, 16 * e)
                pool.indirect_dma_start(acc_dram[:, :], bass.IndirectOffsetOnAxis(ap=c_idxT[:, e:e + 1], axis=0),
                                        c_eo[e % 2], None, compute_op=ALU.add).then_inc(c_added, 16)

        w_d = [w_odd[:, j * 1024:(j + 1) * 1024].rearrange("p (k n) -> p k n", k=k)
               for j, k in enumerate((DT, XI // P, DT, XI // P))]
        d_qk = area(10256, DT, B // 2, XH * L)
        d_aT = d_qk
        d_q = split("d_q", 18448, XI // P, HALF)
        d_wk = split("d_wk", 32032, XI // P, D)
        d_oT = area(22544, XI // P, HALF)
        d_p = [[area(24592 + 260 * (2 * s + j), NK) for j in range(2)] for s in range(2)]
        d_n = [split(f"d_n{s}", 25632 + 1024 * s, 2, D) for s in range(3)]
        d_pT = [split(f"d_pT{s}", 28704 + 1024 * s, 2, XH * L) for s in range(2)]
        EDGE = EDGE_ROWS[-1] + 1
        d_nl = [rounded(f"d_nl{s}", 30752 + 256 * s, D)[0:EDGE, :] for s in range(3)]
        d_pl = [rounded(f"d_pl{s}", 31520 + 256 * s, XH * L)[0:EDGE, :] for s in range(2)]
        d_mx, d_nb, d_sum, d_inv = (small[:, 64 * j:64 * j + 64] for j in range(4))
        (d_qd, d_q_out, d_qkd, d_qk_act, d_qk_dve, d_s, d_nbias, d_exp, d_norm, d_turn, d_turned, d_av, d_a_out,
         d_o, d_o_out, d_y, d_x, d_clear, d_nhi, d_nlo, d_phi, d_q_lo) = (sem("d_" + n) for n in (
             "q", "q_out", "qk", "qk_act", "qk_dve", "s", "nbias", "exp", "norm", "turn", "turned", "av", "a_out",
             "o", "o_out", "y", "x", "clear", "rows_hi", "rows_lo", "p_hi", "q_lo"))

        def sp_stage_d(sp):
            sp.wait_ge(x_done, 3)
            sp.wait_ge(d_clear, 1)
            sp_context(sp, 3, (d_s, 2 * BG), (d_nlo, 2 * BG))
            sp_weights(sp, 4)
            sp_weights(sp, 5)

        def pe_stage_d(pe):
            wait_weights(pe, 3)
            for half in range(2):
                b0 = half * (B // 2)
                pe_wait_zT(pe, 3, half)
                for m in range(XI // P):
                    for k in range(DT):
                        i = pe.matmul(bank[4 + m][:, :], w_d[0][:, k, m * P:m * P + P],
                                      zT[:, k, half * HALF:half * HALF + HALF], start=(k == 0), stop=(k == DT - 1))
                    i.then_inc(d_qd, 1)
                if half == 0:
                    pe_turn_z(pe, 3, 1)
                    pe.wait_ge(d_clear, 3)
                    pe_wait_zT(pe, 3, 1)
                for c in range(16):
                    h, dt = c // 2, c % 2
                    r = (h % 2) * 64
                    if c >= 4:
                        pe.wait_ge((d_qk_act, d_qk_dve)[c % 2], 8 * half + (c - 4) // 2 + 1)
                    elif half:
                        pe.wait_ge(d_x, 4)
                    if c % 4 == 0:
                        pe.wait_ge(d_q_lo, 4 * half + h // 2 + 1)
                    matmul3(pe, bank[c % 4][:, :], d_wk, d_q, (slice(r, r + 64), h // 2, slice(dt * P, dt * P + P)),
                            (slice(r, r + 64), h // 2), True, True).then_inc(d_qkd, 1)
                pe.wait_ge(d_qk_act, 8 * (half + 1))
                pe.wait_ge(d_qk_dve, 8 * (half + 1))

                def scores(bb):
                    b = b0 + bb
                    s = (b // BG) % 2
                    if b % BG == 0:
                        pe.wait_ge(keys_loaded[s], KEYS_A + 16 * (b // BG // 2 + 1))
                    for j in range(2):
                        if b >= 1:
                            pe.wait_ge(d_exp, 2 * b - 1 + j)
                        for k in range(DT):
                            i = pe.matmul(bank[j][:, 0:NK], d_qk[:, k, bb, j * P:j * P + P], ringT[s][:, k, b % BG, :],
                                          start=(k == 0), stop=(k == DT - 1))
                        i.then_inc(d_s, 1)

                def turn(bb):
                    b = b0 + bb
                    pe.wait_ge(d_norm, 2 * b + 2)
                    if b >= 1:
                        pe.wait_ge(d_turned, 2 * b)
                    for j in range(2):
                        p = d_p[b % 2][j]
                        for k in range(2):
                            pe.transpose(bank[2 + b % 2][:, k * 256 + j * P:k * 256 + j * P + P],
                                         p[:, k * P:k * P + P], ident)
                        i = pe.transpose(bank[6][0:EDGE, j * P:j * P + P], p[:, NK - 1:NK].broadcast_to([P, EDGE]), ident)
                    i.then_inc(d_turn, 1)

                def values(bb):
                    b = b0 + bb
                    pe.wait_ge(d_turned, 2 * b + 1)
                    pe.wait_ge(d_nlo, 2 * b + 2)
                    if b >= 2:
                        pe.wait_ge(d_a_out, b - 1)
                    for dt in range(DT):
                        o = bank[4 + b % 2][:, dt * 256:dt * 256 + 256]
                        for k in range(2):
                            matmul3(pe, o, d_n[b % 3], d_pT[b % 2], (slice(None), k, slice(dt * P, dt * P + P)),
                                    (slice(None), k), k == 0, False)
                        if dt == 0:
                            pe.wait_ge(d_turned, 2 * b + 2)
                        i = pe.matmul(o, d_nl[b % 3][:, dt * P:dt * P + P], d_pl[b % 2], start=False, stop=True)
                    i.then_inc(d_av, 1)

                for t in range(B // 2 + 2):
                    if t < B // 2:
                        scores(t)
                    if t >= 2:
                        values(t - 2)
                    if 1 <= t <= B // 2:
                        turn(t - 1)
                pe.wait_ge(d_a_out, (half + 1) * (B // 2))
                if half:
                    pe_turn_z(pe, 4, 0)
                for m in range(XI // P):
                    if m >= 2:
                        pe.wait_ge(d_o_out, 4 * half + m - 1)
                    for h in (2 * m, 2 * m + 1):
                        r = (h % 2) * 64
                        for k in range(DT):
                            i = pe.matmul(bank[6 + m % 2][r:r + 64, :], w_d[2][:, k, h * XD:h * XD + XD],
                                          d_aT[:, k, :, h * L:h * L + L], start=(k == 0), stop=(k == DT - 1))
                    i.then_inc(d_o, 1)
                pe.wait_ge(d_o_out, 4 * (half + 1))
                for g in range(4 * half, 4 * half + 4):
                    if g % 4 >= 2:
                        pe.wait_ge(d_x, g - 1)
                    for m in range(XI // P):
                        pe.matmul(bank[2 + g % 2][:, 0:D], d_oT[:, m, g % 4 * P:g % 4 * P + P], w_d[3][:, m, :],
                                  start=(m == 0), stop=False)
                    pe.matmul(bank[2 + g % 2][:, 0:D], ones[:, :], brow[:, R_BO:R_BO + D],
                              start=False, stop=True).then_inc(d_y, 1)

        def act_stage_d(act):
            for half in range(2):
                for m in range(XI // P):
                    act.wait_ge(d_qd, 4 * half + m + 1)
                    act.activation(d_q[0][:, m, :], bank[4 + m][:, :], ACT.Copy).then_inc(d_q_out, 1)
                for c in range(0, 16, 2):
                    act.wait_ge(d_qkd, 16 * half + c + 1)
                    act.activation(d_qk[:, 0, :, (c // 2) * L:(c // 2) * L + L],
                                   bank[c % 4][:, :].rearrange("p (b i) -> p b i", i=L), ACT.Copy).then_inc(d_qk_act, 1)

                def exps(bb):
                    b = half * (B // 2) + bb
                    for j in range(2):
                        t = 2 * b + j
                        act.wait_ge(d_nbias, b + 1)
                        if b >= 2:
                            act.wait_ge(d_turn, b - 1)
                        act.activation(d_p[b % 2][j], bank[j][:, 0:NK], ACT.Exp, bias=d_nb[:, t:t + 1],
                                       scale=XD ** -0.5, accum_out=d_sum[:, t:t + 1]).then_inc(d_exp, 1)

                def turned(bb):
                    b = half * (B // 2) + bb
                    act.wait_ge(d_turn, b + 1)
                    if b >= 2:
                        act.wait_ge(d_av, b - 1)
                    act.activation(d_pT[b % 2][0].rearrange("p k r -> p (k r)"), bank[2 + b % 2][:, :],
                                   ACT.Copy).then_inc(d_phi, 1)
                    act.activation(d_pl[b % 2], bank[6][0:EDGE, 0:256], ACT.Copy).then_inc(d_phi, 1)

                def rows(bb):
                    b = half * (B // 2) + bb
                    s = (b // BG) % 2
                    if b % BG == 0:
                        act.wait_ge(rows_loaded[s], ROWS_A + 64 * (b // BG // 2 + 1))
                    if b >= 3:
                        act.wait_ge(d_av, b - 2)
                    act.activation(d_n[b % 3][0], ringN[s][:, b % BG], ACT.Copy).then_inc(d_nhi, 1)
                    act.activation(d_nl[b % 3], ringL[s][0:EDGE, b % BG * D:b % BG * D + D], ACT.Copy).then_inc(d_nhi, 1)

                if half:
                    act_std(act, 4, 0)
                for t in range(B // 2 + 1):
                    if t < B // 2:
                        exps(t)
                    if t >= 1:
                        turned(t - 1)
                    if t < B // 2:
                        rows(t)
                if half:
                    act_zT(act, 4, 0)
                for m in range(XI // P):
                    act.wait_ge(d_o, 4 * half + m + 1)
                    act.activation(d_oT[:, m, :], bank[6 + m % 2][:, :], ACT.Copy).then_inc(d_o_out, 1)
            act_std(act, 4, 1)
            act_zT(act, 4, 1)

        def dve_stage_d(dve):
            for half in range(2):
                for m in range(XI // P):
                    dve.wait_ge(d_q_out, 4 * half + m + 1)
                    dve.tensor_tensor(d_q[1][:, m, :], bank[4 + m][:, :], d_q[0][:, m, :].bitcast(F32),
                                      ALU.subtract).then_inc(d_q_lo, 1)
                for c in range(1, 16, 2):
                    dve.wait_ge(d_qkd, 16 * half + c + 1)
                    dve.tensor_copy(d_qk[:, 1, :, (c // 2) * L:(c // 2) * L + L],
                                    bank[c % 4][:, :].rearrange("p (b i) -> p b i", i=L)).then_inc(d_qk_dve, 1)

                def maxima(bb):
                    t = 2 * (half * (B // 2) + bb)
                    for j in range(2):
                        dve.wait_ge(d_s, t + j + 1)
                        i = dve.tensor_reduce(d_mx[:, t + j:t + j + 1], bank[j][:, 0:NK], AX_X, ALU.max)
                    link(dve, i)
                    dve.tensor_scalar(d_nb[:, t:t + 2], d_mx[:, t:t + 2], -XD ** -0.5, None,
                                      ALU.mult).then_inc(d_nbias, 1)

                def normalize(bb):
                    b = half * (B // 2) + bb
                    dve.wait_ge(d_exp, 2 * b + 2)
                    link(dve, dve.reciprocal(d_inv[:, 2 * b:2 * b + 2], d_sum[:, 2 * b:2 * b + 2]))
                    for j in range(2):
                        p = d_p[b % 2][j]
                        dve.tensor_scalar(p, p, d_inv[:, 2 * b + j:2 * b + j + 1], None, ALU.mult).then_inc(d_norm, 1)

                def lows(bb):
                    b = half * (B // 2) + bb
                    dve.wait_ge(d_phi, 2 * b + 1)
                    hi, lo = d_pT[b % 2]
                    dve.tensor_tensor(lo.rearrange("p k r -> p (k r)"), bank[2 + b % 2][:, :],
                                      hi.bitcast(F32).rearrange("p k r -> p (k r)"), ALU.subtract).then_inc(d_turned, 1)
                    r = EDGE_ROWS[2]
                    pl = d_pl[b % 2][r:r + 1, :]
                    dve.wait_ge(d_phi, 2 * b + 2)
                    dve.tensor_tensor(pl, bank[6][r:r + 1, 0:256], pl.bitcast(F32), ALU.subtract).then_inc(d_turned, 1)

                def values_out(bb):
                    b = half * (B // 2) + bb
                    dve.wait_ge(d_av, b + 1)
                    dve.tensor_copy(d_aT[:, :, bb, :], bank[4 + b % 2][:, :].rearrange("p (k r) -> p k r", k=DT)).then_inc(d_a_out, 1)

                for t in range(B // 2 + 2):
                    if t < B // 2:
                        maxima(t)
                    if 1 <= t <= B // 2:
                        normalize(t - 1)
                    if t >= 2:
                        values_out(t - 2)
                    if 1 <= t <= B // 2:
                        lows(t - 1)
                    if half and t == 2:
                        dve_scale(dve, 4, 0)
                if half:
                    dve_zT(dve, 4, 0)
                for g in range(4 * half, 4 * half + 4):
                    dve.wait_ge(d_y, g + 1)
                    dve.tensor_tensor(x[:, g, :], bank[2 + g % 2][:, 0:D], x[:, g, :], ALU.add).then_inc(d_x, 1)
                    dve.wait_ge(d_x, g + 1)
                    i = dve_stats(dve, g)
                link(dve, i)
                if half == 0:
                    dve_variances(dve, 0)
            dve.memset(tick[:, :], 0.0).then_inc(x_done, 1)
            dve_variances(dve, 1)
            dve_scale(dve, 4, 1)
            dve_zT(dve, 4, 1)

        def pool_stage_d(pool):
            pool.wait_ge(x_done, 3)
            pool.memset(arena[0:EDGE, 8208:10256], 0.0).then_inc(d_clear, 1)
            wait_weights(pool, 3)
            pool.wait_ge(d_clear, 1)
            pool.tensor_copy(d_wk[0], w_d[1]).then_inc(d_clear, 1)
            pool.wait_ge(d_clear, 2)
            pool.tensor_tensor(d_wk[1], w_d[1], d_wk[0].bitcast(F32), ALU.subtract).then_inc(d_clear, 1)
            for b in range(B):
                s = (b // BG) % 2
                pool.wait_ge(d_nhi, 2 * b + 2)
                if b >= 1:
                    pool.wait_ge(d_nlo, 2 * b)
                if b % BG == 0:
                    pool.wait_ge(rows_loaded[s], ROWS_A + 64 * (b // BG // 2 + 1))
                hi, lo = d_n[b % 3]
                pool.tensor_tensor(lo, ringN[s][:, b % BG], hi.bitcast(F32), ALU.subtract).then_inc(d_nlo, 1)
                pool.wait_ge(d_nlo, 2 * b + 1)
                r = EDGE_ROWS[1]
                nl = d_nl[b % 3][r:r + 1, :]
                pool.tensor_tensor(nl, ringL[s][r:r + 1, b % BG * D:b % BG * D + D], nl.bitcast(F32),
                                   ALU.subtract).then_inc(d_nlo, 1)

        f_z = split("f_z", 0, DT, T)
        f_w1 = split("f_w1", 4096, DT, I1)
        f_w2 = split("f_w2", 8192, I1 // P, D)
        f_hT = [split(f"f_hT{s}", 12288 + 8192 * s, I1 // P, 512) for s in range(2)]
        f_raw1, f_raw2 = area(28672, DT, I1), area(30720, I1 // P, D)
        f_tmp = [area(32768 + 512 * s, 512) for s in range(2)]
        f_r1 = w_odd[:, 0:1024].rearrange("p (k n) -> p k n", k=DT)
        f_r2 = w_odd[:, 1024:1024 + RH // P * E1].rearrange("p (k n) -> p k n", k=RH // P)
        f_rh = area(24576, RH // P, T)
        f_p, f_rank = area(33792, G, E1), area(33824, G, E1)
        f_cw = area(33856, G, E1)
        f_gt, f_eq = area(33888, G, E1, E1), area(34016, G, E1, E1)
        f_m, f_r = small[:, 0:G], small[:, 8:16]
        f_loaded = [sem("f_loaded_w1"), sem("f_loaded_w2")]
        f_split = [sem("f_split_w1"), sem("f_split_w2")]
        (f_rhd, f_rh_out, f_h, f_gel, f_y, f_x, f_hi, f_lo) = (
            sem("f_" + n) for n in ("rh", "rh_out", "h", "gel", "y", "x", "hi", "lo"))
        NF = 2 * E1

        def sp_stage_f(sp):
            for e in range(E1):
                for j, (raw, name) in enumerate(((f_raw1, "f_w1"), (f_raw2, "f_w2"))):
                    if e == 0 and j == 0:
                        sp.wait_ge(x_done, 5)
                    if e >= 1:
                        sp.wait_ge(f_split[j], 2 * e)
                    sp.dma_start(raw.rearrange("p k n -> p (k n)"), a[name][e]).then_inc(f_loaded[j], 16)

        def pool_stage_f(pool):
            for e in range(E1):
                for j, (raw, (hi, lo)) in enumerate(((f_raw1, f_w1), (f_raw2, f_w2))):
                    pool.wait_ge(f_loaded[j], 16 * (e + 1))
                    if e >= 1:
                        pool.wait_ge(*((f_h, 16 * e), (f_y, 8 * e))[j])
                    pool.tensor_copy(hi, raw).then_inc(f_split[j], 1)
                    pool.wait_ge(f_split[j], 2 * e + 1)
                    pool.tensor_tensor(lo, raw, hi.bitcast(F32), ALU.subtract).then_inc(f_split[j], 1)

        def pe_stage_f(pe):
            wait_weights(pe, 5)
            for c in range(8):
                m, n = c % 4, c // 4
                if c == 4:
                    pe_turn_z(pe, 5, 1)
                if m == 0:
                    pe_wait_zT(pe, 5, n)
                if c >= 4:
                    pe.wait_ge(f_rh_out, c - 3)
                for k in range(DT):
                    i = pe.matmul(bank[c % 4][:, :], f_r1[:, k, m * P:m * P + P],
                                  zT[:, k, n * 512:n * 512 + 512], start=(k == 0), stop=(k == DT - 1))
                i.then_inc(f_rhd, 1)

            def first(i):
                e, n = i // 2, i % 2
                if n == 0:
                    pe.wait_ge(f_split[0], 2 * (e + 1))
                for m in range(I1 // P):
                    c = 8 * i + m
                    if c >= 4:
                        pe.wait_ge(f_gel, c - 3)
                    else:
                        pe.wait_ge(f_rh_out, 5 + c)
                    if c == 0:
                        pe.wait_ge(f_hi, 2)
                        pe.wait_ge(f_lo, 2)
                    for k in range(DT):
                        j = matmul3(pe, bank[c % 4][:, :], f_w1, f_z, (slice(None), k, slice(m * P, m * P + P)),
                                    (slice(None), k, slice(n * 512, n * 512 + 512)), k == 0, k == DT - 1)
                    j.then_inc(f_h, 1)

            def logits():
                pe.wait_ge(f_rh_out, 8)
                for g in range(G):
                    o = bank[4][:, g * E1:g * E1 + E1]
                    for m in range(RH // P):
                        pe.matmul(o, f_rh[:, m, g * P:g * P + P], f_r2[:, m, :], start=(m == 0), stop=False)
                    j = pe.matmul(o, ones[:, :], brow[:, R_RB2:R_RB2 + E1], start=False, stop=True)
                j.then_inc(r_logit, 1)

            def second(i):
                e, n = i // 2, i % 2
                pe.wait_ge(f_lo, 2 + 8 * (i + 1))
                if n == 0:
                    pe.wait_ge(f_split[1], 2 * (e + 1))
                if i == 0:
                    pe.wait_ge(r_sub, 2)
                for g in range(4):
                    if i >= 1:
                        pe.wait_ge(f_x, 4 * (i - 1) + g + 1)
                    o = bank[4 + g][:, 0:D]
                    for m in range(I1 // P):
                        matmul3(pe, o, f_hT[i % 2], f_w2, (slice(None), m, slice(g * P, g * P + P)),
                                (slice(None), m), m == 0, False)
                    pe.matmul(o, ones[:, :], brow[:, R_BE2 + e * D:R_BE2 + (e + 1) * D],
                              start=False, stop=True).then_inc(f_y, 1)

            logits()
            for e in range(E1):
                first(2 * e)
                first(2 * e + 1)
                second(2 * e)
                second(2 * e + 1)

        def act_stage_f(act):
            act.wait_ge(ln_zT_act, 12)
            act.wait_ge(ln_zT_dve, 12)
            for n in range(2):
                act.activation(f_z[0][:, :, n * 512:n * 512 + 512], zT[:, :, n * 512:n * 512 + 512],
                               ACT.Copy).then_inc(f_hi, 1)
            for c in range(8):
                m, n = c % 4, c // 4
                act.wait_ge(f_rhd, c + 1)
                act.activation(f_rh[:, m, n * 512:n * 512 + 512], bank[c % 4][:, :], ACT.Gelu,
                               bias=bcol[:, K_RB1 + m:K_RB1 + m + 1]).then_inc(f_rh_out, 1)
            act.wait_ge(r_sub, 2)
            act.activation(f_p, f_p, ACT.Exp).then_inc(r_exp, 1)
            for c in range(8 * NF):
                e, m = c // 16, c % 8
                act.wait_ge(f_h, c + 1)
                if c >= 2:
                    act.wait_ge(f_lo, c + 1)
                act.activation(f_tmp[c % 2], bank[c % 4][:, :], ACT.Gelu,
                               bias=bcol[:, K_BE1 + e * 8 + m:K_BE1 + e * 8 + m + 1]).then_inc(f_gel, 1)

        def dve_stage_f(dve):
            for n in range(2):
                dve.wait_ge(f_hi, n + 1)
                c = slice(n * 512, n * 512 + 512)
                dve.tensor_tensor(f_z[1][:, :, c], zT[:, :, c], f_z[0][:, :, c].bitcast(F32),
                                  ALU.subtract).then_inc(f_lo, 1)
            dve.wait_ge(r_logit, 2)
            lg = bank[4][:, 0:G * E1].rearrange("p (g e) -> p g e", g=G)
            m_b, r_b = (t[:, :, None].broadcast_to([P, G, E1]) for t in (f_m, f_r))
            link(dve, dve.tensor_reduce(f_m, lg, AX_X, ALU.max))
            dve.tensor_tensor(f_p, lg, m_b, ALU.subtract).then_inc(r_sub, 1)
            dve.wait_ge(r_exp, 2)
            link(dve, dve.tensor_reduce(f_r, f_p, AX_X, ALU.add))
            link(dve, dve.reciprocal(f_r, f_r))
            link(dve, dve.tensor_tensor(f_p, f_p, r_b, ALU.mult))
            other = f_p[:, :, None, :].broadcast_to([P, G, E1, E1])
            own = f_p[:, :, :, None].broadcast_to([P, G, E1, E1])
            tri = const[:, None, C_TRI:C_TRI + E1 * E1].broadcast_to([P, G, E1 * E1])
            dve.tensor_tensor(f_gt, other, own, ALU.is_gt)
            link(dve, dve.tensor_tensor(f_eq, other, own, ALU.is_equal))
            eq, gt = (t.rearrange("p g e f -> p g (e f)") for t in (f_eq, f_gt))
            link(dve, dve.tensor_tensor(eq, eq, tri, ALU.mult))
            link(dve, dve.tensor_tensor(gt, gt, eq, ALU.add))
            link(dve, dve.tensor_reduce(f_rank, f_gt, AX_X, ALU.add))
            link(dve, dve.scalar_tensor_tensor(out=f_cw, in0=f_rank, scalar=2.0, in1=f_p, op0=ALU.is_lt,
                                     op1=ALU.mult))

            def parts(i):
                for m in range(I1 // P):
                    c = 8 * i + m
                    dve.wait_ge(f_gel, c + 1)
                    if m == 0 and i >= 2:
                        dve.wait_ge(f_y, 4 * (i - 1))
                    hi, lo = (t[:, m, :] for t in f_hT[i % 2])
                    dve.tensor_copy(hi, f_tmp[c % 2]).then_inc(f_hi, 1)
                    dve.wait_ge(f_hi, c + 3)
                    dve.tensor_tensor(lo, f_tmp[c % 2], hi.bitcast(F32), ALU.subtract).then_inc(f_lo, 1)

            def residual(i):
                e, n = i // 2, i % 2
                for g in range(4):
                    dve.wait_ge(f_y, 4 * i + g + 1)
                    if e:
                        dve.wait_ge(f_x, 4 * (i - 2) + g + 1)
                    xs = x[:, 4 * n + g, :]
                    dve.scalar_tensor_tensor(out=xs, in0=bank[4 + g][:, 0:D], scalar=f_cw[:, 4 * n + g, e:e + 1],
                                             in1=xs, op0=ALU.mult, op1=ALU.add).then_inc(f_x, 1)

            for e in range(E1):
                parts(2 * e)
                parts(2 * e + 1)
                residual(2 * e)
                residual(2 * e + 1)

        block = ctx.enter_context(nc.Block())
        last = 5 if stop is None else stop

        @block.sync
        def _(sp):
            for half in range(2):
                gs = slice(4 * half, 4 * half + 4)
                sp.dma_start(x[:, gs, :], a["x"].rearrange("(g p) d -> p g d", p=P)[:, gs, :]).then_inc(loaded_x[half], 16)
                if half == 0:
                    sp.dma_start(const[:, :], a["const"]).then_inc(loaded_c, 16)
            sp_weights(sp, 0)
            sp.dma_start(bcol[:, :], a["bcol"]).then_inc(loaded_c, 16)
            sp.dma_start(brow_raw, a["brow"]).then_inc(bias_raw, 16)

            sp_stage_a(sp)
            sp_weights(sp, 1)
            if last >= 2:
                sp_stage_c(sp)
            if last >= 3:
                sp_stage_d(sp)
            if last >= 5:
                sp_stage_f(sp)
            if last == 2:
                sp.wait_ge(loaded_x[1], 32)
            for first, end in ((0, 4), (4, 7), (7, G)):
                if last == 5:
                    sp.wait_ge(f_x, 4 * NF - G + end)
                else:
                    sp.wait_ge(x_done, last + 1)
                gs = slice(first, end)
                sp.dma_start(out.rearrange("(g p) d -> p g d", p=P)[:, gs, :], x[:, gs, :]).then_inc(stored, 16)
            sp.wait_ge(stored, 48)

        stages = range(last + 1)

        @block.tensor
        def _(pe):
            for k in stages:
                if k == 0:
                    pe.wait_ge(loaded_c, 32)
                    pe_turn_z(pe, 0, 0)
                (pe_stage_a, lambda e: pe_self(e, 1, w_b), pe_stage_c, pe_stage_d,
                 lambda e: pe_self(e, 4, w_e), pe_stage_f)[k](pe)
                if k == 2:
                    pe.wait_ge(c_added, 16 * E0)
                    pe_keep_warm(pe, WARM_ADDED, 1)
                if k in (0, 1, 2, 4):
                    pe_turn_z(pe, k + 1, 0)
                    if k in (1, 4):
                        pe_keep_warm(pe, WARM_LN, LN_BANK[k + 1] + 3)
                if k == last and k < 5:
                    pe_turn_z(pe, k + 1, 1)

        @block.scalar
        def _(act):
            act_layernorm(act, 0)
            act.wait_ge(bias_set, 1)
            act.wait_ge(bias_raw, 16)
            act.activation(brow[0:1, :], brow_raw, ACT.Copy).then_inc(bias_set, 1)
            for k in stages:
                (act_stage_a, act_stage_b, act_stage_c, act_stage_d, act_stage_e, act_stage_f)[k](act)
                if k in (0, 1, 2, 4):
                    act_layernorm(act, k + 1)

        @block.vector
        def _(dve):
            dve.memset(bias_one, 1.0)
            link(dve, dve.memset(bias_zero, 0.0))
            dve.tensor_copy(ones[:, :], bias_one)
            dve.tensor_copy(brow[:, :], bias_zero).then_inc(bias_set, 1)
            dve_layernorm_loaded(dve, 0, 16)
            for k in stages:
                (dve_stage_a, dve_stage_b, dve_stage_c, dve_stage_d, dve_stage_e, dve_stage_f)[k](dve)

        @block.gpsimd
        def _(pool):
            pool.wait_ge(bias_set, 2)
            pool.tensor_tensor(brow[BIAS_ROWS - 1:BIAS_ROWS, :], brow_raw, brow[0:1, :].bitcast(F32),
                               ALU.subtract).then_inc(bias_set, 1)
            if last >= 1:
                pool_self(pool, 1)
            if last >= 2:
                pool_stage_c(pool)
            if last >= 3:
                pool_stage_d(pool)
            if last >= 4:
                pool_self(pool, 4)
            if last >= 5:
                pool_stage_f(pool)


def constants():
    p = np.arange(P)
    c = np.zeros((P, C_END), np.float32)
    c[:, C_ID:C_ID + P] = np.eye(P)
    c[:, C_CAUSAL:C_CAUSAL + L] = np.where(np.arange(L)[None] <= (p % L)[:, None], 0.0, NEG)
    c[:, C_HEAD:C_HEAD + HPT] = (p // HD)[:, None] == np.arange(HPT)[None]
    c[:, C_BATCH:C_BATCH + BG] = (p // L)[:, None] == np.arange(BG)[None]
    c[:, C_INV:C_INV + L] = (1.0 / np.arange(1, L + 1))[None]
    exponent = np.arange(HD // 2, dtype=np.float32) * np.float32(2.0 / HD)
    inv_freq = np.float32(10000.0) ** (-exponent)
    angles = inv_freq[(p % HD) // 2][:, None] * np.arange(L, dtype=np.float32)[None]
    c[:, C_COS:C_COS + L] = np.cos(angles)
    c[:, C_SIN:C_SIN + L] = np.sin(angles) * np.where(p % 2 == 0, -1.0, 1.0)[:, None]
    e = np.arange(E1)
    c[:, C_TRI:C_TRI + E1 * E1] = (e[None, :] < e[:, None]).reshape(1, -1)
    return c


def tiled(w):
    k, n = w.shape
    return w.reshape(k // P, P, n).transpose(1, 0, 2).reshape(P, -1)


def lay_out(i):
    v = {}
    v["x"] = i["x"].reshape(T, D)
    v["const"] = constants()
    col = lambda w: w.reshape(-1, P).T
    ba = i["L0_attn_b_attn"]
    v["bcol"] = np.concatenate([col(i["L0_xattn_b"]), col(ba[0:D]), col(ba[D:2 * D]), col(i["L1_ffn_rb1"]),
                                col(i["L1_ffn_be1"])], 1)
    v["brow"] = np.concatenate([i["L0_xattn_b"], ba[2 * D:], i["L0_attn_b_proj"], i["L1_xattn_bo"],
                                i["L1_ffn_rb2"], i["L1_ffn_be2"].reshape(-1)])[None]
    c = i["ctx_1024"].reshape(G, BG, NK, D)
    v["ctxT"] = c.reshape(G, BG, NK, DT, P).transpose(0, 4, 3, 1, 2).reshape(G, P, -1)
    v["ctx"] = c[:, :, 0:2 * P].reshape(G, BG, 2, P, D).transpose(0, 3, 1, 2, 4).reshape(G, P, -1)
    v["ctx_last"] = c[:, :, 2 * P].reshape(B, D)
    w = i["L0_xattn_W"]
    v["w0"] = np.concatenate([tiled(w), tiled(w.T)], 1)
    w = i["L0_attn_w_attn"]
    v["w1"] = np.concatenate([tiled(w[:, 0:D]), tiled(w[:, D:2 * D]), tiled(w[:, 2 * D:]), tiled(i["L0_attn_w_proj"])], 1)
    v["w2"] = np.concatenate([tiled(i["L0_ffn_Sg"].T), tiled(i["L0_ffn_Su"].T), tiled(i["L0_ffn_Sd"].T),
                              tiled(i["L0_ffn_gate_w"].T)], 1)
    v["w3"] = np.concatenate([tiled(i["L1_xattn_Wq"]), tiled(i["L1_xattn_Wk"].T), tiled(i["L1_xattn_Wv"]),
                              tiled(i["L1_xattn_Wo"])], 1)
    v["w4"] = np.concatenate([tiled(i[f"L1_attn_{n}"].T) for n in ("Wq", "Wk", "Wv", "Wo")], 1)
    v["w5"] = np.concatenate([tiled(i["L1_ffn_rW1"]), tiled(i["L1_ffn_rW2"])], 1)
    for n, s in (("we_g", "L0_ffn_Wg"), ("we_u", "L0_ffn_Wu"), ("we_d", "L0_ffn_Wd")):
        w = i[s].transpose(0, 2, 1)
        v[n] = w.reshape(E0, w.shape[1] // P, P, w.shape[2]).transpose(0, 2, 1, 3).reshape(E0, P, -1)
    for n, s in (("f_w1", "L1_ffn_We1"), ("f_w2", "L1_ffn_We2")):
        w = i[s]
        v[n] = w.reshape(E1, w.shape[1] // P, P, w.shape[2]).transpose(0, 2, 1, 3).reshape(E1, P, -1)
    return {k: np.ascontiguousarray(t) for k, t in v.items()}


def kernel(**inputs):
    import concourse.bacc as bacc
    from concourse.bass_utils import run_bass_kernel_spmd

    arrays = lay_out({k: np.asarray(t) for k, t in inputs.items()})
    nc = bacc.Bacc("TRN2", target_bir_lowering=False, num_devices=1)
    ins = {k: nc.dram_tensor(f"in_{k}", t.shape, mybir.dt.from_np(t.dtype), kind="ExternalInput").ap()
           for k, t in arrays.items()}
    out = nc.dram_tensor("out", [T, D], F32, kind="ExternalOutput").ap()
    build(nc, ins, out)
    r = run_bass_kernel_spmd(nc, [{f"in_{k}": t for k, t in arrays.items()}], core_ids=[0])
    return r.results[0]["out"].reshape(B, L, D)
```
